# Optimizing a Trainium2 kernel written in Bass

```python
import numpy as np
import jax
import jax.numpy as jnp

def _softmax(x, axis=-1):
    return jax.nn.softmax(x, axis=axis)

def _gelu(x):
    return jax.nn.gelu(x, approximate=True)

def _silu(x):
    return jax.nn.silu(x)

def _sigmoid(x):
    return jax.nn.sigmoid(x)

def _layernorm(x, axis=-1, eps=1e-05):
    m = jnp.mean(x, axis=axis, keepdims=True)
    v = jnp.var(x, axis=axis, keepdims=True)
    return (x - m) / jnp.sqrt(v + eps)

def _scatter_add(tgt, idx, src, axis=0):
    return tgt.at[idx].add(src)

def _segment_sum(src, seg, n):
    return jax.ops.segment_sum(src, seg, n)
kernel_name = 'mk_flamingo_gated_d1_seqx_r4_53b5e7'

def setup_inputs(seed: int=0):
    np.random.seed(seed)
    _w = jnp.asarray

    def _rec_inputs():
        import jax
        import jax.numpy as jnp
        _rk = jax.random.key(seed)
        x = -0.0002928 + 1 * jax.random.normal(jax.random.fold_in(_rk, 1), (8, 512, 256), jnp.float32)
        _lenS = 512 - jax.random.randint(jax.random.fold_in(_rk, 7), (8,), 0, max(1, 512 // 4) + 1, jnp.int32)
        _lenS2 = 512 - jax.random.randint(jax.random.fold_in(_rk, 8), (8,), 0, max(1, 512 // 4) + 1, jnp.int32)
        _ctx_1024P = jax.random.normal(jax.random.fold_in(_rk, 11), (8, 16, 256), jnp.float32)
        _ctx_1024c = jax.random.dirichlet(jax.random.fold_in(_rk, 511), 0.3 * jnp.ones((16,), jnp.float32), (8, 512))
        _ctx_1024t = jnp.einsum('bsk,bkd->bsd', _ctx_1024c, _ctx_1024P)
        _ctx_1024t = _ctx_1024t * jax.lax.rsqrt(jnp.mean(jnp.square(_ctx_1024t)) + 1e-12) * 0.953939
        ctx_1024 = -1.39393e-06 + 0.999914 * (_ctx_1024t + 0.3 * jax.random.normal(jax.random.fold_in(_rk, 611), (8, 512, 256), jnp.float32))
        fside_BxSx4_0 = jax.random.uniform(jax.random.fold_in(_rk, 12), (8, 512, 4), jnp.float32, 0.0, 0.999884)
        _g = jax.random.normal(jax.random.fold_in(_rk, 9001), (2, 1), jnp.float32)
        _g = jnp.sign(_g) * jnp.maximum(jnp.abs(_g), 1.0) + (_g == 0) * 1.0
        g_xattn = _g[0]
        g_ffn = _g[1]
        return (x, ctx_1024, fside_BxSx4_0, g_xattn, g_ffn)
    x, ctx_1024, fside_BxSx4_0, g_xattn, g_ffn = _rec_inputs()

    def _L0_xattn_setup():
        import jax, jax.numpy as jnp
        import numpy as np
        D_MODEL = 256
        H = 16
        D_K = 64
        D_V = 64
        D_G = D_MODEL // H
        WAVE_LEN = 1000.0
        B = 8
        N = 128

        def box_relational_embedding(boxes, dim_g=D_G):
            x_min, y_min, x_max, y_max = jnp.split(boxes, 4, axis=-1)
            cx = (x_min + x_max) * 0.5
            cy = (y_min + y_max) * 0.5
            w = x_max - x_min + 1.0
            h = y_max - y_min + 1.0
            delta_x = jnp.log(jnp.clip(jnp.abs((cx - jnp.swapaxes(cx, 1, 2)) / w), 0.001, None))
            delta_y = jnp.log(jnp.clip(jnp.abs((cy - jnp.swapaxes(cy, 1, 2)) / h), 0.001, None))
            delta_w = jnp.log(w / jnp.swapaxes(w, 1, 2))
            delta_h = jnp.log(h / jnp.swapaxes(h, 1, 2))
            pos = jnp.stack([delta_x, delta_y, delta_w, delta_h], axis=-1)
            n_freq = dim_g // 8
            feat_range = jnp.arange(n_freq, dtype=jnp.float32)
            dim_mat = 1.0 / WAVE_LEN ** (feat_range / n_freq)
            mul = (100.0 * pos)[..., None] * dim_mat
            b, n = (pos.shape[0], pos.shape[1])
            mul = mul.reshape(b, n, n, 4 * n_freq)
            return jnp.concatenate([jnp.sin(mul), jnp.cos(mul)], axis=-1)
        key = jax.random.key(seed)
        ks = jax.random.split(key, 12)
        s = 0.02
        inp = {'queries': jax.random.normal(ks[0], (B, N, D_MODEL), jnp.float32), 'keys': jax.random.normal(ks[1], (B, N, D_MODEL), jnp.float32), 'values': jax.random.normal(ks[2], (B, N, D_MODEL), jnp.float32), 'boxes': jax.random.uniform(ks[3], (B, N, 4), jnp.float32), 'Wq': jax.random.normal(ks[4], (H * D_K, D_MODEL), jnp.float32) * s, 'bq': jnp.zeros((H * D_K,), jnp.float32), 'Wk': jax.random.normal(ks[5], (H * D_K, D_MODEL), jnp.float32) * s, 'bk': jnp.zeros((H * D_K,), jnp.float32), 'Wv': jax.random.normal(ks[6], (H * D_V, D_MODEL), jnp.float32) * s, 'bv': jnp.zeros((H * D_V,), jnp.float32), 'Wo': jax.random.normal(ks[7], (D_MODEL, H * D_V), jnp.float32) * s, 'bo': jnp.zeros((D_MODEL,), jnp.float32), 'Wg': jax.random.normal(ks[8], (H, D_G), jnp.float32) * s, 'bg': jnp.zeros((H,), jnp.float32)}
        return inp
    _L0_xattn_all = _L0_xattn_setup()
    _L0_xattn_in = {k: v for k, v in _L0_xattn_all.items() if k in ('Wq', 'bq', 'Wk', 'bk', 'Wv', 'bv', 'Wo', 'bo', 'Wg', 'bg')}
    del _L0_xattn_all

    def _L0_ffn_setup():
        import jax, jax.numpy as jnp
        import numpy as np
        EMB, HID, E, TOPK = (256, 1024, 8, 2)
        key = jax.random.key(seed)
        ks = jax.random.split(key, 10)
        s = 0.02
        return {'x': jax.random.normal(ks[0], (4, 512, EMB), jnp.float32), 'rw1': s * jax.random.normal(ks[1], (EMB, HID), jnp.float32), 'rb1': jnp.zeros((HID,), jnp.float32), 'rw2': s * jax.random.normal(ks[2], (HID, E), jnp.float32), 'rb2': jnp.zeros((E,), jnp.float32), 'w1': s * jax.random.normal(ks[3], (E, EMB, HID), jnp.float32), 'b1': jnp.zeros((E, HID), jnp.float32), 'w2': s * jax.random.normal(ks[4], (E, HID, EMB), jnp.float32), 'b2': jnp.zeros((E, EMB), jnp.float32)}
    _L0_ffn_all = _L0_ffn_setup()
    _L0_ffn_in = {k: v for k, v in _L0_ffn_all.items() if k in ('rw1', 'rb1', 'rw2', 'rb2', 'w1', 'b1', 'w2', 'b2')}
    del _L0_ffn_all
    return {'x': x, 'ctx_1024': ctx_1024, 'fside_BxSx4_0': fside_BxSx4_0, 'g_xattn': g_xattn, 'g_ffn': g_ffn, 'L0_xattn_Wq': _L0_xattn_in['Wq'], 'L0_xattn_bq': _L0_xattn_in['bq'], 'L0_xattn_Wk': _L0_xattn_in['Wk'], 'L0_xattn_bk': _L0_xattn_in['bk'], 'L0_xattn_Wv': _L0_xattn_in['Wv'], 'L0_xattn_bv': _L0_xattn_in['bv'], 'L0_xattn_Wo': _L0_xattn_in['Wo'], 'L0_xattn_bo': _L0_xattn_in['bo'], 'L0_xattn_Wg': _L0_xattn_in['Wg'], 'L0_xattn_bg': _L0_xattn_in['bg'], 'L0_ffn_rw1': _L0_ffn_in['rw1'], 'L0_ffn_rb1': _L0_ffn_in['rb1'], 'L0_ffn_rw2': _L0_ffn_in['rw2'], 'L0_ffn_rb2': _L0_ffn_in['rb2'], 'L0_ffn_w1': _L0_ffn_in['w1'], 'L0_ffn_b1': _L0_ffn_in['b1'], 'L0_ffn_w2': _L0_ffn_in['w2'], 'L0_ffn_b2': _L0_ffn_in['b2']}

def reference(x, ctx_1024, fside_BxSx4_0, g_xattn, g_ffn, L0_xattn_Wq, L0_xattn_bq, L0_xattn_Wk, L0_xattn_bk, L0_xattn_Wv, L0_xattn_bv, L0_xattn_Wo, L0_xattn_bo, L0_xattn_Wg, L0_xattn_bg, L0_ffn_rw1, L0_ffn_rb1, L0_ffn_rw2, L0_ffn_rb2, L0_ffn_w1, L0_ffn_b1, L0_ffn_w2, L0_ffn_b2):
    import jax
    import jax.numpy as jnp

    def _L0_xattn_ref(queries, keys, values, boxes, Wq, bq, Wk, bk, Wv, bv, Wo, bo, Wg, bg):
        import jax, jax.numpy as jnp
        import numpy as np
        D_MODEL = 256
        H = 16
        D_K = 64
        D_V = 64
        D_G = D_MODEL // H
        WAVE_LEN = 1000.0
        B = 8
        N = 128

        def box_relational_embedding(boxes, dim_g=D_G):
            x_min, y_min, x_max, y_max = jnp.split(boxes, 4, axis=-1)
            cx = (x_min + x_max) * 0.5
            cy = (y_min + y_max) * 0.5
            w = x_max - x_min + 1.0
            h = y_max - y_min + 1.0
            delta_x = jnp.log(jnp.clip(jnp.abs((cx - jnp.swapaxes(cx, 1, 2)) / w), 0.001, None))
            delta_y = jnp.log(jnp.clip(jnp.abs((cy - jnp.swapaxes(cy, 1, 2)) / h), 0.001, None))
            delta_w = jnp.log(w / jnp.swapaxes(w, 1, 2))
            delta_h = jnp.log(h / jnp.swapaxes(h, 1, 2))
            pos = jnp.stack([delta_x, delta_y, delta_w, delta_h], axis=-1)
            n_freq = dim_g // 8
            feat_range = jnp.arange(n_freq, dtype=jnp.float32)
            dim_mat = 1.0 / WAVE_LEN ** (feat_range / n_freq)
            mul = (100.0 * pos)[..., None] * dim_mat
            b, n = (pos.shape[0], pos.shape[1])
            mul = mul.reshape(b, n, n, 4 * n_freq)
            return jnp.concatenate([jnp.sin(mul), jnp.cos(mul)], axis=-1)
        b, nq, _ = queries.shape
        nk = keys.shape[1]
        emb = box_relational_embedding(boxes)
        g = jax.nn.relu(jnp.einsum('bnmd,hd->bhnm', emb, Wg) + bg[None, :, None, None])
        q = (queries @ Wq.T + bq).reshape(b, nq, H, D_K).transpose(0, 2, 1, 3)
        k = (keys @ Wk.T + bk).reshape(b, nk, H, D_K).transpose(0, 2, 1, 3)
        v = (values @ Wv.T + bv).reshape(b, nk, H, D_V).transpose(0, 2, 1, 3)
        a = jnp.einsum('bhqd,bhkd->bhqk', q, k) / jnp.sqrt(jnp.float32(D_K))
        mn = jax.nn.softmax(jnp.log(jnp.clip(g, 1e-06, None)) + a, axis=-1)
        out = jnp.einsum('bhqk,bhkd->bqhd', mn, v).reshape(b, nq, H * D_V)
        return out @ Wo.T + bo

    def _L0_ffn_ref(x, rw1, rb1, rw2, rb2, w1, b1, w2, b2):
        import jax, jax.numpy as jnp
        import numpy as np
        EMB, HID, E, TOPK = (256, 1024, 8, 2)
        B, S, D = x.shape
        logits = jax.nn.silu(jnp.einsum('bsd,dh->bsh', x, rw1) + rb1)
        logits = jnp.einsum('bsh,he->bse', logits, rw2) + rb2
        k_logits, k_index = jax.lax.top_k(logits, TOPK)
        k_prob = jax.nn.softmax(k_logits, axis=-1)
        xf = x.reshape(B * S, D)
        k_index_f = k_index.reshape(B * S, TOPK)
        k_prob_f = k_prob.reshape(B * S, TOPK)
        out = jnp.zeros_like(xf)
        for e in range(E):
            we = jnp.sum(jnp.where(k_index_f == e, k_prob_f, 0.0), axis=-1)
            h = jax.nn.silu(xf @ w1[e] + b1[e]) @ w2[e] + b2[e]
            out = out + we[:, None] * h
        return out.reshape(B, S, D)
    x = x + jnp.tanh(g_xattn[0]) * _L0_xattn_ref(_layernorm(x, axis=-1), ctx_1024, ctx_1024, fside_BxSx4_0, L0_xattn_Wq, L0_xattn_bq, L0_xattn_Wk, L0_xattn_bk, L0_xattn_Wv, L0_xattn_bv, L0_xattn_Wo, L0_xattn_bo, L0_xattn_Wg, L0_xattn_bg)
    x = x + jnp.tanh(g_ffn[0]) * _L0_ffn_ref(_layernorm(x, axis=-1), L0_ffn_rw1, L0_ffn_rb1, L0_ffn_rw2, L0_ffn_rb2, L0_ffn_w1, L0_ffn_b1, L0_ffn_w2, L0_ffn_b2)
    return x

_drawn_inputs = setup_inputs


def setup_inputs(seed=0):
    import zlib

    import numpy as np

    out = dict(_drawn_inputs(seed))
    spreads = {'L0_xattn_bq': (0.0, 0.8),
     'L0_xattn_bk': (0.0, 0.8),
     'L0_xattn_bv': (0.0, 0.1),
     'L0_xattn_bo': (0.0, 0.1),
     'L0_xattn_bg': (0.0, 0.296),
     'L0_ffn_rb1': (0.0, 0.1),
     'L0_ffn_rb2': (0.0, 0.1),
     'L0_ffn_b1': (0.0, 0.36),
     'L0_ffn_b2': (0.0, 0.1)}
    factors = {'L0_xattn_Wq': 8.0, 'L0_xattn_Wk': 8.0}
    for name, (base, spread) in spreads.items():
        noise = np.random.default_rng([zlib.crc32(name.encode()), seed]).standard_normal(out[name].shape)
        drawn = base * np.exp(spread * noise) if base else spread * noise
        out[name] = jnp.asarray(drawn.astype(out[name].dtype))
    for name, factor in factors.items():
        out[name] = (out[name] * factor).astype(out[name].dtype)
    return out
```

```python
from contextlib import ExitStack

import concourse.bass as bass
from concourse import mybir

P = 128
B, S, D = 8, 512, 256
H, DK = 16, 64
HD = H * DK
E, HID = 8, 1024
TOK = B * S
NT = TOK // P
KD = D // P
NB = S // P
PAIRS = H // 2
EPS = 1e-5
FREQ = (1.0, 1000.0 ** -0.5)
TWO_PI = 6.283185307179586
HALF_PI = TWO_PI / 4
ROUND = 12582912.0
GEO_MIN = 1e-6
SLOT_TILE = 256
N_TILES = 2 * TOK // SLOT_TILE + E
SLOTS = N_TILES * SLOT_TILE
ZROWS = 11
SEP = 9
GEO_K = SEP + 64
YCOLS = H * P

ALU = mybir.AluOpType
ACT = mybir.ActivationFunctionType
F32 = mybir.dt.float32
F32R = mybir.dt.float32r
I32 = mybir.dt.int32
U32 = mybir.dt.uint32
AX = mybir.AxisListType.X


class Space:

    def __init__(self, nc, ctx, tag):
        self.nc, self.ctx, self.tag = nc, ctx, tag

    def sb(self, name, shape, dtype=F32):
        return self.ctx.enter_context(self.nc.sbuf_tensor(self.tag + name, shape, dtype))

    def ps(self, name, shape, dtype=F32):
        return self.ctx.enter_context(self.nc.psum_tensor(self.tag + name, shape, dtype))

    def sem(self, name):
        return self.ctx.enter_context(self.nc.semaphore(self.tag + name))


def make_identity(nc, pool, ident, done):
    nc.gpsimd.memset(ident[:], 0.0).then_inc(done, 1)
    pool.wait_ge(done, 1)
    nc.gpsimd.affine_select(out=ident[:], in_=ident[:], compare_op=ALU.not_equal, fill=1.0, base=0,
                            pattern=[[-1, P]], channel_multiplier=1).then_inc(done, 1)


def box_terms(nc, boxes, wg_rows, bg_row, y_dram, z_dram, centre, inv_size):
    with ExitStack() as ctx:
        m = Space(nc, ctx, "box_")
        bx = m.sb("bx", [P, NT, 4])
        size = m.sb("size", [P, NT, 2])
        lg = m.sb("lg", [P, NT, 2])
        turn = m.sb("turn", [P, NT, 4])
        whole = m.sb("whole", [P, NT, 4])
        frac = m.sb("frac", [P, NT, 4])
        mag = m.sb("mag", [P, NT, 4])
        halfpi = m.sb("halfpi", [P, 1])
        sc = m.sb("sc", [P, NT, 2, 4])
        wgb = m.sb("wgb", [P, H, H])
        z = m.sb("z", [P, NT, ZROWS])
        y = m.sb("y", [P, NT, SEP, H])
        tmp = m.sb("tmp", [P, NT, 4, H])
        ident = m.sb("ident", [P, P])
        row = [m.sb(f"row{i}", [SEP, YCOLS]) for i in range(2)]
        zrow = m.sb("zrow", [ZROWS, NT * P])
        psy = [m.ps(f"psy{i}", [P, 512]) for i in range(4)]

        loaded, ident_done = m.sem("loaded"), m.sem("ident_done")
        step, logs, sines = m.sem("step"), m.sem("logs"), m.sem("sines")
        turned, moved, row_moved = m.sem("turned"), m.sem("moved"), m.sem("row_moved")
        row_stored = [m.sem(f"row_stored{i}") for i in range(2)]
        z_stored = m.sem("z_stored")
        block = ctx.enter_context(nc.Block())

        @block.sync
        def _(sp):
            sp.dma_start(bx[:], boxes.rearrange("(t p) c -> p t c", p=P)).then_inc(loaded, 16)
            sp.dma_start(wgb[:], wg_rows.partition_broadcast(P)).then_inc(loaded, 16)
            sp.dma_start(y[:, 0, SEP - 1, :], bg_row.partition_broadcast(P)).then_inc(loaded, 16)
            for t in range(NT):
                sp.wait_ge(row_moved, 4 * (t + 1))
                sp.dma_start(y_dram[t], row[t % 2][:]).then_inc(row_stored[t % 2], 16)
            sp.wait_ge(row_moved, 4 * NT + NT * P // 512)
            sp.dma_start(z_dram.rearrange("k b m -> k (b m)"), zrow[:]).then_inc(z_stored, 16)
            for i in range(2):
                sp.wait_ge(row_stored[i], 16 * NT // 2)
            sp.wait_ge(z_stored, 16)

        @block.gpsimd
        def _(pool):
            make_identity(nc, pool, ident, ident_done)

        @block.vector
        def _(dve):
            count = [0]

            def link(ins):
                count[0] += 1
                ins.then_inc(step, 1)
                dve.wait_ge(step, count[0])

            nc.vector.memset(halfpi[:], HALF_PI)
            nc.vector.memset(z[:, :, SEP - 1:SEP], 1.0)
            dve.wait_ge(loaded, 48)
            link(nc.vector.tensor_tensor(size[:], bx[:, :, 2:4], bx[:, :, 0:2], ALU.subtract))
            link(nc.vector.tensor_scalar(size[:], size[:], 1.0, None, ALU.add))
            nc.vector.reciprocal(inv_size[:], size[:])
            link(nc.vector.tensor_tensor(centre[:], bx[:, :, 0:2], bx[:, :, 2:4], ALU.add))
            link(nc.vector.tensor_scalar(centre[:], centre[:], 0.5, None, ALU.mult))
            nc.vector.tensor_copy(z[:, :, SEP:ZROWS], centre[:])
            nc.vector.tensor_copy(y[:, 1:NT, SEP - 1, :],
                                  y[:, 0, SEP - 1, :].unsqueeze(1).to_broadcast([P, NT - 1, H]))
            dve.wait_ge(logs, 1)
            for f in range(2):
                link(nc.vector.tensor_scalar(turn[:, :, f:4:2], lg[:], 100.0 * FREQ[f] / TWO_PI, None, ALU.mult))
            link(nc.vector.tensor_scalar(whole[:], turn[:], ROUND, None, ALU.add))
            link(nc.vector.tensor_scalar(whole[:], whole[:], ROUND, None, ALU.subtract))
            link(nc.vector.tensor_tensor(frac[:], turn[:], whole[:], ALU.subtract))
            link(nc.vector.tensor_single_scalar(mag[:].bitcast(I32), frac[:].bitcast(I32), 0x7FFFFFFF, op=ALU.bitwise_and))
            dve.wait_ge(sines, 2)
            nc.vector.tensor_copy(z[:, :, 0:8], sc[:].rearrange("p t s k -> p t (s k)"))

            def times(out, s, w):
                a = sc[:, :, s, :].unsqueeze(3).to_broadcast([P, NT, 4, H])
                c = wgb[:, w:w + 4, :].unsqueeze(1).to_broadcast([P, NT, 4, H])
                link(nc.vector.tensor_tensor(out, a, c, ALU.mult))

            times(y[:, :, 0:4, :], 1, 4)
            times(tmp[:], 0, 12)
            link(nc.vector.tensor_tensor(y[:, :, 0:4, :], y[:, :, 0:4, :], tmp[:], ALU.add))
            times(y[:, :, 4:8, :], 1, 12)
            times(tmp[:], 0, 4)
            link(nc.vector.tensor_tensor(y[:, :, 4:8, :], y[:, :, 4:8, :], tmp[:], ALU.subtract))
            dve.sem_inc(moved, 1)

        @block.scalar
        def _(act):
            act.wait_ge(step, 2)
            nc.scalar.activation(lg[:], size[:], ACT.Ln).then_inc(logs, 1)
            act.wait_ge(step, 10)
            nc.scalar.activation(sc[:, :, 1, :], frac[:], ACT.Sin, scale=TWO_PI).then_inc(sines, 1)
            nc.scalar.activation(sc[:, :, 0, :], mag[:], ACT.Sin, scale=-TWO_PI, bias=halfpi[:]).then_inc(sines, 1)
            for i in range(4 * NT + NT * P // 512):
                act.wait_ge(turned, i + 1)
                t = i // 4
                if t < NT:
                    if t >= 2 and i % 4 == 0:
                        act.wait_ge(row_stored[t % 2], 16 * (t // 2))
                    dst = row[t % 2][:, (i % 4) * 512:(i % 4 + 1) * 512]
                else:
                    j = i - 4 * NT
                    dst = zrow[:, j * 512:(j + 1) * 512]
                rows = SEP if t < NT else ZROWS
                nc.scalar.copy(dst, psy[i % 4][0:rows, :]).then_inc(row_moved, 1)

        @block.tensor
        def _(pe):
            pe.wait_ge(ident_done, 2)
            pe.wait_ge(moved, 1)
            for i in range(4 * NT + NT * P // 512):
                if i >= 4:
                    pe.wait_ge(row_moved, i - 3)
                for q in range(4):
                    if i < 4 * NT:
                        src = y[:, i // 4, :, (i % 4) * 4 + q]
                    else:
                        src = z[:, (i - 4 * NT) * 4 + q, :]
                    rows = SEP if i < 4 * NT else ZROWS
                    last = nc.tensor.transpose(psy[i % 4][0:rows, q * P:(q + 1) * P], src, ident[:])
                last.then_inc(turned, 1)


def project(nc, x, ctx_t, wq, wk, wv, bq, bk, q_dram, k_dram, v_dram, negm_dram):
    with ExitStack() as ctx:
        m = Space(nc, ctx, "prj_")
        wq_sb, wk_sb, wv_sb = (m.sb(n, [P, KD, HD]) for n in ("wq", "wk", "wv"))
        bq_sb, bk_sb = m.sb("bq", [P, PAIRS]), m.sb("bk", [P, PAIRS])
        ident = m.sb("ident", [P, P])
        eps = m.sb("eps", [P, 1])
        xt = m.sb("xt", [P, NB, D])
        ct = m.sb("ct", [P, KD, S])
        stats, mv = m.sb("stats", [P, NB, 6]), m.sb("mv", [P, NB, 2])
        sd, rstd = m.sb("sd", [P, NB]), m.sb("rstd", [P, NB])
        xn_t = m.sb("xn_t", [P, KD, S])
        q_sb, k_sb, v_sb = m.sb("q", [P, PAIRS, S]), m.sb("k", [P, PAIRS, S]), m.sb("v", [P, NB, HD])
        q_r = [m.sb(f"q_r{i}", [P, S], F32R) for i in range(2)]
        k_r = [m.sb(f"k_r{i}", [P, S], F32R) for i in range(2)]
        top = m.sb("top", [P, NB, H])
        negm = m.sb("negm", [H, S])
        ps_t = m.ps("ps_t", [P, 2, 512])
        ps_p = [m.ps(f"ps_p{i}", [P, 512]) for i in range(2)]
        ps_s = [m.ps(f"ps_s{i}", [P, 2, 512]) for i in range(2)]

        w_in, x_in, c_in, ident_done, eps_done = (m.sem(n) for n in ("w_in", "x_in", "c_in", "ident_done", "eps_done"))
        stat, scaled, normed, turned, xn_ready = (m.sem(n) for n in ("stat", "scaled", "normed", "turned", "xn_ready"))
        proj_done, proj_moved, rounded, score_done, max_done = (
            m.sem(n) for n in ("proj_done", "proj_moved", "rounded", "score_done", "max_done"))
        max_turned, negm_ready, stored = m.sem("max_turned"), m.sem("negm_ready"), m.sem("stored")
        relay = m.sem("relay")
        NPROJ = 2 * PAIRS + 2 * NB
        NSC = PAIRS * NB
        block = ctx.enter_context(nc.Block())

        @block.sync
        def _(sp):
            for dst, src in ((wq_sb, wq), (wk_sb, wk), (wv_sb, wv)):
                sp.dma_start(dst[:], src.rearrange("(k p) n -> p k n", p=P)).then_inc(w_in, 16)
            sp.dma_start(bq_sb[:], bq).then_inc(w_in, 16)
            sp.dma_start(bk_sb[:], bk).then_inc(w_in, 16)
            with sp.Fori(0, B) as b:
                sp.wait_ge(turned, b + 1)
                sp.sem_inc(relay, 1)
                sp.dma_start(xt[:], x[bass.ds(b * S, S), :].rearrange("(t p) d -> p t d", p=P)).then_inc(x_in, 16)
                sp.wait_ge(proj_done, b * NPROJ + NPROJ)
                sp.sem_inc(relay, 1)
                sp.dma_start(ct[:], ctx_t[:, bass.ds(b * S, S)].rearrange("(k p) s -> p k s", p=P)).then_inc(c_in, 16)

        @block.gpsimd
        def _(pool):
            make_identity(nc, pool, ident, ident_done)

        @block.vector
        def _(dve):
            nc.vector.memset(eps[:], EPS)
            dve.wait_ge(w_in, 80)
            nc.vector.tensor_scalar(bq_sb[:], bq_sb[:], DK ** -0.5, None, ALU.mult).then_inc(eps_done, 1)
            with dve.Fori(0, B) as b:
                dve.wait_ge(x_in, b * 16 + 16)
                for t in range(NB):
                    nc.vector.bn_stats(stats[:, t, :], xt[:, t, :]).then_inc(stat, 1)
                dve.wait_ge(stat, b * (2 * NB + 1) + NB)
                dve.sem_inc(relay, 1)
                for t in range(NB):
                    nc.vector.bn_aggr(mv[:, t, :], stats[:, t, :]).then_inc(stat, 1)
                dve.wait_ge(scaled, b + 1)
                nc.vector.reciprocal(rstd[:], sd[:]).then_inc(stat, 1)
                dve.wait_ge(stat, b * (2 * NB + 1) + 2 * NB + 1)
                for t in range(NB):
                    nc.vector.tensor_scalar(xt[:, t, :], xt[:, t, :], mv[:, t, 0:1], rstd[:, t:t + 1],
                                            ALU.subtract, ALU.mult).then_inc(normed, 1)
                for j in range(PAIRS):
                    for t in range(NB):
                        i = j * NB + t
                        dve.wait_ge(score_done, b * NSC + i + 1 + 2 * NB)
                        nc.vector.tensor_reduce(top[:, t, 2 * j:2 * j + 2], ps_s[i % 2][:], op=ALU.max,
                                                axis=AX).then_inc(max_done, 1)

        @block.scalar
        def _(act):
            act.wait_ge(eps_done, 1)
            act.wait_ge(w_in, 80)
            with act.Fori(0, B) as b:
                act.wait_ge(stat, b * (2 * NB + 1) + 2 * NB)
                nc.scalar.activation(sd[:], mv[:, :, 1], ACT.Sqrt, bias=eps[:]).then_inc(scaled, 1)
                act.wait_ge(turned, b + 2)
                nc.scalar.copy(xn_t[:], ps_t[:]).then_inc(xn_ready, 1)
                for i in range(NPROJ):
                    act.wait_ge(proj_done, b * NPROJ + NPROJ + i + 1)
                    if i == 0:
                        act.wait_ge(stored, b * 64 + 64)
                    src = ps_p[i % 2][:]
                    if i < 2 * PAIRS and i % 2 == 0:
                        ins = nc.scalar.activation(q_sb[:, i // 2, :], src, ACT.Identity, bias=bq_sb[:, i // 2:i // 2 + 1],
                                                   scale=DK ** -0.5)
                    elif i < 2 * PAIRS:
                        ins = nc.scalar.activation(k_sb[:, i // 2, :], src, ACT.Identity, bias=bk_sb[:, i // 2:i // 2 + 1])
                    else:
                        t, half = divmod(i - 2 * PAIRS, 2)
                        ins = nc.scalar.copy(v_sb[:, t, half * 512:(half + 1) * 512], src)
                    ins.then_inc(proj_moved, 1)
                    if i < 2 * PAIRS:
                        j = i // 2
                        act.wait_ge(score_done, b * NSC + NB * (j + 1))
                        if i % 2 == 0:
                            ins = nc.scalar.activation(q_r[j % 2][:], src, ACT.Identity, bias=bq_sb[:, j:j + 1], scale=DK ** -0.5)
                        else:
                            ins = nc.scalar.activation(k_r[j % 2][:], src, ACT.Identity, bias=bk_sb[:, j:j + 1])
                        ins.then_inc(rounded, 1)
                act.wait_ge(max_turned, b + 1)
                nc.scalar.activation(negm[:], ps_t[0:H, 0, :], ACT.Copy, scale=-1.0).then_inc(negm_ready, 1)
                act.wait_ge(proj_moved, b * NPROJ + NPROJ + 2)
                act.dma_start(q_dram[bass.ds(b, 1)].rearrange("o p j s -> p (o j) s"), q_sb[:]).then_inc(stored, 16)
                act.dma_start(k_dram[bass.ds(b, 1)].rearrange("o p j s -> p (o j) s"), k_sb[:]).then_inc(stored, 16)
                act.dma_start(v_dram[bass.ds(b, 1)].rearrange("o p t n -> p (o t) n"), v_sb[:]).then_inc(stored, 16)
                act.wait_ge(negm_ready, b + 2)
                act.dma_start(negm_dram[bass.ds(b, 1)].rearrange("o h s -> h (o s)"), negm[:]).then_inc(stored, 16)
            act.wait_ge(stored, 64 * B + 64)

        @block.tensor
        def _(pe):
            for free, count in ((turned, 1), (proj_done, NPROJ), (proj_moved, 2), (score_done, 2 * NB),
                                (max_done, 2), (negm_ready, 1), (stored, 64)):
                pe.sem_inc(free, count)
            pe.wait_ge(ident_done, 2)
            pe.wait_ge(w_in, 80)
            with pe.Fori(0, B) as b:
                pe.wait_ge(normed, b * NB + NB)
                pe.wait_ge(negm_ready, b + 1)
                for t in range(NB):
                    for k in range(KD):
                        last = nc.tensor.transpose(ps_t[:, k, t * P:(t + 1) * P], xt[:, t, k * P:(k + 1) * P], ident[:])
                last.then_inc(turned, 1)
                pe.wait_ge(xn_ready, b + 1)
                pe.wait_ge(c_in, b * 16 + 16)

                def products(i):
                    pe.wait_ge(proj_moved, b * NPROJ + i + 1)
                    if 2 <= i < 2 * PAIRS + 2:
                        pe.wait_ge(rounded, b * 2 * PAIRS + i - 1)
                    out = ps_p[i % 2][:]
                    for k in range(KD):
                        if i < 2 * PAIRS:
                            w, src = (wq_sb, xn_t) if i % 2 == 0 else (wk_sb, ct)
                            j = i // 2
                            last = nc.tensor.matmul(out, w[:, k, j * P:(j + 1) * P], src[:, k, :], start=k == 0, stop=k == KD - 1)
                        else:
                            t, half = divmod(i - 2 * PAIRS, 2)
                            last = nc.tensor.matmul(out, ct[:, k, t * P:(t + 1) * P], wv_sb[:, k, half * 512:(half + 1) * 512],
                                                    start=k == 0, stop=k == KD - 1)
                    last.then_inc(proj_done, 1)

                def scores(j):
                    pe.wait_ge(rounded, b * 2 * PAIRS + 2 * j + 2)
                    for t in range(NB):
                        i = j * NB + t
                        pe.wait_ge(max_done, b * NSC + i + 1)
                        for half in range(2):
                            r = slice(64 * half, 64 * half + 64)
                            last = nc.tensor.matmul(ps_s[i % 2][:, half, :], q_r[j % 2][r, t * P:(t + 1) * P],
                                                    k_r[j % 2][r, :], start=True, stop=True)
                        last.then_inc(score_done, 1)

                for j in range(PAIRS):
                    products(2 * j)
                    products(2 * j + 1)
                    if j >= 1:
                        scores(j - 1)
                for i in range(2 * PAIRS, NPROJ):
                    products(i)
                scores(PAIRS - 1)
                pe.wait_ge(max_done, b * NSC + NSC + 2)
                for t in range(NB):
                    last = nc.tensor.transpose(ps_t[0:H, 0, t * P:(t + 1) * P], top[:, t, :], ident[:])
                last.then_inc(max_turned, 1)


def attend(nc, x, q_dram, k_dram, v_dram, negm_dram, y_dram, z_dram, wg_feat, wo, bv, bo, gate,
           centre, inv_size, x1_dram):
    with ExitStack() as ctx:
        m = Space(nc, ctx, "att_")
        prob = [m.sb(f"prob{i}", [P, H, S]) for i in range(2)]
        q_sb = m.sb("q", [P, PAIRS, S])
        k_sb = [m.sb(f"k{i}", [P, PAIRS, P]) for i in range(2)]
        v_sb = [m.sb(f"v{i}", [P, PAIRS, 192]) for i in range(2)]
        acc = m.sb("acc", [P, H, S])
        stat = [m.sb(f"stat{i}", [GEO_K, 16, P]) for i in range(2)]
        wide = [m.sb(f"wide{i}", [GEO_K, H, P]) for i in range(2)]
        feat = m.sb("feat", [P, 8, NB, P])
        cm = m.sb("cm", [P, 2, S])
        dist = m.sb("dist", [P, 2, NB, P])
        frac = m.sb("frac", [P, 2, 2, NB, P])
        negm = m.sb("negm", [H, S], F32R)
        negm_in_sb = m.sb("negm_in", [H, S])
        ident_r = m.sb("ident_r", [H, H], F32R)
        bias_row = m.sb("bias_row", [P, D])
        tg, halfpi, wcol = m.sb("tg", [P, 1]), m.sb("halfpi", [P, 1]), m.sb("wcol", [GEO_K, H])
        bv_sb = m.sb("bv", [P, PAIRS])
        flat = feat[:].rearrange("p f n m -> p (f n m)")
        wo_sb = flat[:, 0:2048].rearrange("p (j d) -> p j d", j=PAIRS)
        x_sb = flat[:, 2048:3072].rearrange("p (t d) -> p t d", t=NB)
        x1_sb = flat[:, 3072:4096].rearrange("p (t d) -> p t d", t=NB)
        bvw = frac[:].rearrange("p a b n m -> p (a b n m)")[:, 0:PAIRS * P].rearrange("p (j n) -> p j n", j=PAIRS)
        ones16 = dist[0:H, 0, 0, 0:H]
        mask = dist[0:GEO_K, 0, 1, :]
        ps_s = [m.ps(f"ps_s{i}", [P, 2, 512]) for i in range(2)]
        ps_g = [m.ps(f"ps_g{i}", [P, 512]) for i in range(2)]
        ps_o = [m.ps(f"ps_o{i}", [P, 512]) for i in range(2)]

        sem = m.sem
        pro_in, pro_pool, pro_dve, pro_act, pro_pe = (sem(n) for n in ("pro_in", "pro_pool", "pro_dve", "pro_act", "pro_pe"))
        q_in, nm_in, c_in, w_in, relay = (sem(n) for n in ("q_in", "nm_in", "c_in", "w_in", "relay"))
        k_in, v_in, stat_in = ([sem(f"{n}{i}") for i in range(2)] for n in ("k_in", "v_in", "stat_in"))
        nm_ready, s_done, exp_done, g_done, mult_done = (sem(n) for n in ("nm_ready", "s_done", "exp_done", "g_done", "mult_done"))
        pv_done, acc_done, normed, out_done, x1_done, x1_stored = (
            sem(n) for n in ("pv_done", "acc_done", "normed", "out_done", "x1_done", "x1_stored"))
        delta, clipped, logs, turns, fracs, mags, sines = (
            sem(n) for n in ("delta", "clipped", "logs", "turns", "fracs", "mags", "sines"))
        turned2 = sem('x1_part')
        SP_, G_, V_ = 8 * NB, 16 * NB, H * NB
        STAT = 18 * 16
        block = ctx.enter_context(nc.Block())

        @block.sync
        def _(sp):
            sp.dma_start(wo_sb, wo.rearrange("(j p) d -> p j d", p=P)).then_inc(pro_in, 16)
            sp.dma_start(bias_row[:], bo.partition_broadcast(P)).then_inc(pro_in, 16)
            sp.dma_start(bv_sb[:], bv).then_inc(pro_in, 16)
            sp.dma_start(tg[:], gate.partition_broadcast(P)).then_inc(pro_in, 16)
            sp.wait_ge(pro_pool, 1)
            for n in range(8):
                sp.dma_start(wcol[SEP + 8 * n:SEP + 8 * n + 8, :], wg_feat).then_inc(pro_in, 16)
            sp.wait_ge(pro_pe, 1)
            sp.wait_ge(pro_dve, 4)
            with sp.Fori(0, B) as b:
                sp.wait_ge(s_done, b * SP_ + 16)
                sp.sem_inc(relay, 1)
                sp.dma_start(q_sb[:], q_dram[bass.ds(b, 1)].rearrange("o p j s -> p (o j) s")).then_inc(q_in, 16)
                sp.dma_start(negm_in_sb[:], negm_dram[bass.ds(b, 1)].rearrange("o h s -> h (o s)")).then_inc(nm_in, 16)
                sp.wait_ge(delta, b * 12 + 1)
                sp.sem_inc(relay, 1)
                for c in range(2):
                    sp.dma_start(cm[:, c, :], z_dram[SEP + c, bass.ds(b, 1), :].rearrange("o s -> (o s)").partition_broadcast(P)
                                 ).then_inc(c_in, 16)

                def load_kv(u):
                    i = u % 2
                    sp.wait_ge(s_done, b * SP_ + 8 * (u + 1))
                    sp.sem_inc(relay, 1)
                    sp.dma_start(k_sb[i][:], k_dram[bass.ds(b, 1), :, :, u * P:(u + 1) * P].rearrange("o p j s -> p (o j) s")
                                 ).then_inc(k_in[i], 16)
                    sp.wait_ge(pv_done, b * V_ + H * (u + 1))
                    sp.sem_inc(relay, 1)
                    src = v_dram[bass.ds(b, 1), :, u, :].rearrange("o p (j e d) -> p (o j) e d", e=2, d=DK)
                    for e in range(2):
                        sp.dma_start(v_sb[i][:, :, 128 * e:128 * e + DK], src[:, :, e, :]).then_inc(v_in[i], 16)

                load_kv(0)
                load_kv(1)
                for w in range(NB):
                    for blk in range(NB):
                        k = NB * w + blk
                        i = k % 2
                        sp.wait_ge(g_done, b * G_ + 4 * (k + 1))
                        sp.sem_inc(relay, 1)
                        sp.wait_ge(sines, b * 8 + 2 * (w + 1) + 2)
                        sp.sem_inc(relay, 1)
                        for grp in range(16):
                            sp.dma_start(stat[i][SEP:GEO_K, grp, :], feat[8 * grp:8 * grp + 8, :, blk, :]).then_inc(stat_in[i], 16)
                        sp.dma_start(stat[i][0:SEP, :, :],
                                     z_dram[0:SEP, bass.ds(b, 1), w * P:(w + 1) * P].to_broadcast([SEP, 16, P])).then_inc(stat_in[i], 16)
                        sp.dma_start(wide[i][0:SEP, :, :],
                                     y_dram[bass.ds(b * NB + blk, 1)].rearrange("o k (h n) -> k (o h) n", h=H)).then_inc(stat_in[i], 16)
                    if w + 2 < NB:
                        load_kv(w + 2)
                for i in range(2):
                    sp.wait_ge(stat_in[i], (b + 1) * 8 * STAT)
                sp.sem_inc(relay, 1)
                sp.dma_start(wo_sb, wo.rearrange("(j p) d -> p j d", p=P)).then_inc(w_in, 16)
                sp.dma_start(x_sb, x[bass.ds(b * S, S), :].rearrange("(t p) d -> p t d", p=P)).then_inc(w_in, 16)
                sp.wait_ge(x1_done, b * NB + NB + 1)
                sp.sem_inc(relay, 1)
                sp.dma_start(x1_dram[bass.ds(b * S, S), :].rearrange("(t p) d -> p t d", p=P), x1_sb).then_inc(x1_stored, 16)
            sp.wait_ge(x1_stored, 16 * B + 16)

        @block.gpsimd
        def _(pool):
            nc.gpsimd.memset(wcol[:], 0.0).then_inc(pro_pool, 1)
            nc.gpsimd.memset(mask, 1.0).then_inc(pro_pool, 1)
            nc.gpsimd.memset(ones16, 1.0).then_inc(pro_pool, 1)
            pool.wait_ge(pro_pool, 3)
            nc.gpsimd.affine_select(out=mask, in_=mask, compare_op=ALU.is_ge, fill=0.0, base=-SEP,
                                    pattern=[[0, 16], [-8, 8]], channel_multiplier=1).then_inc(pro_pool, 1)
            pool.wait_ge(pro_pool, 4)
            nc.gpsimd.affine_select(out=mask, in_=mask, compare_op=ALU.is_ge, fill=0.0, base=SEP + 7,
                                    pattern=[[0, 16], [8, 8]], channel_multiplier=-1).then_inc(pro_pool, 1)
            nc.gpsimd.affine_select(out=ones16, in_=ones16, compare_op=ALU.is_equal, fill=0.0, base=0,
                                    pattern=[[-1, H]], channel_multiplier=1).then_inc(pro_pool, 1)
            pool.wait_ge(pro_dve, 4)
            with pool.Fori(0, B) as b:
                pool.wait_ge(c_in, b * 32 + 32)
                pool.sem_inc(relay, 1)
                for u in range(NB):
                    rows = cm[:, :, u * P:(u + 1) * P].unsqueeze(2).to_broadcast([P, 2, NB, P])
                    for c in range(2):
                        cols = centre[:, bass.ds(b * NB, NB), c].unsqueeze(2).to_broadcast([P, NB, P])
                        if c == 0:
                            pool.wait_ge(fracs, b * NB + u + 1)
                            pool.sem_inc(relay, 1)
                        last = nc.gpsimd.tensor_tensor(dist[:, c], rows[:, c], cols, ALU.subtract)
                    last.then_inc(delta, 1)
                    pool.wait_ge(delta, b * 12 + 3 * u + 2)
                    pool.sem_inc(relay, 1)
                    for c in range(2):
                        cols = inv_size[:, bass.ds(b * NB, NB), c].unsqueeze(2).to_broadcast([P, NB, P])
                        last = nc.gpsimd.tensor_tensor(dist[:, c], dist[:, c], cols, ALU.mult)
                    last.then_inc(delta, 1)
                    pool.wait_ge(delta, b * 12 + 3 * u + 3)
                    nc.gpsimd.tensor_tensor(dist[:], dist[:], dist[:], ALU.mult).then_inc(delta, 1)

        @block.scalar
        def _(act):
            act.wait_ge(pro_in, 192)
            nc.scalar.activation(tg[:], tg[:], ACT.Tanh).then_inc(pro_act, 1)
            act.wait_ge(pro_dve, 4)
            with act.Fori(0, B) as b:
                act.wait_ge(nm_in, b * 16 + 16)
                nc.scalar.copy(negm[:], negm_in_sb[:]).then_inc(nm_ready, 1)
                for u in range(NB):
                    act.wait_ge(clipped, b * NB + u + 1)
                    nc.scalar.activation(dist[:], dist[:], ACT.Ln).then_inc(logs, 1)
                    for j in range(PAIRS):
                        k = PAIRS * u + j
                        act.wait_ge(s_done, b * SP_ + k + 1 + 16)
                        nc.scalar.activation(prob[u % 2][:, 2 * j:2 * j + 2, :], ps_s[k % 2][:], ACT.Exp).then_inc(exp_done, 1)
                    act.wait_ge(fracs, b * NB + u + 2)
                    if u == 0:
                        act.wait_ge(x1_stored, b * 16 + 16)
                    else:
                        for i in range(2):
                            act.wait_ge(stat_in[i], b * 8 * STAT + 2 * u * STAT)
                    nc.scalar.activation(feat[:, 0:4], frac[:].rearrange("p a b n m -> p (a b) n m"), ACT.Sin,
                                         scale=TWO_PI).then_inc(sines, 1)
                    act.wait_ge(mags, b * NB + u + 1)
                    nc.scalar.activation(feat[:, 4:8], frac[:].rearrange("p a b n m -> p (a b) n m"), ACT.Sin,
                                         scale=-TWO_PI, bias=halfpi[:]).then_inc(sines, 1)

        @block.vector
        def _(dve):
            nc.vector.memset(halfpi[:], HALF_PI)
            for i in range(2):
                nc.vector.memset(v_sb[i][:, :, DK:128], 1.0)
            dve.wait_ge(pro_in, 192)
            dve.wait_ge(pro_pool, 6)
            for i in range(2):
                nc.vector.tensor_tensor(wide[i][:], mask.unsqueeze(1).to_broadcast([GEO_K, H, P]),
                                        wcol[:].unsqueeze(2).to_broadcast([GEO_K, H, P]), ALU.mult)
            nc.vector.tensor_copy(bvw, bv_sb[:].unsqueeze(2).to_broadcast([P, PAIRS, P])).then_inc(pro_dve, 1)
            nc.vector.tensor_copy(ident_r[:], ones16).then_inc(pro_dve, 1)
            dve.wait_ge(pro_pe, 1)
            dve.wait_ge(pro_act, 1)
            nc.vector.tensor_tensor(bias_row[:], ps_g[0][:, 0:D], bias_row[:], ALU.add).then_inc(pro_dve, 1)
            dve.wait_ge(pro_dve, 3)
            nc.vector.tensor_scalar(bias_row[:], bias_row[:], tg[:], None, ALU.mult).then_inc(pro_dve, 1)
            dve.wait_ge(pro_dve, 4)
            with dve.Fori(0, B) as b:
                def clip(u):
                    dve.wait_ge(delta, b * 12 + 3 * u + 4)
                    nc.vector.tensor_scalar(dist[:], dist[:], 1e-6, None, ALU.max).then_inc(clipped, 1)

                def fractions(u):
                    dve.wait_ge(logs, b * NB + u + 1)
                    dve.wait_ge(sines, b * 8 + 2 * u + 2)
                    for f in range(2):
                        nc.vector.tensor_scalar(frac[:, f], dist[:], 50.0 * FREQ[f] / TWO_PI, ROUND, ALU.mult, ALU.add
                                                ).then_inc(turns, 1)
                    for f in range(2):
                        dve.wait_ge(turns, b * 16 + 4 * u + 1 + f)
                        nc.vector.tensor_scalar(frac[:, f], frac[:, f], ROUND, None, ALU.subtract).then_inc(turns, 1)
                    for f in range(2):
                        dve.wait_ge(turns, b * 16 + 4 * u + 3 + f)
                        last = nc.vector.scalar_tensor_tensor(
                            out=frac[:, f].rearrange("p b n m -> p (b n m)"), in0=dist[:].rearrange("p b n m -> p (b n m)"),
                            scalar=50.0 * FREQ[f] / TWO_PI, in1=frac[:, f].rearrange("p b n m -> p (b n m)"),
                            op0=ALU.mult, op1=ALU.subtract)
                    last.then_inc(fracs, 1)

                def magnitudes(u):
                    dve.wait_ge(sines, b * 8 + 2 * u + 3)
                    v = frac[:].bitcast(I32)
                    nc.vector.tensor_single_scalar(v, v, 0x7FFFFFFF, op=ALU.bitwise_and).then_inc(mags, 1)

                clip(0)
                for s in range(NB + 1):
                    w = s - 1
                    if w < 0:
                        fractions(0)
                        magnitudes(0)
                        clip(1)
                        continue
                    for c in range(16):
                        k = 16 * w + c
                        if c == 0:
                            dve.wait_ge(exp_done, b * SP_ + 8 * (w + 1) + 2)
                        dve.wait_ge(g_done, b * G_ + k + 1 + 8)
                        e = prob[w % 2][:, :, 32 * c:32 * c + 32]
                        nc.vector.scalar_tensor_tensor(out=e, in0=ps_g[k % 2][:].rearrange("p (h n) -> p h n", h=H),
                                                       scalar=GEO_MIN, in1=e, op0=ALU.max, op1=ALU.mult).then_inc(mult_done, 1)
                        if c == 7 and s < NB:
                            fractions(s)
                    for h in range(H):
                        k = H * w + h
                        dve.wait_ge(pv_done, b * V_ + k + 1 + 2 * H)
                        if w == 0:
                            ins = nc.vector.tensor_copy(acc[:, h, :], ps_o[k % 2][:])
                        else:
                            ins = nc.vector.tensor_tensor(acc[:, h, :], ps_o[k % 2][:], acc[:, h, :], ALU.add)
                        ins.then_inc(acc_done, 1)
                        if h == 9 and s < NB:
                            magnitudes(s)
                    if s + 1 < NB:
                        clip(s + 1)
                rec = frac[:].rearrange("p a b n m -> p (a b) (n m)")
                heads = acc[:].rearrange("p (j e) s -> p j e s", e=2)
                dve.wait_ge(acc_done, (b + 1) * V_ + 2)
                dve.wait_ge(sines, b * 8 + 10)
                for half in range(2):
                    js = slice(4 * half, 4 * half + 4)
                    nc.vector.reciprocal(rec[0:64], heads[64:128, js, 0, :]).then_inc(normed, 1)
                    nc.vector.reciprocal(rec[64:128], heads[0:64, js, 1, :]).then_inc(normed, 1)
                    dve.wait_ge(normed, b * 8 + 4 * half + 2)
                    nc.vector.tensor_tensor(heads[0:64, js, 0, :], heads[0:64, js, 0, :], rec[0:64], ALU.mult).then_inc(normed, 1)
                    nc.vector.tensor_tensor(heads[64:128, js, 0, :], heads[64:128, js, 1, :], rec[64:128], ALU.mult).then_inc(normed, 1)
                    dve.wait_ge(normed, b * 8 + 4 * half + 4)
                dve.wait_ge(w_in, b * 32 + 32)
                for t in range(NB):
                    dve.wait_ge(out_done, b * NB + t + 1)
                    nc.vector.scalar_tensor_tensor(out=x1_sb[:, t, :], in0=ps_g[t % 2][:, 0:D], scalar=tg[:], in1=bias_row[:],
                                                   op0=ALU.mult, op1=ALU.add).then_inc(turned2, 1)
                    dve.wait_ge(turned2, b * NB + t + 1)
                    nc.vector.tensor_tensor(x1_sb[:, t, :], x1_sb[:, t, :], x_sb[:, t, :], ALU.add).then_inc(x1_done, 1)

        @block.tensor
        def _(pe):
            for free, count in ((s_done, 16), (pv_done, 2 * H), (g_done, 8), (sines, 2), (delta, 1), (x1_done, 1),
                                (exp_done, 2), (mult_done, 2), (acc_done, 2), (x1_stored, 16), (fracs, 1)):
                pe.sem_inc(free, count)
            pe.wait_ge(pro_in, 192)
            pe.wait_ge(pro_dve, 1)
            for j in range(PAIRS):
                last = nc.tensor.matmul(ps_g[0][:, 0:D], bvw[:, j, :], wo_sb[:, j, :], start=j == 0, stop=j == PAIRS - 1)
            last.then_inc(pro_pe, 1)
            pe.wait_ge(pro_dve, 4)
            with pe.Fori(0, B) as b:
                def scores(u, j):
                    k = PAIRS * u + j
                    pe.wait_ge(exp_done, b * SP_ + k + 1)
                    for e in range(2):
                        r = slice(64 * e, 64 * e + 64)
                        nc.tensor.matmul(ps_s[k % 2][:, e, :], k_sb[u % 2][r, j, :], q_sb[r, j, :], start=True, stop=False)
                    for e in range(2):
                        h = 2 * j + e
                        last = nc.tensor.matmul(ps_s[k % 2][:, e, :], ident_r[:, h:h + 1].to_broadcast([H, P]), negm[:],
                                                start=False, stop=True)
                    last.then_inc(s_done, 1)

                def geometry(w, c):
                    k = 16 * w + c
                    blk = NB * w + c // 4
                    if c % 4 == 0:
                        pe.wait_ge(stat_in[blk % 2], b * 8 * STAT + STAT * (blk // 2 + 1))
                    pe.wait_ge(mult_done, b * G_ + k + 1)
                    out = ps_g[k % 2][:].rearrange("p (h n) -> p h n", h=H)
                    for g in range(4):
                        grp = 4 * (c % 4) + g
                        last = nc.tensor.matmul(out[:, :, 8 * g:8 * g + 8], stat[blk % 2][:, grp, :],
                                                wide[blk % 2][:, :, 8 * grp:8 * grp + 8], start=True, stop=True)
                    last.then_inc(g_done, 1)

                for s in range(NB + 1):
                    w = s - 1
                    if s == 0:
                        pe.wait_ge(q_in, b * 16 + 16)
                        pe.wait_ge(nm_ready, b + 1)
                    if s == 1:
                        pe.wait_ge(x1_done, b * NB + 1)
                    if s < NB:
                        pe.wait_ge(k_in[s % 2], b * 32 + 16 * (s // 2) + 16)
                    for j in range(PAIRS):
                        if s < NB:
                            scores(s, j)
                        if w >= 0:
                            geometry(w, 2 * j)
                            geometry(w, 2 * j + 1)
                    if w < 0:
                        continue
                    pe.wait_ge(mult_done, b * G_ + 16 * (w + 1) + 2)
                    pe.wait_ge(v_in[w % 2], b * 64 + 32 * (w // 2) + 32)
                    for h in range(H):
                        k = H * w + h
                        pe.wait_ge(acc_done, b * V_ + k + 1)
                        c = 0 if h % 2 == 0 else DK
                        nc.tensor.matmul(ps_o[k % 2][:], v_sb[w % 2][:, h // 2, c:c + P], prob[w % 2][:, h, :],
                                         start=True, stop=True).then_inc(pv_done, 1)
                pe.wait_ge(normed, b * 8 + 8)
                pe.wait_ge(w_in, b * 32 + 32)
                for t in range(NB):
                    if t >= 2:
                        pe.wait_ge(x1_done, b * NB + t)
                    for j in range(PAIRS):
                        last = nc.tensor.matmul(ps_g[t % 2][:, 0:D], acc[:, 2 * j, t * P:(t + 1) * P], wo_sb[:, j, :],
                                                start=j == 0, stop=j == PAIRS - 1)
                    last.then_inc(out_done, 1)


def route(nc, x1_dram, rw1, rb1, rw2, rb2, gate, xs_dram, slot, weight, tile_expert):
    with ExitStack() as ctx:
        m = Space(nc, ctx, "rt_")
        rw1_sb, rb1_sb = m.sb("rw1", [P, KD, HID]), m.sb("rb1", [P, HID // P])
        rw2_sb, rb2_sb = m.sb("rw2", [P, HID // P, E]), m.sb("rb2", [P, E])
        tg = m.sb("tg", [P, 1])
        ident, eps, zeros = m.sb("ident", [P, P]), m.sb("eps", [P, 1]), m.sb("zeros", [P, 8, D])
        below, ones = m.sb("below", [P, P]), m.sb("ones", [P, P])
        xt = [m.sb(f"xt{i}", [P, NB, D]) for i in range(1)][0]
        xn = m.sb("xn", [P, NT, D])
        stats, mv = m.sb("stats", [P, NB, 6]), m.sb("mv", [P, NB, 2])
        sd, rstd = m.sb("sd", [P, NB]), m.sb("rstd", [P, NB])
        xn_t, hid = m.sb("xn_t", [P, KD, S]), m.sb("hid", [P, HID // P, S])
        lg = m.sb("lg", [P, NT, E])
        top, top_i = m.sb("top", [P, NT, 8]), m.sb("top_i", [P, NT, 8], U32)
        top_f = m.sb("top_f", [P, NT, 2])
        iota_i, iota_f = m.sb("iota_i", [P, E], I32), m.sb("iota_f", [P, E])
        one_hot = [m.sb(f"one_hot{i}", [P, NT, E]) for i in range(2)]
        both, before, upto, total = (m.sb(n, [P, NT, E]) for n in ("both", "before", "upto", "total"))
        gap, den = m.sb("gap", [P, NT]), m.sb("den", [P, NT])
        tiles, tiles_r, first = m.sb("tiles", [P, E]), m.sb("tiles_r", [P, E]), m.sb("first", [P, E])
        slot_f = m.sb("slot_f", [P, NT, 2])
        tile_i, reached = m.sb("tile_i", [1, N_TILES], I32), m.sb("reached", [1, N_TILES, E])
        tile_f, te_f = m.sb("tile_f", [1, N_TILES]), m.sb("te_f", [1, N_TILES])
        ps_t = m.ps("ps_t", [P, 2, 512])
        ps_h = [m.ps(f"ps_h{i}", [P, 512]) for i in range(2)]
        ps_l, ps_c, ps_n = m.ps("ps_l", [P, NB, E]), m.ps("ps_c", [P, 512]), m.ps("ps_n", [P, 512])

        sem = m.sem
        w_in, x_in, zeroed, zero_stored, pool_done, eps_done, relay = (
            sem(n) for n in ("w_in", "x_in", "zeroed", "zero_stored", "pool_done", "eps_done", "relay"))
        stat, scaled, normed, kept, turned, xn_ready = (sem(n) for n in ("stat", "scaled", "normed", "kept", "turned", "xn_ready"))
        h_done, h_ready, l_done, l_ready = (sem(n) for n in ("h_done", "h_ready", "l_done", "l_ready"))
        tg_done, step, gap_exp, counted, slots_ready, scattered = (
            sem(n) for n in ("tg_done", "step", "gap_exp", "counted", "slots_ready", "scattered"))
        NH = HID // P
        block = ctx.enter_context(nc.Block())

        @block.sync
        def _(sp):
            sp.dma_start(rw1_sb[:], rw1.rearrange("(k p) n -> p k n", p=P)).then_inc(w_in, 16)
            sp.dma_start(rb1_sb[:], rb1).then_inc(w_in, 16)
            sp.dma_start(rw2_sb[:], rw2.rearrange("(j p) e -> p j e", p=P)).then_inc(w_in, 16)
            sp.dma_start(rb2_sb[:], rb2.partition_broadcast(P)).then_inc(w_in, 16)
            sp.dma_start(tg[:], gate.partition_broadcast(P)).then_inc(w_in, 16)
            sp.wait_ge(zeroed, 1)
            for i in range(SLOTS // (8 * P)):
                sp.dma_start(xs_dram[i * 8 * P:(i + 1) * 8 * P, :].rearrange("(t p) d -> p t d", p=P), zeros[:]).then_inc(zero_stored, 16)
            with sp.Fori(0, B) as b:
                sp.wait_ge(kept, b + 1)
                sp.sem_inc(relay, 1)
                sp.wait_ge(turned, b + 1)
                sp.sem_inc(relay, 1)
                sp.dma_start(xt[:], x1_dram[bass.ds(b * S, S), :].rearrange("(t p) d -> p t d", p=P)).then_inc(x_in, 16)
            sp.wait_ge(zero_stored, 16 * (SLOTS // (8 * P)))

        @block.gpsimd
        def _(pool):
            nc.gpsimd.memset(zeros[:], 0.0).then_inc(zeroed, 1)
            make_identity(nc, pool, ident, pool_done)
            nc.gpsimd.memset(ones[:], 1.0).then_inc(pool_done, 1)
            pool.wait_ge(pool_done, 3)
            nc.gpsimd.affine_select(out=below[:], in_=ones[:], compare_op=ALU.is_gt, fill=0.0, base=0,
                                    pattern=[[1, P]], channel_multiplier=-1).then_inc(pool_done, 1)
            nc.gpsimd.iota(iota_i[:], pattern=[[1, E]], base=0, channel_multiplier=0).then_inc(pool_done, 1)
            nc.gpsimd.iota(tile_i[:], pattern=[[SLOT_TILE, N_TILES]], base=0, channel_multiplier=0).then_inc(pool_done, 1)
            with pool.Fori(0, B) as b:
                pool.wait_ge(normed, b * NB + NB)
                pool.sem_inc(relay, 1)
                nc.gpsimd.tensor_copy(xn[:, bass.ds(b * NB, NB), :], xt[:]).then_inc(kept, 1)
            pool.wait_ge(kept, B + 1)
            pool.wait_ge(slots_ready, 1)
            pool.wait_ge(zero_stored, 16 * (SLOTS // (8 * P)))
            for t in range(NT):
                for c in range(2):
                    nc.gpsimd.indirect_dma_start(xs_dram, bass.IndirectOffsetOnAxis(slot[:, c, t:t + 1], 0), xn[:, t, :], None
                                                 ).then_inc(scattered, 16)
            pool.wait_ge(scattered, 32 * NT)

        @block.vector
        def _(dve):
            nc.vector.memset(eps[:], EPS).then_inc(eps_done, 1)
            with dve.Fori(0, B) as b:
                dve.wait_ge(x_in, b * 16 + 16)
                for t in range(NB):
                    nc.vector.bn_stats(stats[:, t, :], xt[:, t, :]).then_inc(stat, 1)
                dve.wait_ge(stat, b * (2 * NB + 1) + NB)
                dve.sem_inc(relay, 1)
                for t in range(NB):
                    nc.vector.bn_aggr(mv[:, t, :], stats[:, t, :]).then_inc(stat, 1)
                dve.wait_ge(scaled, b + 1)
                nc.vector.reciprocal(rstd[:], sd[:]).then_inc(stat, 1)
                dve.wait_ge(stat, b * (2 * NB + 1) + 2 * NB + 1)
                for t in range(NB):
                    nc.vector.tensor_scalar(xt[:, t, :], xt[:, t, :], mv[:, t, 0:1], rstd[:, t:t + 1],
                                            ALU.subtract, ALU.mult).then_inc(normed, 1)
                dve.wait_ge(l_done, b + 1)
                nc.vector.tensor_tensor(lg[:, bass.ds(b * NB, NB), :], ps_l[:], rb2_sb[:].unsqueeze(1).to_broadcast([P, NB, E]),
                                        ALU.add).then_inc(l_ready, 1)
            count = [0]

            def link(ins):
                count[0] += 1
                ins.then_inc(step, 1)
                dve.wait_ge(step, count[0])

            dve.wait_ge(l_ready, B + 1)
            dve.wait_ge(pool_done, 6)
            for t in range(NT):
                last = nc.vector.max(top[:, t, :], lg[:, t, :])
            link(last)
            for t in range(NT):
                nc.vector.max_index(top_i[:, t, :], top[:, t, :], lg[:, t, :])
            nc.vector.tensor_copy(iota_f[:], iota_i[:])
            nc.vector.tensor_copy(tile_f[:], tile_i[:])
            link(nc.vector.tensor_tensor(gap[:], top[:, :, 1], top[:, :, 0], ALU.subtract))
            link(nc.vector.tensor_copy(top_f[:], top_i[:, :, 0:2]))
            for c in range(2):
                link(nc.vector.tensor_tensor(one_hot[c][:], top_f[:, :, c:c + 1].to_broadcast([P, NT, E]),
                                             iota_f[:].unsqueeze(1).to_broadcast([P, NT, E]), ALU.is_equal))
            nc.vector.tensor_tensor(both[:], one_hot[0][:], one_hot[1][:], ALU.add).then_inc(counted, 1)
            dve.wait_ge(gap_exp, 1)
            link(nc.vector.tensor_scalar(den[:], gap[:], 1.0, None, ALU.add))
            link(nc.vector.reciprocal(den[:], den[:]))
            link(nc.vector.tensor_scalar(weight[:, 0, :], den[:], tg[:], None, ALU.mult))
            nc.vector.tensor_tensor(weight[:, 1, :], weight[:, 0, :], gap[:], ALU.mult)
            dve.wait_ge(counted, 2)
            link(nc.vector.tensor_copy(total[:].rearrange("p t e -> p (t e)"), ps_n[:, 0:NT * E]))
            for e in range(E):
                last = nc.vector.tensor_tensor_scan(out=upto[:, :, e], data0=total[:, :, e], data1=zeros[:, 0, 0:NT],
                                                    initial=0.0, op0=ALU.add, op1=ALU.add)
            link(last)
            nc.vector.tensor_tensor(before[:], upto[:], total[:], ALU.subtract)
            link(nc.vector.tensor_scalar(tiles[:], upto[:, NT - 1, :], 1.0 / SLOT_TILE,
                                         (SLOT_TILE - 1.0) / SLOT_TILE - 0.5 + 0.5 / SLOT_TILE, ALU.mult, ALU.add))
            link(nc.vector.tensor_scalar(tiles_r[:], tiles[:], ROUND, None, ALU.add))
            link(nc.vector.tensor_scalar(tiles[:], tiles_r[:], ROUND, float(SLOT_TILE), ALU.subtract, ALU.mult))
            link(nc.vector.tensor_tensor_scan(out=first[:], data0=tiles[:], data1=zeros[:, 0, 0:E], initial=0.0,
                                              op0=ALU.add, op1=ALU.add))
            link(nc.vector.tensor_tensor(first[:], first[:], tiles[:], ALU.subtract))
            link(nc.vector.tensor_tensor(before[:].rearrange("p t e -> p (t e)"), before[:].rearrange("p t e -> p (t e)"),
                                         ps_c[:, 0:NT * E], ALU.add))
            link(nc.vector.tensor_tensor(before[:], before[:], first[:].unsqueeze(1).to_broadcast([P, NT, E]), ALU.add))
            for c in range(2):
                link(nc.vector.tensor_tensor(one_hot[c][:], one_hot[c][:], before[:], ALU.mult))
                link(nc.vector.tensor_reduce(slot_f[:, :, c], one_hot[c][:], op=ALU.add, axis=AX))
                nc.vector.tensor_copy(slot[:, c, :], slot_f[:, :, c])
            link(nc.vector.tensor_tensor(reached[:], first[0:1, :].unsqueeze(1).to_broadcast([1, N_TILES, E]),
                                         tile_f[:].unsqueeze(2).to_broadcast([1, N_TILES, E]), ALU.is_le))
            link(nc.vector.tensor_reduce(te_f[:], reached[:, :, 1:E], op=ALU.add, axis=AX))
            nc.vector.tensor_copy(tile_expert[:], te_f[:]).then_inc(slots_ready, 1)

        @block.scalar
        def _(act):
            act.wait_ge(eps_done, 1)
            act.wait_ge(w_in, 80)
            with act.Fori(0, B) as b:
                act.wait_ge(stat, b * (2 * NB + 1) + 2 * NB)
                nc.scalar.activation(sd[:], mv[:, :, 1], ACT.Sqrt, bias=eps[:]).then_inc(scaled, 1)
                act.wait_ge(turned, b + 2)
                nc.scalar.copy(xn_t[:], ps_t[:]).then_inc(xn_ready, 1)
                for j in range(NH):
                    act.wait_ge(h_done, b * NH + j + 1)
                    nc.scalar.activation(hid[:, j, :], ps_h[j % 2][:], ACT.Silu, bias=rb1_sb[:, j:j + 1]).then_inc(h_ready, 1)
            nc.scalar.activation(tg[:], tg[:], ACT.Tanh).then_inc(tg_done, 1)
            act.wait_ge(step, 3)
            act.wait_ge(tg_done, 1)
            nc.scalar.activation(gap[:], gap[:], ACT.Exp).then_inc(gap_exp, 1)

        @block.tensor
        def _(pe):
            for free, count in ((kept, 1), (turned, 1), (h_ready, 2), (l_ready, 1)):
                pe.sem_inc(free, count)
            pe.wait_ge(pool_done, 2)
            pe.wait_ge(w_in, 80)
            with pe.Fori(0, B) as b:
                pe.wait_ge(normed, b * NB + NB)
                for t in range(NB):
                    for k in range(KD):
                        last = nc.tensor.transpose(ps_t[:, k, t * P:(t + 1) * P], xt[:, t, k * P:(k + 1) * P], ident[:])
                last.then_inc(turned, 1)
                pe.wait_ge(xn_ready, b + 1)
                for j in range(NH):
                    pe.wait_ge(h_ready, b * NH + j + 1)
                    for k in range(KD):
                        last = nc.tensor.matmul(ps_h[j % 2][:], rw1_sb[:, k, j * P:(j + 1) * P], xn_t[:, k, :],
                                                start=k == 0, stop=k == KD - 1)
                    last.then_inc(h_done, 1)
                pe.wait_ge(h_ready, b * NH + NH + 2)
                pe.wait_ge(l_ready, b + 1)
                for t in range(NB):
                    for j in range(NH):
                        last = nc.tensor.matmul(ps_l[:, t, :], hid[:, j, t * P:(t + 1) * P], rw2_sb[:, j, :],
                                                start=j == 0, stop=j == NH - 1)
                last.then_inc(l_done, 1)
            pe.wait_ge(counted, 1)
            pe.wait_ge(pool_done, 4)
            flat = both[:].rearrange("p t e -> p (t e)")
            nc.tensor.matmul(ps_c[:, 0:NT * E], below[:], flat, start=True, stop=True)
            nc.tensor.matmul(ps_n[:, 0:NT * E], ones[:], flat, start=True, stop=True).then_inc(counted, 1)


def experts(nc, xs_dram, ys_dram, w1, b1, w2, b2, tile_expert):
    TB = SLOT_TILE // P
    NH = HID // P
    with ExitStack() as ctx:
        m = Space(nc, ctx, "ex_")
        w1_sb = [m.sb(f"w1{i}", [P, KD, HID]) for i in range(2)]
        w2_sb = [m.sb(f"w2{i}", [P, NH, D]) for i in range(2)]
        b1_sb = [m.sb(f"b1{i}", [P, NH]) for i in range(2)]
        b2_sb = [m.sb(f"b2{i}", [P, D]) for i in range(2)]
        xt = [m.sb(f"xt{i}", [P, TB, D]) for i in range(2)]
        x_t = [m.sb(f"x_t{i}", [P, KD, SLOT_TILE]) for i in range(2)]
        hid = [m.sb(f"hid{i}", [P, NH, SLOT_TILE]) for i in range(2)]
        yt = [m.sb(f"yt{i}", [P, TB, D]) for i in range(2)]
        ident = m.sb("ident", [P, P])
        ps_t = m.ps("ps_t", [P, KD, SLOT_TILE])
        ps_h = [m.ps(f"ps_h{i}", [P, 512]) for i in range(4)]
        ps_y = [m.ps(f"ps_y{i}", [P, TB, D]) for i in range(2)]
        sem = m.sem
        load_in = [sem(f"load_in{i}") for i in range(2)]
        stored = [sem(f"stored{i}") for i in range(2)]
        y_free, ident_done, relay, turned, x_ready, h_done, h_ready, y_done, y_ready = (
            sem(n) for n in ("y_free", "ident_done", "relay", "turned", "x_ready", "h_done", "h_ready", "y_done", "y_ready"))
        block = ctx.enter_context(nc.Block())

        @block.sync
        def _(sp):
            with sp.Fori(0, N_TILES // 2) as pair:
                for i in range(2):
                    tile = pair * 2 + i
                    e = sp.value_load(tile_expert[0:1, bass.ds(tile, 1)], min_val=0, max_val=E - 1)
                    sp.wait_ge(y_ready, pair * 2 + i + 1)
                    sp.sem_inc(relay, 1)
                    sp.dma_start(xt[i][:], xs_dram[bass.ds(tile * SLOT_TILE, SLOT_TILE), :].rearrange("(t p) d -> p t d", p=P)
                                 ).then_inc(load_in[i], 16)
                    sp.dma_start(w1_sb[i][:], w1[bass.ds(e, 1)].rearrange("o (k p) n -> p (o k) n", p=P)).then_inc(load_in[i], 16)
                    sp.dma_start(b1_sb[i][:], b1[bass.ds(e, 1)].rearrange("o p j -> p (o j)")).then_inc(load_in[i], 16)
                    sp.dma_start(b2_sb[i][:], b2[bass.ds(e, 1)].rearrange("o d -> (o d)").partition_broadcast(P)).then_inc(load_in[i], 16)
                    sp.dma_start(w2_sb[i][:], w2[bass.ds(e, 1)].rearrange("o (j p) d -> p (o j) d", p=P)).then_inc(load_in[i], 16)

        @block.gpsimd
        def _(pool):
            make_identity(nc, pool, ident, ident_done)
            with pool.Fori(0, N_TILES // 2) as pair:
                for i in range(2):
                    pool.wait_ge(y_ready, pair * 2 + i + 3)
                    pool.sem_inc(relay, 1)
                    pool.dma_start(ys_dram[bass.ds((pair * 2 + i) * SLOT_TILE, SLOT_TILE), :].rearrange("(t p) d -> p t d", p=P),
                                   yt[i][:]).then_inc(stored[i], 16)
                    pool.wait_ge(stored[i], pair * 16 + 16)
                    pool.sem_inc(y_free, 1)

        @block.scalar
        def _(act):
            with act.Fori(0, N_TILES // 2) as pair:
                for i in range(2):
                    tile = pair * 2 + i
                    act.wait_ge(load_in[i], pair * 80 + 80)
                    for j in range(NH):
                        act.wait_ge(h_done, tile * NH + j + 1)
                        nc.scalar.activation(hid[i][:, j, :], ps_h[j % 4][:, 0:SLOT_TILE], ACT.Silu, bias=b1_sb[i][:, j:j + 1]
                                             ).then_inc(h_ready, 1)

        @block.vector
        def _(dve):
            with dve.Fori(0, N_TILES // 2) as pair:
                for i in range(2):
                    tile = pair * 2 + i
                    dve.wait_ge(turned, tile + 1)
                    nc.vector.tensor_copy(x_t[i][:], ps_t[:]).then_inc(x_ready, 1)
                    dve.wait_ge(y_done, tile + 3)
                    dve.wait_ge(y_free, tile + 1)
                    nc.vector.tensor_tensor(yt[i][:], ps_y[i][:], b2_sb[i][:].unsqueeze(1).to_broadcast([P, TB, D]), ALU.add
                                            ).then_inc(y_ready, 1)

        @block.tensor
        def _(pe):
            for free, count in ((y_done, 2), (x_ready, 1), (h_ready, 4), (y_ready, 2), (y_free, 2)):
                pe.sem_inc(free, count)
            pe.wait_ge(ident_done, 2)
            with pe.Fori(0, N_TILES // 2) as pair:
                for i in range(2):
                    tile = pair * 2 + i
                    pe.wait_ge(load_in[i], pair * 80 + 80)
                    pe.wait_ge(x_ready, tile + 1)
                    for t in range(TB):
                        for k in range(KD):
                            last = nc.tensor.transpose(ps_t[:, k, t * P:(t + 1) * P], xt[i][:, t, k * P:(k + 1) * P], ident[:])
                    last.then_inc(turned, 1)
                    pe.wait_ge(x_ready, tile + 2)
                    for j in range(NH):
                        pe.wait_ge(h_ready, tile * NH + j + 1)
                        for k in range(KD):
                            last = nc.tensor.matmul(ps_h[j % 4][:, 0:SLOT_TILE], w1_sb[i][:, k, j * P:(j + 1) * P], x_t[i][:, k, :],
                                                    start=k == 0, stop=k == KD - 1)
                        last.then_inc(h_done, 1)
                    pe.wait_ge(h_ready, tile * NH + NH + 4)
                    pe.wait_ge(y_ready, tile + 1)
                    for t in range(TB):
                        for j in range(NH):
                            last = nc.tensor.matmul(ps_y[i][:, t, :], hid[i][:, j, t * P:(t + 1) * P], w2_sb[i][:, j, :],
                                                    start=j == 0, stop=j == NH - 1)
                    last.then_inc(y_done, 1)


def combine(nc, x1_dram, ys_dram, slot, weight, out):
    with ExitStack() as ctx:
        m = Space(nc, ctx, "cb_")
        DEPTH = 4
        x1 = m.sb("x1", [P, NT, D])
        row = [[m.sb(f"row{c}_{i}", [P, D]) for i in range(DEPTH)] for c in range(2)]
        sem = m.sem
        x_in = sem("x_in")
        gathered = [sem(f"gathered{i}") for i in range(DEPTH)]
        added, ready, stored = sem("added"), sem("ready"), sem("stored")
        block = ctx.enter_context(nc.Block())

        @block.gpsimd
        def _(pool):
            for t in range(NT):
                if t >= DEPTH:
                    pool.wait_ge(ready, t - DEPTH + 1)
                for c in range(2):
                    nc.gpsimd.indirect_dma_start(row[c][t % DEPTH][:], None, ys_dram, bass.IndirectOffsetOnAxis(slot[:, c, t:t + 1], 0)
                                                 ).then_inc(gathered[t % DEPTH], 16)

        @block.vector
        def _(dve):
            dve.wait_ge(x_in, 16)
            for t in range(NT):
                dve.wait_ge(gathered[t % DEPTH], 32 * (t // DEPTH) + 32)
                nc.vector.scalar_tensor_tensor(out=x1[:, t, :], in0=row[0][t % DEPTH][:], scalar=weight[:, 0, t:t + 1],
                                               in1=x1[:, t, :], op0=ALU.mult, op1=ALU.add).then_inc(added, 1)
                dve.wait_ge(added, t + 1)
                nc.vector.scalar_tensor_tensor(out=x1[:, t, :], in0=row[1][t % DEPTH][:], scalar=weight[:, 1, t:t + 1],
                                               in1=x1[:, t, :], op0=ALU.mult, op1=ALU.add).then_inc(ready, 1)

        @block.sync
        def _(sp):
            view = out.rearrange("(t p) d -> p t d", p=P)
            sp.dma_start(x1[:], x1_dram.rearrange("(t p) d -> p t d", p=P)).then_inc(x_in, 16)
            for t in range(0, NT, 4):
                sp.wait_ge(ready, t + 4)
                sp.dma_start(view[:, t:t + 4, :], x1[:, t:t + 4, :]).then_inc(stored, 16)
            sp.wait_ge(stored, 16 * NT // 4)


def program(nc, x, ctx_t, boxes, g_xattn, g_ffn, wq, bq, wk, bk, wv, bv, wo, bo, wg_rows, wg_feat, bg,
            rw1, rb1, rw2, rb2, w1, b1, w2, b2, out):
    def scratch(name, shape):
        return nc.dram_tensor(name, shape, F32, kind="Internal").ap()

    q_dram, k_dram = scratch("q_rows", [B, P, PAIRS, S]), scratch("k_rows", [B, P, PAIRS, S])
    v_dram, negm_dram = scratch("v_rows", [B, P, NB, HD]), scratch("neg_max", [B, H, S])
    y_dram, z_dram = scratch("y_geometry", [NT, SEP, YCOLS]), scratch("z_geometry", [ZROWS, B, S])
    x1_dram = scratch("x1_rows", [TOK, D])
    xs_dram, ys_dram = scratch("expert_in", [SLOTS, D]), scratch("expert_out", [SLOTS, D])
    with ExitStack() as ctx:
        m = Space(nc, ctx, "")
        with ExitStack() as boxes_ctx:
            k = Space(nc, boxes_ctx, "")
            centre, inv_size = k.sb("centre", [P, NT, 2]), k.sb("inv_size", [P, NT, 2])
            box_terms(nc, boxes, wg_rows, bg, y_dram, z_dram, centre, inv_size)
            project(nc, x, ctx_t, wq, wk, wv, bq, bk, q_dram, k_dram, v_dram, negm_dram)
            attend(nc, x, q_dram, k_dram, v_dram, negm_dram, y_dram, z_dram, wg_feat, wo, bv, bo, g_xattn,
                   centre, inv_size, x1_dram)
        slot = m.sb("slot", [P, 2, NT], U32)
        weight = m.sb("weight", [P, 2, NT])
        tile_expert = m.sb("tile_expert", [1, N_TILES], I32)
        route(nc, x1_dram, rw1, rb1, rw2, rb2, g_ffn, xs_dram, slot, weight, tile_expert)
        experts(nc, xs_dram, ys_dram, w1, b1, w2, b2, tile_expert)
        combine(nc, x1_dram, ys_dram, slot, weight, out)


def kernel(**inputs):
    import numpy as np
    import concourse.bacc as bacc
    from concourse.bass_utils import run_bass_kernel_spmd

    a = {n.replace("L0_xattn_", "").replace("L0_ffn_", "ffn_"): np.asarray(v) for n, v in inputs.items()}
    per_row = lambda v: v.reshape(-1, P).T
    laid = {
        "x": a["x"].reshape(TOK, D), "ctx_t": a["ctx_1024"].reshape(TOK, D).T, "boxes": a["fside_BxSx4_0"].reshape(TOK, 4),
        "g_xattn": a["g_xattn"], "g_ffn": a["g_ffn"],
        "wq": a["Wq"].T, "bq": per_row(a["bq"]), "wk": a["Wk"].T, "bk": per_row(a["bk"]),
        "wv": a["Wv"].T, "bv": per_row(a["bv"]), "wo": a["Wo"].T, "bo": a["bo"],
        "wg_rows": a["Wg"].T, "wg_feat": a["Wg"].T[[0, 2, 1, 3, 8, 10, 9, 11]], "bg": a["bg"],
        "rw1": a["ffn_rw1"], "rb1": per_row(a["ffn_rb1"]), "rw2": a["ffn_rw2"], "rb2": a["ffn_rb2"],
        "w1": a["ffn_w1"], "b1": a["ffn_b1"].reshape(E, -1, P).transpose(0, 2, 1), "w2": a["ffn_w2"], "b2": a["ffn_b2"],
    }
    laid = {n: np.ascontiguousarray(v) for n, v in laid.items()}
    nc = bacc.Bacc("TRN2", target_bir_lowering=False, num_devices=1)
    handles = {n: nc.dram_tensor("in_" + n, v.shape, mybir.dt.from_np(v.dtype), kind="ExternalInput").ap() for n, v in laid.items()}
    out = nc.dram_tensor("out", [TOK, D], F32, kind="ExternalOutput").ap()
    program(nc, out=out, **handles)
    got = run_bass_kernel_spmd(nc, [{"in_" + n: v for n, v in laid.items()}], core_ids=[0]).results[0]["out"]
    return got.reshape(B, S, D)
```

```python
from contextlib import ExitStack

import concourse.bass as bass
from concourse import mybir

P = 128
B, S, D = 8, 512, 256
H, DK = 16, 64
HD = H * DK
E, HID = 8, 1024
TOK = B * S
NT = TOK // P
KD = D // P
NB = S // P
PAIRS = H // 2
EPS = 1e-5
FREQ = (1.0, 1000.0 ** -0.5)
TWO_PI = 6.283185307179586
HALF_PI = TWO_PI / 4
ROUND = 12582912.0
GEO_MIN = 1e-6
SLOT_TILE = 256
N_TILES = 2 * TOK // SLOT_TILE + E
SLOTS = N_TILES * SLOT_TILE
SEP = 9
YCOLS = H * P

ALU = mybir.AluOpType
ACT = mybir.ActivationFunctionType
F32 = mybir.dt.float32
F32R = mybir.dt.float32r
I32 = mybir.dt.int32
U32 = mybir.dt.uint32
AX = mybir.AxisListType.X




def wait(eng, sem, value):
    if not isinstance(value, int) or value > 0:
        eng.wait_ge(sem, value)


class Space:

    def __init__(self, nc, ctx, tag):
        self.nc, self.ctx, self.tag = nc, ctx, tag

    def sb(self, name, shape, dtype=F32):
        return self.ctx.enter_context(self.nc.sbuf_tensor(self.tag + name, shape, dtype))

    def ps(self, name, shape, dtype=F32):
        return self.ctx.enter_context(self.nc.psum_tensor(self.tag + name, shape, dtype))

    def sem(self, name):
        return self.ctx.enter_context(self.nc.semaphore(self.tag + name))


def make_identity(nc, pool, ident, done):
    nc.gpsimd.memset(ident[:], 0.0).then_inc(done, 1)
    pool.wait_ge(done, 1)
    nc.gpsimd.affine_select(out=ident[:], in_=ident[:], compare_op=ALU.not_equal, fill=1.0, base=0,
                            pattern=[[-1, P]], channel_multiplier=1).then_inc(done, 1)


def box_terms(nc, boxes, wg_rows, bg_row, y_dram, z_dram, c_dram, centre, inv_size):
    with ExitStack() as ctx:
        m = Space(nc, ctx, "box_")
        bx = m.sb("bx", [P, NT, 4])
        size = m.sb("size", [P, NT, 2])
        lg = m.sb("lg", [P, NT, 2])
        turn = m.sb("turn", [P, NT, 4])
        whole = m.sb("whole", [P, NT, 4])
        frac = m.sb("frac", [P, NT, 4])
        mag = m.sb("mag", [P, NT, 4])
        halfpi = m.sb("halfpi", [P, 1])
        sc = m.sb("sc", [P, NT, 2, 4])
        wgb = m.sb("wgb", [P, H, H])
        z = m.sb("z", [P, NT, SEP])
        y = m.sb("y", [P, NT, SEP, H])
        tmp = m.sb("tmp", [P, NT, 4, H])
        ident = m.sb("ident", [P, P])
        row = [[m.sb(f"row{part}{i}", [SEP, YCOLS], F32R) for i in range(2)] for part in ("hi", "lo")]
        zrow = [m.sb(f"zrow{part}", [SEP, NT * P], F32R) for part in ("hi", "lo")]
        crow = m.sb("crow", [2, NT * P])
        psy = [m.ps(f"psy{i}", [P, 512]) for i in range(4)]

        loaded, ident_done = m.sem("loaded"), m.sem("ident_done")
        step, logs, sines = m.sem("step"), m.sem("logs"), m.sem("sines")
        turned, moved, row_moved = m.sem("turned"), m.sem("moved"), m.sem("row_moved")
        row_stored = [m.sem(f"row_stored{i}") for i in range(2)]
        row_low, z_stored = m.sem("row_low"), m.sem("z_stored")
        NY, NZ = 4 * NT, NT * P // 512

        def place(part, i):
            if i < NY:
                return row[part][i // 4 % 2][:, (i % 4) * 512:(i % 4 + 1) * 512]
            return zrow[part][:, (i - NY) * 512:(i - NY + 1) * 512]

        block = ctx.enter_context(nc.Block())

        @block.sync
        def _(sp):
            sp.dma_start(bx[:], boxes.rearrange("(t p) c -> p t c", p=P)).then_inc(loaded, 16)
            sp.dma_start(wgb[:], wg_rows.partition_broadcast(P)).then_inc(loaded, 16)
            sp.dma_start(y[:, 0, SEP - 1, :], bg_row.partition_broadcast(P)).then_inc(loaded, 16)
            for t in range(NT):
                sp.wait_ge(row_moved, 4 * (t + 1))
                sp.wait_ge(row_low, 4 * (t + 1))
                for part, stack in ((0, 0), (0, 1), (1, 2)):
                    sp.dma_start(y_dram[t, stack], row[part][t % 2][:].bitcast(F32)).then_inc(row_stored[t % 2], 16)
            sp.wait_ge(row_moved, NY + 2 * NZ)
            sp.wait_ge(row_low, NY + NZ)
            for part, stack in ((0, 0), (1, 1), (0, 2)):
                sp.dma_start(z_dram[stack].rearrange("k b m -> k (b m)"), zrow[part][:].bitcast(F32)).then_inc(z_stored, 16)
            sp.dma_start(c_dram.rearrange("c b m -> c (b m)"), crow[:]).then_inc(z_stored, 16)
            for i in range(2):
                sp.wait_ge(row_stored[i], 48 * NT // 2)
            sp.wait_ge(z_stored, 64)

        @block.gpsimd
        def _(pool):
            make_identity(nc, pool, ident, ident_done)

        @block.vector
        def _(dve):
            count = [0]

            def link(ins):
                count[0] += 1
                ins.then_inc(step, 1)
                dve.wait_ge(step, count[0])

            nc.vector.memset(halfpi[:], HALF_PI)
            nc.vector.memset(z[:, :, SEP - 1:SEP], 1.0)
            dve.wait_ge(loaded, 48)
            link(nc.vector.tensor_tensor(size[:], bx[:, :, 2:4], bx[:, :, 0:2], ALU.subtract))
            link(nc.vector.tensor_scalar(size[:], size[:], 1.0, None, ALU.add))
            nc.vector.reciprocal(inv_size[:], size[:])
            link(nc.vector.tensor_tensor(centre[:], bx[:, :, 0:2], bx[:, :, 2:4], ALU.add))
            link(nc.vector.tensor_scalar(centre[:], centre[:], 0.5, None, ALU.mult))
            nc.vector.tensor_copy(y[:, 1:NT, SEP - 1, :],
                                  y[:, 0, SEP - 1, :].unsqueeze(1).to_broadcast([P, NT - 1, H]))
            dve.wait_ge(logs, 1)
            for f in range(2):
                link(nc.vector.tensor_scalar(turn[:, :, f:4:2], lg[:], 100.0 * FREQ[f] / TWO_PI, None, ALU.mult))
            link(nc.vector.tensor_scalar(whole[:], turn[:], ROUND, None, ALU.add))
            link(nc.vector.tensor_scalar(whole[:], whole[:], ROUND, None, ALU.subtract))
            link(nc.vector.tensor_tensor(frac[:], turn[:], whole[:], ALU.subtract))
            link(nc.vector.tensor_single_scalar(mag[:].bitcast(I32), frac[:].bitcast(I32), 0x7FFFFFFF, op=ALU.bitwise_and))
            dve.wait_ge(sines, 2)
            nc.vector.tensor_copy(z[:, :, 0:8], sc[:].rearrange("p t s k -> p t (s k)"))

            def times(out, s, w):
                a = sc[:, :, s, :].unsqueeze(3).to_broadcast([P, NT, 4, H])
                c = wgb[:, w:w + 4, :].unsqueeze(1).to_broadcast([P, NT, 4, H])
                link(nc.vector.tensor_tensor(out, a, c, ALU.mult))

            times(y[:, :, 0:4, :], 1, 4)
            times(tmp[:], 0, 12)
            link(nc.vector.tensor_tensor(y[:, :, 0:4, :], y[:, :, 0:4, :], tmp[:], ALU.add))
            times(y[:, :, 4:8, :], 1, 12)
            times(tmp[:], 0, 4)
            link(nc.vector.tensor_tensor(y[:, :, 4:8, :], y[:, :, 4:8, :], tmp[:], ALU.subtract))
            dve.sem_inc(moved, 1)
            for i in range(NY + NZ):
                dve.wait_ge(row_moved, i + 1)
                nc.vector.tensor_tensor(place(1, i), psy[i % 4][0:SEP, :], place(0, i).bitcast(F32), ALU.subtract).then_inc(row_low, 1)

        @block.scalar
        def _(act):
            act.wait_ge(step, 2)
            nc.scalar.activation(lg[:], size[:], ACT.Ln).then_inc(logs, 1)
            act.wait_ge(step, 10)
            nc.scalar.activation(sc[:, :, 1, :], frac[:], ACT.Sin, scale=TWO_PI).then_inc(sines, 1)
            nc.scalar.activation(sc[:, :, 0, :], mag[:], ACT.Sin, scale=-TWO_PI, bias=halfpi[:]).then_inc(sines, 1)
            for i in range(NY + 2 * NZ):
                act.wait_ge(turned, i + 1)
                t = i // 4
                if i < NY and t >= 2 and i % 4 == 0:
                    act.wait_ge(row_stored[t % 2], 48 * (t // 2))
                if i < NY + NZ:
                    nc.scalar.copy(place(0, i), psy[i % 4][0:SEP, :]).then_inc(row_moved, 1)
                else:
                    j = i - NY - NZ
                    nc.scalar.copy(crow[:, j * 512:(j + 1) * 512], psy[i % 4][0:2, :]).then_inc(row_moved, 1)

        @block.tensor
        def _(pe):
            pe.wait_ge(ident_done, 2)
            pe.wait_ge(moved, 1)
            for i in range(NY + 2 * NZ):
                if i >= 4:
                    pe.wait_ge(row_moved, i - 3)
                    pe.wait_ge(row_low, min(i - 3, NY + NZ))
                for q in range(4):
                    if i < NY:
                        src, rows = y[:, i // 4, :, (i % 4) * 4 + q], SEP
                    elif i < NY + NZ:
                        src, rows = z[:, (i - NY) * 4 + q, :], SEP
                    else:
                        src, rows = centre[:, (i - NY - NZ) * 4 + q, :], 2
                    last = nc.tensor.transpose(psy[i % 4][0:rows, q * P:(q + 1) * P], src, ident[:])
                last.then_inc(turned, 1)


def project(nc, x, ctx_t, wq, wk, wv, bq, bk, q_dram, k_dram, v_dram, negm_dram):
    with ExitStack() as ctx:
        m = Space(nc, ctx, "prj_")
        stage = m.sb("stage", [P, KD, HD])
        w_sb = [[m.sb(f"w{n}_{part}", [P, KD, HD], F32R) for part in ("hi", "lo")] for n in "qkv"]
        bq_sb, bk_sb = m.sb("bq", [P, PAIRS]), m.sb("bk", [P, PAIRS])
        ident = m.sb("ident", [P, P])
        eps = m.sb("eps", [P, 1])
        xt = m.sb("xt", [P, NB, D])
        ct = m.sb("ct", [P, KD, S])
        ct_p = [m.sb(f"ct_{part}", [P, KD, S], F32R) for part in ("hi", "lo")]
        xn_p = [m.sb(f"xn_{part}", [P, KD, S], F32R) for part in ("hi", "lo")]
        stats, mv = m.sb("stats", [P, NB, 6]), m.sb("mv", [P, NB, 2])
        sd, rstd = m.sb("sd", [P, NB]), m.sb("rstd", [P, NB])
        q_p, k_p = ([m.sb(f"{n}_{part}", [P, PAIRS, S], F32R) for part in ("hi", "lo")] for n in "qk")
        v_p = [m.sb(f"v_{part}", [P, NB, HD], F32R) for part in ("hi", "lo")]
        top = m.sb("top", [P, NB, H])
        negm = m.sb("negm", [H, S], F32R)
        ps_t = m.ps("ps_t", [P, 2, 512])
        ps_p = [m.ps(f"ps_p{i}", [P, 512]) for i in range(2)]
        ps_s = [m.ps(f"ps_s{i}", [P, 2, 512]) for i in range(2)]

        w_in, w_high, w_ready, b_in, x_in, c_in, ident_done, relay = (
            m.sem(n) for n in ("w_in", "w_high", "w_ready", "b_in", "x_in", "c_in", "ident_done", "relay"))
        stat, scaled, normed, turned, xn_high, xn_ready, ct_high, ct_ready = (
            m.sem(n) for n in ("stat", "scaled", "normed", "turned", "xn_high", "xn_ready", "ct_high", "ct_ready"))
        proj_done, high, low, score_done, max_done = (m.sem(n) for n in ("proj_done", "high", "low", "score_done", "max_done"))
        max_turned, negm_ready, stored = m.sem("max_turned"), m.sem("negm_ready"), m.sem("stored")
        NPROJ = 2 * PAIRS + 2 * NB
        NSC = PAIRS * NB
        STORED = 11 * 16
        block = ctx.enter_context(nc.Block())

        def score_turns(i):
            if i < 2 * PAIRS:
                n = 2 * (i - 2)
                return range(n, n + 2)
            n = 2 * (2 * PAIRS - 2) + (i - 2 * PAIRS)
            return range(n, n + 1) if n < NSC else range(0)

        @block.sync
        def _(sp):
            sp.dma_start(bq_sb[:], bq).then_inc(b_in, 16)
            sp.dma_start(bk_sb[:], bk).then_inc(b_in, 16)
            for i, w in enumerate((wq, wk, wv)):
                if i:
                    sp.wait_ge(w_ready, i)
                sp.dma_start(stage[:], w.rearrange("(k p) n -> p k n", p=P)).then_inc(w_in, 16)

            def load(b):
                wait(sp, turned, b)
                if not isinstance(b, int):
                    sp.sem_inc(relay, 1)
                sp.dma_start(xt[:], x[bass.ds(b * S, S), :].rearrange("(t p) d -> p t d", p=P)).then_inc(x_in, 16)
                wait(sp, ct_ready, b)
                if not isinstance(b, int):
                    sp.sem_inc(relay, 1)
                sp.dma_start(ct[:], ctx_t[:, bass.ds(b * S, S)].rearrange("(k p) s -> p k s", p=P)).then_inc(c_in, 16)

            load(0)
            with sp.Fori(1, B) as b:
                load(b)

        @block.gpsimd
        def _(pool):
            make_identity(nc, pool, ident, ident_done)

            def split_context(b):
                pool.wait_ge(ct_high, b + 1)
                nc.gpsimd.tensor_tensor(ct_p[1][:], ct[:], ct_p[0][:].bitcast(F32), ALU.subtract).then_inc(ct_ready, 1)

            split_context(0)
            with pool.Fori(1, B) as b:
                split_context(b)

        @block.vector
        def _(dve):
            nc.vector.memset(eps[:], EPS)
            for i in range(3):
                dve.wait_ge(w_high, i + 1)
                if i == 0:
                    nc.vector.scalar_tensor_tensor(out=w_sb[0][1][:].rearrange("p k n -> p (k n)"), in0=stage[:].rearrange("p k n -> p (k n)"),
                                                   scalar=DK ** -0.5, in1=w_sb[0][0][:].rearrange("p k n -> p (k n)").bitcast(F32),
                                                   op0=ALU.mult, op1=ALU.subtract).then_inc(w_ready, 1)
                else:
                    nc.vector.tensor_tensor(w_sb[i][1][:], stage[:], w_sb[i][0][:].bitcast(F32), ALU.subtract).then_inc(w_ready, 1)
            dve.wait_ge(b_in, 32)
            nc.vector.tensor_scalar(bq_sb[:], bq_sb[:], DK ** -0.5, None, ALU.mult).then_inc(w_ready, 1)
            dve.wait_ge(w_ready, 4)

            def sequence(b):
                dve.wait_ge(x_in, b * 16 + 16)
                for t in range(NB):
                    nc.vector.bn_stats(stats[:, t, :], xt[:, t, :]).then_inc(stat, 1)
                dve.wait_ge(stat, b * (2 * NB + 1) + NB)
                dve.sem_inc(relay, 1)
                for t in range(NB):
                    nc.vector.bn_aggr(mv[:, t, :], stats[:, t, :]).then_inc(stat, 1)
                dve.wait_ge(scaled, b + 1)
                nc.vector.reciprocal(rstd[:], sd[:]).then_inc(stat, 1)
                dve.wait_ge(stat, b * (2 * NB + 1) + 2 * NB + 1)
                for t in range(NB):
                    nc.vector.tensor_scalar(xt[:, t, :], xt[:, t, :], mv[:, t, 0:1], rstd[:, t:t + 1],
                                            ALU.subtract, ALU.mult).then_inc(normed, 1)
                dve.wait_ge(xn_high, b + 1)
                nc.vector.tensor_tensor(xn_p[1][:], ps_t[:], xn_p[0][:].bitcast(F32), ALU.subtract).then_inc(xn_ready, 1)

                def low_part(i):
                    dve.wait_ge(high, b * NPROJ + i + 1)
                    src = ps_p[i % 2][:]
                    if i < 2 * PAIRS:
                        (hi, lo), bias, j = (q_p, bq_sb, i // 2) if i % 2 == 0 else (k_p, bk_sb, i // 2)
                        nc.vector.scalar_tensor_tensor(out=lo[:, j, :], in0=src, scalar=bias[:, j:j + 1], in1=hi[:, j, :].bitcast(F32),
                                                       op0=ALU.add, op1=ALU.subtract).then_inc(low, 1)
                    else:
                        t, half = divmod(i - 2 * PAIRS, 2)
                        at = slice(half * 512, (half + 1) * 512)
                        nc.vector.tensor_tensor(v_p[1][:, t, at], src, v_p[0][:, t, at].bitcast(F32), ALU.subtract).then_inc(low, 1)

                def maximum(i):
                    j, t = divmod(i, NB)
                    dve.wait_ge(score_done, b * NSC + i + 1)
                    nc.vector.tensor_reduce(top[:, t, 2 * j:2 * j + 2], ps_s[i % 2][:], op=ALU.max, axis=AX).then_inc(max_done, 1)

                for i in range(NPROJ):
                    low_part(i)
                    if i >= 2:
                        for n in score_turns(i):
                            maximum(n)

            sequence(0)
            with dve.Fori(1, B) as b:
                sequence(b)

        @block.scalar
        def _(act):
            for i in range(3):
                act.wait_ge(w_in, 16 * i + 16)
                if i == 0:
                    nc.scalar.activation(w_sb[0][0][:], stage[:], ACT.Copy, scale=DK ** -0.5).then_inc(w_high, 1)
                else:
                    nc.scalar.copy(w_sb[i][0][:], stage[:]).then_inc(w_high, 1)
            act.wait_ge(w_ready, 4)

            def sequence(b):
                act.wait_ge(stat, b * (2 * NB + 1) + 2 * NB)
                nc.scalar.activation(sd[:], mv[:, :, 1], ACT.Sqrt, bias=eps[:]).then_inc(scaled, 1)
                act.wait_ge(c_in, b * 16 + 16)
                wait(act, proj_done, b * NPROJ)
                nc.scalar.copy(ct_p[0][:], ct[:]).then_inc(ct_high, 1)
                act.wait_ge(turned, b + 1)
                nc.scalar.copy(xn_p[0][:], ps_t[:]).then_inc(xn_high, 1)
                for i in range(NPROJ):
                    act.wait_ge(proj_done, b * NPROJ + i + 1)
                    if i == 0:
                        wait(act, stored, b * STORED)
                    src = ps_p[i % 2][:]
                    if i < 2 * PAIRS:
                        hi, bias, j = (q_p[0], bq_sb, i // 2) if i % 2 == 0 else (k_p[0], bk_sb, i // 2)
                        ins = nc.scalar.activation(hi[:, j, :], src, ACT.Identity, bias=bias[:, j:j + 1])
                    else:
                        t, half = divmod(i - 2 * PAIRS, 2)
                        ins = nc.scalar.copy(v_p[0][:, t, half * 512:(half + 1) * 512], src)
                    ins.then_inc(high, 1)
                act.wait_ge(high, b * NPROJ + NPROJ)
                act.sem_inc(relay, 1)
                act.wait_ge(low, b * NPROJ + NPROJ)
                act.sem_inc(relay, 1)
                for dram, parts in ((q_dram, q_p), (k_dram, k_p)):
                    for part in range(2):
                        for e in range(2):
                            act.dma_start(dram[part][bass.ds(b, 1)].rearrange("o d (j e) s -> d (o j) e s", e=2)[:, :, e, :],
                                          parts[part][64 * e:64 * e + 64].bitcast(F32)).then_inc(stored, 16)
                for part in range(2):
                    act.dma_start(v_dram[part][bass.ds(b, 1)].rearrange("o p t n -> p (o t) n"), v_p[part][:].bitcast(F32)).then_inc(stored, 16)
                act.wait_ge(max_turned, b + 1)
                nc.scalar.activation(negm[:], ps_t[0:H, 0, :], ACT.Copy, scale=-1.0).then_inc(negm_ready, 1)
                act.wait_ge(negm_ready, b + 1)
                act.sem_inc(relay, 1)
                act.dma_start(negm_dram[bass.ds(b, 1)].rearrange("o h s -> h (o s)"), negm[:].bitcast(F32)).then_inc(stored, 16)

            sequence(0)
            with act.Fori(1, B) as b:
                sequence(b)
            act.wait_ge(stored, STORED * B)

        @block.tensor
        def _(pe):
            pe.wait_ge(ident_done, 2)
            pe.wait_ge(w_ready, 4)

            def sequence(b):
                pe.wait_ge(normed, b * NB + NB)
                wait(pe, negm_ready, b)
                for t in range(NB):
                    for k in range(KD):
                        last = nc.tensor.transpose(ps_t[:, k, t * P:(t + 1) * P], xt[:, t, k * P:(k + 1) * P], ident[:])
                last.then_inc(turned, 1)
                pe.wait_ge(xn_ready, b + 1)
                pe.wait_ge(ct_ready, b + 1)

                def product(i):
                    wait(pe, low, b * NPROJ + i - 1)
                    out = ps_p[i % 2][:]
                    n = 0
                    for k in range(KD):
                        for a, c in ((0, 0), (0, 1), (1, 0)):
                            if i < 2 * PAIRS:
                                w, src = (w_sb[0], xn_p) if i % 2 == 0 else (w_sb[1], ct_p)
                                j = i // 2
                                lhs, rhs = w[a][:, k, j * P:(j + 1) * P], src[c][:, k, :]
                            else:
                                t, half = divmod(i - 2 * PAIRS, 2)
                                lhs, rhs = ct_p[a][:, k, t * P:(t + 1) * P], w_sb[2][c][:, k, half * 512:(half + 1) * 512]
                            last = nc.tensor.matmul(out, lhs, rhs, start=n == 0, stop=n == 3 * KD - 1)
                            n += 1
                    last.then_inc(proj_done, 1)

                def score(i):
                    j, t = divmod(i, NB)
                    pe.wait_ge(high, b * NPROJ + 2 * j + 2)
                    wait(pe, max_done, b * NSC + i - 1)
                    for e in range(2):
                        r = slice(64 * e, 64 * e + 64)
                        last = nc.tensor.matmul(ps_s[i % 2][:, e, :], q_p[0][r, j, t * P:(t + 1) * P], k_p[0][r, j, :],
                                                start=True, stop=True)
                    last.then_inc(score_done, 1)

                for i in range(NPROJ):
                    product(i)
                    if i >= 2:
                        for n in score_turns(i):
                            score(n)
                pe.wait_ge(max_done, b * NSC + NSC)
                for t in range(NB):
                    last = nc.tensor.transpose(ps_t[0:H, 0, t * P:(t + 1) * P], top[:, t, :], ident[:])
                last.then_inc(max_turned, 1)

            sequence(0)
            with pe.Fori(1, B) as b:
                sequence(b)


def attend(nc, x, q_dram, k_dram, v_dram, negm_dram, y_dram, z_dram, c_dram, wg_feat, wo, bv, bo, gate,
           centre, inv_size, x1_dram):
    RQ = S // 2
    QB = RQ // P
    UNITS = B * 2 * NB
    CH = RQ // 32
    QUADS = H // 4
    with ExitStack() as ctx:
        m = Space(nc, ctx, "att_")
        prob = m.sb("prob", [P, H, RQ])
        p_hi, p_lo = m.sb("p_hi", [P, H, RQ], F32R), m.sb("p_lo", [P, H, RQ], F32R)
        q_hi, q_lo = m.sb("q_hi", [P, H, RQ], F32R), m.sb("q_lo", [P, H, RQ], F32R)
        k_sb = m.sb("k", [P, H, P], F32R)
        v_hi = m.sb("v_hi", [P, PAIRS, 192], F32R)
        v_lo = m.sb("v_lo", [P, PAIRS, 192], F32R)
        negm = m.sb("negm", [P, 2 * RQ], F32R)
        pick = m.sb("pick", [P, PAIRS], F32R)
        acc = m.sb("acc", [P, 2, PAIRS, RQ])
        raw = m.sb("raw", [P, 8, QB, P])
        f_hi = [m.sb(f"f_hi{i}", [P, 8, P], F32R) for i in range(QB)]
        f_lo = [m.sb(f"f_lo{i}", [P, 8, P], F32R) for i in range(QB)]
        wide = [m.sb(f"wide{i}", [P, H, 16], F32R) for i in range(2)]
        ys = m.sb("ys", [P, QB, H, P], F32R)
        zs = [m.sb(f"zs{i}", [P, P], F32R) for i in range(2)]
        feat = m.sb("feat", [P, 8, QB, P])
        cm = [m.sb(f"cm{i}", [P, 2, P]) for i in range(2)]
        dist = [m.sb(f"dist{i}", [P, 2, QB, P]) for i in range(2)]
        turn = m.sb("turn", [P, 2, 2, 2, QB, P])
        frac, mag = turn[:, 0], turn[:, 1]
        wo_hi, wo_lo = m.sb("wo_hi", [P, PAIRS, D], F32R), m.sb("wo_lo", [P, PAIRS, D], F32R)
        x_sb = m.sb("x", [P, QB, D])
        bias_row = m.sb("bias_row", [P, D])
        tg, halfpi = m.sb("tg", [P, 1]), m.sb("halfpi", [P, 1])
        bv_sb = m.sb("bv", [P, PAIRS])
        sums, rec = m.sb("sums", [P, 32]), m.sb("rec", [P, 32])
        rec_hi, rec_lo = m.sb("rec_hi", [P, 32], F32R), m.sb("rec_lo", [P, 32], F32R)
        spread = m.sb("spread", [4, P], F32R)
        recs = p_lo[0:4].rearrange("p h n -> p (h n)")[:, 0:PAIRS * RQ]
        flat = p_hi[:].rearrange("p h n -> p (h n)")
        o_hi = flat[:, 0:PAIRS * RQ].rearrange("p (j n) -> p j n", j=PAIRS)
        o_lo = flat[:, PAIRS * RQ:].rearrange("p (j n) -> p j n", j=PAIRS)
        wo_in = acc[:].rearrange("p e j n -> p (e j n)")[:, 0:PAIRS * D].rearrange("p (j d) -> p j d", j=PAIRS)
        bvw = feat[:].rearrange("p f n m -> p (f n m)")[:, 0:PAIRS * P].rearrange("p (j n) -> p j n", j=PAIRS)
        mask = raw[:, 0, 0, 0:16]
        ident = raw[:, 1, 0, 0:PAIRS]
        wcol = raw[:, 2, 0, 0:H]
        wide_f = raw[:, 4:8].rearrange("p g b m -> p (g b m)")[:, 0:H * 16].rearrange("p (h n) -> p h n", h=H)
        sprd = raw[0:4, 3, 0, :]
        ps_s = [m.ps(f"ps_s{i}", [P, 2, 512]) for i in range(2)]
        ps_g = [m.ps(f"ps_g{i}", [P, 512]) for i in range(2)]
        ps_o = [m.ps(f"ps_o{i}", [P, 512]) for i in range(2)]

        sem = m.sem
        pro_in, pro_pool, pro_dve, pro_act, pro_pe = (sem(n) for n in ("pro_in", "pro_pool", "pro_dve", "pro_act", "pro_pe"))
        q_in, k_in, v_in, y_in, x_in, raw_in, relay = (sem(n) for n in ("q_in", "k_in", "v_in", "y_in", "x_in", "raw_in", "relay"))
        z_in, c_in = ([sem(f"{n}{i}") for i in range(2)] for n in ("z_in", "c_in"))
        delta, clipped, logs, turned, fracs, mags, sines, f_high, f_low = (
            sem(n) for n in ("delta", "clipped", "logs", "turned", "fracs", "mags", "sines", "f_high", "f_low"))
        s_done, exp_done, g_done, mult_done, p_high, p_low, pv_done, acc_done = (
            sem(n) for n in ("s_done", "exp_done", "g_done", "mult_done", "p_high", "p_low", "pv_done", "acc_done"))
        sum_in, rec_done, rec_in, bc_done, normed, o_high, o_low, out_done, x1_part, x1_done, x1_stored = (
            sem(n) for n in ("sum_in", "rec_done", "rec_in", "bc_done", "normed", "o_high", "o_low", "out_done",
                             "x1_part", "x1_done", "x1_stored"))
        block = ctx.enter_context(nc.Block())

        class Unit:
            def __init__(self, b, half, w):
                self.b, self.half, self.w = b, half, w
                self.n, self.r = b * 8 + (4 * half + w), b * 2 + half

            def plus(self, k):
                at = 4 * self.half + self.w + k
                b, at = (self.b + 1, at - 8) if at >= 8 else (self.b, at)
                return Unit(b, at // 4, at % 4)

            def exists(self):
                return not isinstance(self.b, int) or self.b < B

        def every_unit(eng, step):
            for half in range(2):
                for w in range(NB):
                    step(Unit(0, half, w))
            with eng.Fori(1, B - 1) as b:
                for half in range(2):
                    for w in range(NB):
                        step(Unit(b, half, w))
            for half in range(2):
                for w in range(NB):
                    step(Unit(B - 1, half, w))

        first = Unit(0, 0, 0)
        POOL_CHUNKS = (0, 1, 2, 4, 5)

        @block.sync
        def _(sp):
            def after(s, value):
                wait(sp, s, value)
                if not isinstance(value, int):
                    sp.sem_inc(relay, 1)

            sp.dma_start(wo_in, wo.rearrange("(j p) d -> p j d", p=P)).then_inc(pro_in, 16)
            sp.dma_start(bias_row[:], bo.partition_broadcast(P)).then_inc(pro_in, 16)
            sp.dma_start(bv_sb[:], bv).then_inc(pro_in, 16)
            sp.dma_start(tg[:], gate.partition_broadcast(P)).then_inc(pro_in, 16)
            for n in range(16):
                sp.dma_start(wcol[8 * n:8 * n + 8, :], wg_feat).then_inc(pro_in, 16)

            def load_queries(u):
                after(s_done, u.n * QUADS)
                for dst, part in ((q_hi, 0), (q_lo, 1)):
                    for at in (0, 64):
                        sp.dma_start(dst[at:at + 64].bitcast(F32), q_dram[part][bass.ds(u.b, 1), :, :, u.half * RQ:(u.half + 1) * RQ]
                                     .rearrange("o d h s -> d (o h) s")).then_inc(q_in, 16)
                sp.dma_start(negm[0:PAIRS, :].bitcast(F32).rearrange("p (e s) -> p e s", e=2), negm_dram[bass.ds(u.b, 1), :, u.half * RQ:(u.half + 1) * RQ]
                             .rearrange("o (j e) s -> (o j) e s", e=2)).then_inc(q_in, 16)

            def load_keys(u):
                after(s_done, u.n * QUADS)
                for part in range(2):
                    sp.dma_start(k_sb[64 * part:64 * part + 64].bitcast(F32), k_dram[part][bass.ds(u.b, 1), :, :, u.w * P:(u.w + 1) * P]
                                 .rearrange("o d h s -> d (o h) s")).then_inc(k_in, 16)

            def load_values(u):
                after(pv_done, u.n * PAIRS)
                for dst, part in ((v_hi, 0), (v_lo, 1)):
                    src = v_dram[part][bass.ds(u.b, 1), :, u.w, :].rearrange("o p (j e d) -> p (o j) e d", e=2, d=DK)
                    for e in range(2):
                        sp.dma_start(dst[:, :, 128 * e:128 * e + DK].bitcast(F32), src[:, :, e, :]).then_inc(v_in, 16)

            def load_centres(u):
                i = u.w % 2
                if isinstance(u.n, int) and u.n < 2:
                    pass
                else:
                    after(delta, (u.n - 2) * 3 + 1)
                for c in range(2):
                    sp.dma_start(cm[i][:, c, :], c_dram[c, bass.ds(u.b, 1), u.w * P:(u.w + 1) * P].rearrange("o s -> (o s)")
                                 .partition_broadcast(P)).then_inc(c_in[i], 16)

            def load_z(u):
                if not (isinstance(u.n, int) and u.n < 2):
                    after(g_done, (u.n - 1) * CH)
                sp.dma_start(zs[u.w % 2][0:3 * SEP, :].bitcast(F32), z_dram[:, :, bass.ds(u.b, 1), u.w * P:(u.w + 1) * P]
                             .rearrange("t k b s -> (t k) (b s)")).then_inc(z_in[u.w % 2], 16)

            def load_y(u):
                after(g_done, u.n * CH)
                for blk in range(QB):
                    sp.dma_start(ys[0:3 * SEP, blk].bitcast(F32), y_dram[bass.ds(u.r * QB + blk, 1)].rearrange("o t k (h n) -> (o t k) h n", h=H)
                                 ).then_inc(y_in, 16)

            def relabel(u):
                after(sines, u.n * 2 + 2)
                after(f_high, u.n * QB)
                after(f_low, u.n * QB)
                for g in range(8):
                    sp.dma_start(raw[:, g], feat[16 * g:16 * g + 16]).then_inc(raw_in, 16)

            sp.wait_ge(pro_dve, 2)
            load_queries(first)
            load_keys(first)
            load_centres(first)
            load_centres(first.plus(1))
            load_centres(first.plus(2))
            load_values(first)
            sp.wait_ge(pro_dve, 9)
            load_z(first)
            load_y(first)
            relabel(first)
            load_keys(first.plus(1))

            def step(u):
                nxt, last = u.plus(1), u.w == NB - 1
                if u.w == 1:
                    after(x1_stored, u.r * 16)
                    sp.dma_start(x_sb[:], x[bass.ds(u.r * RQ, RQ), :].rearrange("(t p) d -> p t d", p=P)).then_inc(x_in, 16)
                if nxt.exists():
                    if u.plus(3).exists():
                        load_centres(u.plus(3))
                    load_z(nxt)
                    relabel(nxt)
                    if not last:
                        if u.plus(2).exists():
                            load_keys(u.plus(2))
                        load_values(nxt)
                    if u.w == NB - 2 and u.plus(2).exists():
                        load_queries(u.plus(2))
                if last:
                    after(acc_done, (u.n + 1) * PAIRS + 2)
                    for e, at in ((0, 64), (1, 0)):
                        sp.dma_start(sums[64 * e:64 * e + 64, :], acc[at:at + 1, e]).then_inc(sum_in, 16)
                    after(rec_done, (u.r + 1) * 3)
                    for row, (src, at) in enumerate(((rec_hi, 0), (rec_lo, 0), (rec_hi, 64), (rec_lo, 64))):
                        sp.dma_start(recs[row:row + 1, :].bitcast(F32), src[at:at + 64, :].bitcast(F32)).then_inc(rec_in, 16)
                    if nxt.exists():
                        load_y(nxt)
                        load_values(nxt)
                        load_keys(u.plus(2))
                    after(x1_done, u.r + 1)
                    sp.dma_start(x1_dram[bass.ds(u.r * RQ, RQ), :].rearrange("(t p) d -> p t d", p=P), x_sb[:]).then_inc(x1_stored, 16)

            every_unit(sp, step)
            sp.wait_ge(x1_stored, 16 * 2 * B)

        @block.gpsimd
        def _(pool):
            nc.gpsimd.memset(mask, 1.0).then_inc(pro_pool, 1)
            nc.gpsimd.memset(ident, 0.0).then_inc(pro_pool, 1)
            nc.gpsimd.memset(sprd, 1.0).then_inc(pro_pool, 1)
            pool.wait_ge(pro_pool, 3)
            nc.gpsimd.affine_select(out=mask, in_=mask, compare_op=ALU.is_ge, fill=0.0, base=0,
                                    pattern=[[-8, 16]], channel_multiplier=1).then_inc(pro_pool, 1)
            nc.gpsimd.affine_select(out=ident, in_=ident, compare_op=ALU.not_equal, fill=1.0, base=0,
                                    pattern=[[-1, PAIRS]], channel_multiplier=1).then_inc(pro_pool, 1)
            nc.gpsimd.affine_select(out=sprd, in_=sprd, compare_op=ALU.is_ge, fill=0.0, base=0,
                                    pattern=[[-2, 2], [0, 64]], channel_multiplier=1).then_inc(pro_pool, 1)
            pool.wait_ge(pro_pool, 6)
            nc.gpsimd.affine_select(out=mask, in_=mask, compare_op=ALU.is_ge, fill=0.0, base=7,
                                    pattern=[[8, 16]], channel_multiplier=-1).then_inc(pro_pool, 1)
            nc.gpsimd.affine_select(out=sprd, in_=sprd, compare_op=ALU.is_ge, fill=0.0, base=1,
                                    pattern=[[2, 2], [0, 64]], channel_multiplier=-1).then_inc(pro_pool, 1)
            pool.wait_ge(pro_dve, 9)

            def distances(u):
                pool.wait_ge(c_in[u.w % 2], u.b * (4 * 32) + (4 * u.half + u.w) // 2 * 32 + 32)
                pool.sem_inc(relay, 1)
                wait(pool, fracs, u.n - 1)
                pool.sem_inc(relay, 1)
                d = dist[u.w % 2]
                for c in range(2):
                    cols = centre[:, bass.ds(u.r * QB, QB), c].unsqueeze(2).to_broadcast([P, QB, P])
                    last = nc.gpsimd.tensor_tensor(d[:, c], cm[u.w % 2][:, c, :].unsqueeze(1).to_broadcast([P, QB, P]), cols, ALU.subtract)
                last.then_inc(delta, 1)
                pool.wait_ge(delta, u.n * 3 + 1)
                pool.sem_inc(relay, 1)
                for c in range(2):
                    cols = inv_size[:, bass.ds(u.r * QB, QB), c].unsqueeze(2).to_broadcast([P, QB, P])
                    last = nc.gpsimd.tensor_tensor(d[:, c], d[:, c], cols, ALU.mult)
                last.then_inc(delta, 1)
                pool.wait_ge(delta, u.n * 3 + 2)
                nc.gpsimd.tensor_tensor(d[:], d[:], d[:], ALU.mult).then_inc(delta, 1)

            for k in range(3):
                distances(first.plus(k))

            def step(u):
                for c in POOL_CHUNKS:
                    pool.wait_ge(p_high, u.n * CH + (c + 1))
                    at = (slice(None), slice(None), slice(32 * c, 32 * c + 32))
                    nc.gpsimd.tensor_tensor(p_lo[at], prob[at], p_hi[at].bitcast(F32), ALU.subtract).then_inc(p_low, 1)
                if u.plus(3).exists():
                    distances(u.plus(3))
                if u.w == NB - 1:
                    for i in range(4):
                        pool.wait_ge(o_high, u.r * 4 + (i + 1))
                        nc.gpsimd.tensor_tensor(o_lo[:, 2 * i:2 * i + 2], acc[:, 0, 2 * i:2 * i + 2, :],
                                                o_hi[:, 2 * i:2 * i + 2].bitcast(F32), ALU.subtract).then_inc(o_low, 1)

            every_unit(pool, step)

        @block.scalar
        def _(act):
            act.wait_ge(pro_in, 320)
            nc.scalar.activation(tg[:], tg[:], ACT.Tanh).then_inc(pro_act, 1)
            nc.scalar.copy(wo_hi[:], wo_in).then_inc(pro_act, 1)
            act.wait_ge(pro_dve, 9)

            def log(u):
                act.wait_ge(clipped, u.n + 1)
                nc.scalar.activation(dist[u.w % 2][:], dist[u.w % 2][:], ACT.Ln).then_inc(logs, 1)

            def exponential(u, q):
                act.wait_ge(s_done, u.n * QUADS + (q + 1))
                if q == 0:
                    wait(act, p_low, u.n * CH)
                nc.scalar.activation(prob[:, 4 * q:4 * q + 4, :], ps_s[q % 2][:].rearrange("p a (e s) -> p (a e) s", e=2),
                                     ACT.Exp).then_inc(exp_done, 1)

            def waves(u):
                act.wait_ge(fracs, u.n + 1)
                wait(act, raw_in, u.n * 128)
                nc.scalar.activation(feat[:, 0:4], frac.rearrange("p a b n m -> p (a b) n m"), ACT.Sin,
                                     scale=TWO_PI).then_inc(sines, 1)
                act.wait_ge(mags, u.n + 1)
                nc.scalar.activation(feat[:, 4:8], mag.rearrange("p a b n m -> p (a b) n m"), ACT.Sin,
                                     scale=-TWO_PI, bias=halfpi[:]).then_inc(sines, 1)

            def high_features(u, blk):
                act.wait_ge(raw_in, u.n * 128 + 128)
                wait(act, g_done, (u.n - 1) * CH + 4 * (blk + 1))
                nc.scalar.copy(f_hi[blk][:], raw[:, :, blk]).then_inc(f_high, 1)

            log(first)
            waves(first)
            log(first.plus(1))
            for q in range(QUADS):
                exponential(first, q)
            for blk in range(QB):
                high_features(first, blk)

            def step(u):
                nxt = u.plus(1)
                for c in range(CH):
                    act.wait_ge(mult_done, u.n * CH + (c + 1) + 2)
                    if c == 0:
                        wait(act, pv_done, u.n * PAIRS)
                        if u.w == 0:
                            wait(act, out_done, u.r)
                    nc.scalar.copy(p_hi[:, :, 32 * c:32 * c + 32], prob[:, :, 32 * c:32 * c + 32]).then_inc(p_high, 1)
                    if c == 1 and nxt.exists():
                        waves(nxt)
                if u.plus(2).exists():
                    log(u.plus(2))
                if nxt.exists():
                    if u.w < NB - 1:
                        order = (0, 1, "f0", 2, "f1", 3)
                    else:
                        order = ("f0", "f1", 0, 1, 2, 3)
                    for what in order:
                        if what in ("f0", "f1"):
                            high_features(nxt, int(what[1]))
                        else:
                            exponential(nxt, what)
                if u.w == NB - 1:
                    for i in range(4):
                        act.wait_ge(normed, u.r * 8 + (2 * i + 2))
                        nc.scalar.copy(o_hi[:, 2 * i:2 * i + 2], acc[:, 0, 2 * i:2 * i + 2, :]).then_inc(o_high, 1)

            every_unit(act, step)

        @block.vector
        def _(dve):
            nc.vector.memset(halfpi[:], HALF_PI)
            nc.vector.memset(v_hi[:, :, DK:128].bitcast(F32), 1.0)
            nc.vector.memset(v_lo[:, :, DK:128].bitcast(F32), 0.0)
            nc.vector.memset(negm[:].bitcast(F32), 0.0).then_inc(pro_dve, 1)
            nc.vector.memset(ys[:].bitcast(F32), 0.0)
            for i in range(2):
                last = nc.vector.memset(zs[i][:].bitcast(F32), 0.0)
            last.then_inc(pro_dve, 1)
            dve.wait_ge(pro_in, 320)
            dve.wait_ge(pro_pool, 8)
            nc.vector.tensor_tensor(wide_f, mask.unsqueeze(1).to_broadcast([P, H, 16]), wcol.unsqueeze(2).to_broadcast([P, H, 16]),
                                    ALU.mult).then_inc(pro_dve, 1)
            nc.vector.tensor_copy(bvw, bv_sb[:].unsqueeze(2).to_broadcast([P, PAIRS, P])).then_inc(pro_dve, 1)
            nc.vector.tensor_copy(pick[:], ident)
            nc.vector.tensor_copy(spread[:], sprd)
            dve.wait_ge(pro_dve, 4)
            nc.vector.tensor_copy(wide[0][:], wide_f).then_inc(pro_dve, 1)
            dve.wait_ge(pro_dve, 5)
            nc.vector.tensor_tensor(wide[1][:], wide_f, wide[0][:].bitcast(F32), ALU.subtract).then_inc(pro_dve, 1)
            dve.wait_ge(pro_act, 2)
            nc.vector.tensor_tensor(wo_lo[:], wo_in, wo_hi[:].bitcast(F32), ALU.subtract).then_inc(pro_dve, 1)
            dve.wait_ge(pro_pe, 1)
            nc.vector.tensor_tensor(bias_row[:], ps_g[0][:, 0:D], bias_row[:], ALU.add).then_inc(pro_dve, 1)
            dve.wait_ge(pro_dve, 8)
            nc.vector.tensor_scalar(bias_row[:], bias_row[:], tg[:], None, ALU.mult).then_inc(pro_dve, 1)

            def clip(u):
                dve.wait_ge(delta, u.n * 3 + 3)
                nc.vector.tensor_scalar(dist[u.w % 2][:], dist[u.w % 2][:], 1e-6, None, ALU.max).then_inc(clipped, 1)

            def fractions(u, part):
                if part == 0:
                    dve.wait_ge(logs, u.n + 1)
                    wait(dve, sines, u.n * 2)
                    for f in range(2):
                        last = nc.vector.tensor_scalar(frac[:, f], dist[u.w % 2][:], 50.0 * FREQ[f] / TWO_PI, ROUND, ALU.mult, ALU.add)
                    last.then_inc(turned, 1)
                elif part == 1:
                    dve.wait_ge(turned, u.n * 2 + 1)
                    nc.vector.tensor_scalar(frac, frac, ROUND, None, ALU.subtract).then_inc(turned, 1)
                elif part == 2:
                    dve.wait_ge(turned, u.n * 2 + 2)
                    for f in range(2):
                        last = nc.vector.scalar_tensor_tensor(
                            out=frac[:, f].rearrange("p b n m -> p (b n m)"), in0=dist[u.w % 2][:].rearrange("p b n m -> p (b n m)"),
                            scalar=50.0 * FREQ[f] / TWO_PI, in1=frac[:, f].rearrange("p b n m -> p (b n m)"),
                            op0=ALU.mult, op1=ALU.subtract)
                    last.then_inc(fracs, 1)
                else:
                    dve.wait_ge(fracs, u.n + 1)
                    nc.vector.tensor_single_scalar(mag.bitcast(I32), frac.bitcast(I32), 0x7FFFFFFF, op=ALU.bitwise_and).then_inc(mags, 1)

            def low_features(u, blk):
                dve.wait_ge(f_high, u.n * QB + (blk + 1))
                nc.vector.tensor_tensor(f_lo[blk][:], raw[:, :, blk], f_hi[blk][:].bitcast(F32), ALU.subtract).then_inc(f_low, 1)

            def low_part(u, c):
                dve.wait_ge(p_high, u.n * CH + (c + 1))
                at = (slice(None), slice(None), slice(32 * c, 32 * c + 32))
                nc.vector.tensor_tensor(p_lo[at], prob[at], p_hi[at].bitcast(F32), ALU.subtract).then_inc(p_low, 1)

            clip(first)
            for part in range(4):
                fractions(first, part)
            clip(first.plus(1))
            for part in range(2):
                fractions(first.plus(1), part)
            for blk in range(QB):
                low_features(first, blk)

            def step(u):
                nxt, second = u.plus(1), u.plus(2)
                if second.exists():
                    clip(second)
                for c in range(CH):
                    if c == 0:
                        dve.wait_ge(exp_done, (u.n + 1) * QUADS)
                    dve.wait_ge(g_done, u.n * CH + (c + 1))
                    e = prob[:, :, 32 * c:32 * c + 32]
                    nc.vector.scalar_tensor_tensor(out=e, in0=ps_g[c % 2][:].rearrange("p (h n) -> p h n", h=H),
                                                   scalar=GEO_MIN, in1=e, op0=ALU.max, op1=ALU.mult).then_inc(mult_done, 1)
                    if c < 2 and nxt.exists():
                        fractions(nxt, 2 + c)
                    if c == 6:
                        low_part(u, 3)
                low_part(u, 6)
                low_part(u, 7)
                for j in range(PAIRS):
                    dve.wait_ge(pv_done, u.n * PAIRS + (j + 1))
                    at = acc[:, :, j, :]
                    src = ps_o[j % 2][:].rearrange("p (e s) -> p e s", e=2)
                    if u.w == 0:
                        if j == 0:
                            wait(dve, o_low, u.r * 4)
                        ins = nc.vector.tensor_copy(at, src)
                    else:
                        ins = nc.vector.tensor_tensor(at, src, at, ALU.add)
                    ins.then_inc(acc_done, 1)
                    if j in (1, 5) and second.exists():
                        fractions(second, j // 4)
                    if j in (3, 7) and nxt.exists():
                        low_features(nxt, j // 4)
                if u.w < NB - 1:
                    return
                dve.wait_ge(sum_in, u.r * 32 + 32)
                nc.vector.reciprocal(rec[:], sums[:]).then_inc(rec_done, 1)
                dve.wait_ge(rec_done, u.r * 3 + 1)
                nc.vector.tensor_copy(rec_hi[:], rec[:]).then_inc(rec_done, 1)
                dve.wait_ge(rec_done, u.r * 3 + 2)
                nc.vector.tensor_tensor(rec_lo[:], rec[:], rec_hi[:].bitcast(F32), ALU.subtract).then_inc(rec_done, 1)
                for i in range(4):
                    dve.wait_ge(bc_done, u.r * 4 + (i + 1))
                    js = slice(2 * i, 2 * i + 2)
                    src = ps_g[i % 2][:].rearrange("p (j s) -> p j s", j=2)
                    for at, e in ((0, 0), (64, 1)):
                        rows = slice(at, at + 64)
                        nc.vector.tensor_tensor(acc[rows, 0, js, :], acc[rows, e, js, :], src[rows], ALU.mult).then_inc(normed, 1)
                dve.wait_ge(out_done, u.r + 1)
                dve.wait_ge(x_in, u.r * 16 + 16)
                for t in range(QB):
                    last = nc.vector.scalar_tensor_tensor(out=x_sb[:, t, :], in0=ps_o[t][:, 0:D], scalar=tg[:], in1=x_sb[:, t, :],
                                                          op0=ALU.mult, op1=ALU.add)
                last.then_inc(x1_part, 1)
                dve.wait_ge(x1_part, u.r + 1)
                nc.vector.tensor_tensor(x_sb[:], x_sb[:], bias_row[:].unsqueeze(1).to_broadcast([P, QB, D]), ALU.add).then_inc(x1_done, 1)

            every_unit(dve, step)

        @block.tensor
        def _(pe):
            pe.sem_inc(mult_done, 2)
            pe.sem_inc(acc_done, 2)
            pe.wait_ge(pro_in, 320)
            pe.wait_ge(pro_dve, 4)
            for j in range(PAIRS):
                last = nc.tensor.matmul(ps_g[0][:, 0:D], bvw[:, j, :], wo_in[:, j, :], start=j == 0, stop=j == PAIRS - 1)
            last.then_inc(pro_pe, 1)
            pe.wait_ge(pro_dve, 9)

            def scores(u, q):
                if q == 0:
                    pe.wait_ge(k_in, u.n * 32 + 32)
                    if u.w == 0:
                        pe.wait_ge(q_in, u.r * 80 + 80)
                wait(pe, exp_done, u.n * QUADS + (q - 1))
                for a in range(2):
                    nc.tensor.matmul(ps_s[q % 2][:, a, :], pick[:, 2 * q + a:2 * q + a + 1].to_broadcast([P, P]), negm[:],
                                     start=True, stop=False)
                    for e in range(2):
                        h = 4 * q + 2 * a + e
                        out = ps_s[q % 2][:, a, e * RQ:(e + 1) * RQ]
                        nc.tensor.matmul(out, k_sb[:, h, :], q_hi[:, h, :], start=False, stop=False)
                        last = nc.tensor.matmul(out, k_sb[:, h, :], q_lo[:, h, :], start=False, stop=e == 1)
                last.then_inc(s_done, 1)

            def geometry(u, c):
                blk = c // 4
                if c == 0:
                    pe.wait_ge(z_in[u.w % 2], u.b * (4 * 16) + (4 * u.half + u.w) // 2 * 16 + 16)
                    if u.w == 0:
                        pe.wait_ge(y_in, u.r * 32 + 32)
                if c % 4 == 0:
                    pe.wait_ge(f_high, u.n * QB + (blk + 1))
                    pe.wait_ge(f_low, u.n * QB + (blk + 1))
                pe.wait_ge(mult_done, u.n * CH + (c + 1))
                out = ps_g[c % 2][:].rearrange("p (h n) -> p h n", h=H)
                at = 32 * (c % 4)
                nc.tensor.matmul(out, zs[u.w % 2][:], ys[:, blk, :, at:at + 32], start=True, stop=False)
                for g in range(2):
                    grp = 2 * (c % 4) + g
                    for feats, w in ((f_hi, 0), (f_hi, 1), (f_lo, 0)):
                        last = nc.tensor.matmul(out[:, :, 16 * g:16 * g + 16], feats[blk][:, grp, :], wide[w][:],
                                                start=False, stop=g == 1 and feats is f_lo)
                last.then_inc(g_done, 1)

            def values(u, j):
                pe.wait_ge(acc_done, u.n * PAIRS + (j + 1))
                for e in range(2):
                    h = 2 * j + e
                    at = slice(DK * e, DK * e + P)
                    out = ps_o[j % 2][:, e * RQ:(e + 1) * RQ]
                    low = p_lo[:, h, :]
                    nc.tensor.matmul(out, v_hi[:, j, at], p_hi[:, h, :], start=True, stop=False)
                    nc.tensor.matmul(out, v_hi[:, j, at], low, start=False, stop=False)
                    last = nc.tensor.matmul(out, v_lo[:, j, at], p_hi[:, h, :], start=False, stop=True)
                last.then_inc(pv_done, 1)

            for q in range(QUADS):
                scores(first, q)

            def step(u):
                nxt = u.plus(1)
                beside = nxt.exists() and u.w < NB - 1
                for c in range(CH):
                    geometry(u, c)
                if beside:
                    scores(nxt, 0)
                    scores(nxt, 1)
                pe.wait_ge(p_low, u.n * CH + CH)
                pe.wait_ge(v_in, u.n * 64 + 64)
                if u.w == 0:
                    wait(pe, x1_part, u.r)
                for j in range(PAIRS):
                    values(u, j)
                    if beside and j in (1, 3):
                        scores(nxt, 2 + j // 2)
                if u.w < NB - 1:
                    return
                if nxt.exists():
                    for q in range(QUADS):
                        scores(nxt, q)
                pe.wait_ge(rec_in, u.r * 64 + 64)
                for i in range(4):
                    if i < 2:
                        pe.wait_ge(mult_done, (u.n + 1) * CH + 2)
                    else:
                        pe.wait_ge(normed, u.r * 8 + (2 * i - 2))
                    nc.tensor.matmul(ps_g[i % 2][:], spread[:], recs[:, 512 * i:512 * i + 512], start=True, stop=True).then_inc(bc_done, 1)
                pe.wait_ge(acc_done, (u.n + 1) * PAIRS + 2)
                for j in range(PAIRS):
                    if j % 2 == 0:
                        pe.wait_ge(o_low, u.r * 4 + (j // 2 + 1))
                    for t in range(QB):
                        out = ps_o[t][:, 0:D]
                        for o, w in ((o_hi, wo_hi), (o_hi, wo_lo), (o_lo, wo_hi)):
                            last = nc.tensor.matmul(out, o[:, j, t * P:(t + 1) * P], w[:, j, :],
                                                    start=j == 0 and w is wo_hi and o is o_hi, stop=j == PAIRS - 1 and o is o_lo)
                last.then_inc(out_done, 1)

            every_unit(pe, step)


def route(nc, x1_dram, rw1, rb1, rw2, rb2, gate, xs_dram, slot, weight, tile_expert):
    with ExitStack() as ctx:
        m = Space(nc, ctx, "rt_")
        rw1_sb, rb1_sb = m.sb("rw1", [P, KD, HID]), m.sb("rb1", [P, HID // P])
        rw2_sb, rb2_sb = m.sb("rw2", [P, HID // P, E]), m.sb("rb2", [P, E])
        tg = m.sb("tg", [P, 1])
        ident, eps, zeros = m.sb("ident", [P, P]), m.sb("eps", [P, 1]), m.sb("zeros", [P, 8, D])
        below, ones = m.sb("below", [P, P]), m.sb("ones", [P, P])
        xt = [m.sb(f"xt{i}", [P, NB, D]) for i in range(1)][0]
        xn = m.sb("xn", [P, NT, D])
        stats, mv = m.sb("stats", [P, NB, 6]), m.sb("mv", [P, NB, 2])
        sd, rstd = m.sb("sd", [P, NB]), m.sb("rstd", [P, NB])
        xn_t, hid = m.sb("xn_t", [P, KD, S]), m.sb("hid", [P, HID // P, S])
        lg = m.sb("lg", [P, NT, E])
        top, top_i = m.sb("top", [P, NT, 8]), m.sb("top_i", [P, NT, 8], U32)
        top_f = m.sb("top_f", [P, NT, 2])
        iota_i, iota_f = m.sb("iota_i", [P, E], I32), m.sb("iota_f", [P, E])
        one_hot = [m.sb(f"one_hot{i}", [P, NT, E]) for i in range(2)]
        both, before, upto, total = (m.sb(n, [P, NT, E]) for n in ("both", "before", "upto", "total"))
        gap, den = m.sb("gap", [P, NT]), m.sb("den", [P, NT])
        tiles, tiles_r, first = m.sb("tiles", [P, E]), m.sb("tiles_r", [P, E]), m.sb("first", [P, E])
        slot_f = m.sb("slot_f", [P, NT, 2])
        tile_i, reached = m.sb("tile_i", [1, N_TILES], I32), m.sb("reached", [1, N_TILES, E])
        tile_f, te_f = m.sb("tile_f", [1, N_TILES]), m.sb("te_f", [1, N_TILES])
        ps_t = m.ps("ps_t", [P, 2, 512])
        ps_h = [m.ps(f"ps_h{i}", [P, 512]) for i in range(2)]
        ps_l, ps_c, ps_n = m.ps("ps_l", [P, NB, E]), m.ps("ps_c", [P, 512]), m.ps("ps_n", [P, 512])

        sem = m.sem
        w_in, x_in, zeroed, zero_stored, pool_done, eps_done, relay = (
            sem(n) for n in ("w_in", "x_in", "zeroed", "zero_stored", "pool_done", "eps_done", "relay"))
        stat, scaled, normed, kept, turned, xn_ready = (sem(n) for n in ("stat", "scaled", "normed", "kept", "turned", "xn_ready"))
        h_done, h_ready, l_done, l_ready = (sem(n) for n in ("h_done", "h_ready", "l_done", "l_ready"))
        tg_done, step, gap_exp, counted, slots_ready, scattered = (
            sem(n) for n in ("tg_done", "step", "gap_exp", "counted", "slots_ready", "scattered"))
        NH = HID // P
        block = ctx.enter_context(nc.Block())

        @block.sync
        def _(sp):
            sp.dma_start(rw1_sb[:], rw1.rearrange("(k p) n -> p k n", p=P)).then_inc(w_in, 16)
            sp.dma_start(rb1_sb[:], rb1).then_inc(w_in, 16)
            sp.dma_start(rw2_sb[:], rw2.rearrange("(j p) e -> p j e", p=P)).then_inc(w_in, 16)
            sp.dma_start(rb2_sb[:], rb2.partition_broadcast(P)).then_inc(w_in, 16)
            sp.dma_start(tg[:], gate.partition_broadcast(P)).then_inc(w_in, 16)
            sp.wait_ge(zeroed, 1)
            for i in range(SLOTS // (8 * P)):
                sp.dma_start(xs_dram[i * 8 * P:(i + 1) * 8 * P, :].rearrange("(t p) d -> p t d", p=P), zeros[:]).then_inc(zero_stored, 16)
            with sp.Fori(0, B) as b:
                sp.wait_ge(kept, b + 1)
                sp.sem_inc(relay, 1)
                sp.wait_ge(turned, b + 1)
                sp.sem_inc(relay, 1)
                sp.dma_start(xt[:], x1_dram[bass.ds(b * S, S), :].rearrange("(t p) d -> p t d", p=P)).then_inc(x_in, 16)
            sp.wait_ge(zero_stored, 16 * (SLOTS // (8 * P)))

        @block.gpsimd
        def _(pool):
            nc.gpsimd.memset(zeros[:], 0.0).then_inc(zeroed, 1)
            make_identity(nc, pool, ident, pool_done)
            nc.gpsimd.memset(ones[:], 1.0).then_inc(pool_done, 1)
            pool.wait_ge(pool_done, 3)
            nc.gpsimd.affine_select(out=below[:], in_=ones[:], compare_op=ALU.is_gt, fill=0.0, base=0,
                                    pattern=[[1, P]], channel_multiplier=-1).then_inc(pool_done, 1)
            nc.gpsimd.iota(iota_i[:], pattern=[[1, E]], base=0, channel_multiplier=0).then_inc(pool_done, 1)
            nc.gpsimd.iota(tile_i[:], pattern=[[SLOT_TILE, N_TILES]], base=0, channel_multiplier=0).then_inc(pool_done, 1)
            with pool.Fori(0, B) as b:
                pool.wait_ge(normed, b * NB + NB)
                pool.sem_inc(relay, 1)
                nc.gpsimd.tensor_copy(xn[:, bass.ds(b * NB, NB), :], xt[:]).then_inc(kept, 1)
            pool.wait_ge(kept, B + 1)
            pool.wait_ge(slots_ready, 1)
            pool.wait_ge(zero_stored, 16 * (SLOTS // (8 * P)))
            for t in range(NT):
                for c in range(2):
                    nc.gpsimd.indirect_dma_start(xs_dram, bass.IndirectOffsetOnAxis(slot[:, c, t:t + 1], 0), xn[:, t, :], None
                                                 ).then_inc(scattered, 16)
            pool.wait_ge(scattered, 32 * NT)

        @block.vector
        def _(dve):
            nc.vector.memset(eps[:], EPS).then_inc(eps_done, 1)
            with dve.Fori(0, B) as b:
                dve.wait_ge(x_in, b * 16 + 16)
                for t in range(NB):
                    nc.vector.bn_stats(stats[:, t, :], xt[:, t, :]).then_inc(stat, 1)
                dve.wait_ge(stat, b * (2 * NB + 1) + NB)
                dve.sem_inc(relay, 1)
                for t in range(NB):
                    nc.vector.bn_aggr(mv[:, t, :], stats[:, t, :]).then_inc(stat, 1)
                dve.wait_ge(scaled, b + 1)
                nc.vector.reciprocal(rstd[:], sd[:]).then_inc(stat, 1)
                dve.wait_ge(stat, b * (2 * NB + 1) + 2 * NB + 1)
                for t in range(NB):
                    nc.vector.tensor_scalar(xt[:, t, :], xt[:, t, :], mv[:, t, 0:1], rstd[:, t:t + 1],
                                            ALU.subtract, ALU.mult).then_inc(normed, 1)
                dve.wait_ge(l_done, b + 1)
                nc.vector.tensor_tensor(lg[:, bass.ds(b * NB, NB), :], ps_l[:], rb2_sb[:].unsqueeze(1).to_broadcast([P, NB, E]),
                                        ALU.add).then_inc(l_ready, 1)
            count = [0]

            def link(ins):
                count[0] += 1
                ins.then_inc(step, 1)
                dve.wait_ge(step, count[0])

            dve.wait_ge(l_ready, B + 1)
            dve.wait_ge(pool_done, 6)
            for t in range(NT):
                last = nc.vector.max(top[:, t, :], lg[:, t, :])
            link(last)
            for t in range(NT):
                nc.vector.max_index(top_i[:, t, :], top[:, t, :], lg[:, t, :])
            nc.vector.tensor_copy(iota_f[:], iota_i[:])
            nc.vector.tensor_copy(tile_f[:], tile_i[:])
            link(nc.vector.tensor_tensor(gap[:], top[:, :, 1], top[:, :, 0], ALU.subtract))
            link(nc.vector.tensor_copy(top_f[:], top_i[:, :, 0:2]))
            for c in range(2):
                link(nc.vector.tensor_tensor(one_hot[c][:], top_f[:, :, c:c + 1].to_broadcast([P, NT, E]),
                                             iota_f[:].unsqueeze(1).to_broadcast([P, NT, E]), ALU.is_equal))
            nc.vector.tensor_tensor(both[:], one_hot[0][:], one_hot[1][:], ALU.add).then_inc(counted, 1)
            dve.wait_ge(gap_exp, 1)
            link(nc.vector.tensor_scalar(den[:], gap[:], 1.0, None, ALU.add))
            link(nc.vector.reciprocal(den[:], den[:]))
            link(nc.vector.tensor_scalar(weight[:, 0, :], den[:], tg[:], None, ALU.mult))
            nc.vector.tensor_tensor(weight[:, 1, :], weight[:, 0, :], gap[:], ALU.mult)
            dve.wait_ge(counted, 2)
            link(nc.vector.tensor_copy(total[:].rearrange("p t e -> p (t e)"), ps_n[:, 0:NT * E]))
            for e in range(E):
                last = nc.vector.tensor_tensor_scan(out=upto[:, :, e], data0=total[:, :, e], data1=zeros[:, 0, 0:NT],
                                                    initial=0.0, op0=ALU.add, op1=ALU.add)
            link(last)
            nc.vector.tensor_tensor(before[:], upto[:], total[:], ALU.subtract)
            link(nc.vector.tensor_scalar(tiles[:], upto[:, NT - 1, :], 1.0 / SLOT_TILE,
                                         (SLOT_TILE - 1.0) / SLOT_TILE - 0.5 + 0.5 / SLOT_TILE, ALU.mult, ALU.add))
            link(nc.vector.tensor_scalar(tiles_r[:], tiles[:], ROUND, None, ALU.add))
            link(nc.vector.tensor_scalar(tiles[:], tiles_r[:], ROUND, float(SLOT_TILE), ALU.subtract, ALU.mult))
            link(nc.vector.tensor_tensor_scan(out=first[:], data0=tiles[:], data1=zeros[:, 0, 0:E], initial=0.0,
                                              op0=ALU.add, op1=ALU.add))
            link(nc.vector.tensor_tensor(first[:], first[:], tiles[:], ALU.subtract))
            link(nc.vector.tensor_tensor(before[:].rearrange("p t e -> p (t e)"), before[:].rearrange("p t e -> p (t e)"),
                                         ps_c[:, 0:NT * E], ALU.add))
            link(nc.vector.tensor_tensor(before[:], before[:], first[:].unsqueeze(1).to_broadcast([P, NT, E]), ALU.add))
            for c in range(2):
                link(nc.vector.tensor_tensor(one_hot[c][:], one_hot[c][:], before[:], ALU.mult))
                link(nc.vector.tensor_reduce(slot_f[:, :, c], one_hot[c][:], op=ALU.add, axis=AX))
                nc.vector.tensor_copy(slot[:, c, :], slot_f[:, :, c])
            link(nc.vector.tensor_tensor(reached[:], first[0:1, :].unsqueeze(1).to_broadcast([1, N_TILES, E]),
                                         tile_f[:].unsqueeze(2).to_broadcast([1, N_TILES, E]), ALU.is_le))
            link(nc.vector.tensor_reduce(te_f[:], reached[:, :, 1:E], op=ALU.add, axis=AX))
            nc.vector.tensor_copy(tile_expert[:], te_f[:]).then_inc(slots_ready, 1)

        @block.scalar
        def _(act):
            act.wait_ge(eps_done, 1)
            act.wait_ge(w_in, 80)
            with act.Fori(0, B) as b:
                act.wait_ge(stat, b * (2 * NB + 1) + 2 * NB)
                nc.scalar.activation(sd[:], mv[:, :, 1], ACT.Sqrt, bias=eps[:]).then_inc(scaled, 1)
                act.wait_ge(turned, b + 2)
                nc.scalar.copy(xn_t[:], ps_t[:]).then_inc(xn_ready, 1)
                for j in range(NH):
                    act.wait_ge(h_done, b * NH + j + 1)
                    nc.scalar.activation(hid[:, j, :], ps_h[j % 2][:], ACT.Silu, bias=rb1_sb[:, j:j + 1]).then_inc(h_ready, 1)
            nc.scalar.activation(tg[:], tg[:], ACT.Tanh).then_inc(tg_done, 1)
            act.wait_ge(step, 3)
            act.wait_ge(tg_done, 1)
            nc.scalar.activation(gap[:], gap[:], ACT.Exp).then_inc(gap_exp, 1)

        @block.tensor
        def _(pe):
            for free, count in ((kept, 1), (turned, 1), (h_ready, 2), (l_ready, 1)):
                pe.sem_inc(free, count)
            pe.wait_ge(pool_done, 2)
            pe.wait_ge(w_in, 80)
            with pe.Fori(0, B) as b:
                pe.wait_ge(normed, b * NB + NB)
                for t in range(NB):
                    for k in range(KD):
                        last = nc.tensor.transpose(ps_t[:, k, t * P:(t + 1) * P], xt[:, t, k * P:(k + 1) * P], ident[:])
                last.then_inc(turned, 1)
                pe.wait_ge(xn_ready, b + 1)
                for j in range(NH):
                    pe.wait_ge(h_ready, b * NH + j + 1)
                    for k in range(KD):
                        last = nc.tensor.matmul(ps_h[j % 2][:], rw1_sb[:, k, j * P:(j + 1) * P], xn_t[:, k, :],
                                                start=k == 0, stop=k == KD - 1)
                    last.then_inc(h_done, 1)
                pe.wait_ge(h_ready, b * NH + NH + 2)
                pe.wait_ge(l_ready, b + 1)
                for t in range(NB):
                    for j in range(NH):
                        last = nc.tensor.matmul(ps_l[:, t, :], hid[:, j, t * P:(t + 1) * P], rw2_sb[:, j, :],
                                                start=j == 0, stop=j == NH - 1)
                last.then_inc(l_done, 1)
            pe.wait_ge(counted, 1)
            pe.wait_ge(pool_done, 4)
            flat = both[:].rearrange("p t e -> p (t e)")
            nc.tensor.matmul(ps_c[:, 0:NT * E], below[:], flat, start=True, stop=True)
            nc.tensor.matmul(ps_n[:, 0:NT * E], ones[:], flat, start=True, stop=True).then_inc(counted, 1)


def experts(nc, xs_dram, ys_dram, w1, b1, w2, b2, tile_expert):
    TB = SLOT_TILE // P
    NH = HID // P
    with ExitStack() as ctx:
        m = Space(nc, ctx, "ex_")
        w1_sb = [m.sb(f"w1{i}", [P, KD, HID]) for i in range(2)]
        w2_sb = [m.sb(f"w2{i}", [P, NH, D]) for i in range(2)]
        b1_sb = [m.sb(f"b1{i}", [P, NH]) for i in range(2)]
        b2_sb = [m.sb(f"b2{i}", [P, D]) for i in range(2)]
        xt = [m.sb(f"xt{i}", [P, TB, D]) for i in range(2)]
        x_t = [m.sb(f"x_t{i}", [P, KD, SLOT_TILE]) for i in range(2)]
        hid = [m.sb(f"hid{i}", [P, NH, SLOT_TILE]) for i in range(2)]
        yt = [m.sb(f"yt{i}", [P, TB, D]) for i in range(2)]
        ident = m.sb("ident", [P, P])
        ps_t = m.ps("ps_t", [P, KD, SLOT_TILE])
        ps_h = [m.ps(f"ps_h{i}", [P, 512]) for i in range(4)]
        ps_y = [m.ps(f"ps_y{i}", [P, TB, D]) for i in range(2)]
        sem = m.sem
        load_in = [sem(f"load_in{i}") for i in range(2)]
        stored = [sem(f"stored{i}") for i in range(2)]
        y_free, ident_done, relay, turned, x_ready, h_done, h_ready, y_done, y_ready = (
            sem(n) for n in ("y_free", "ident_done", "relay", "turned", "x_ready", "h_done", "h_ready", "y_done", "y_ready"))
        block = ctx.enter_context(nc.Block())

        @block.sync
        def _(sp):
            with sp.Fori(0, N_TILES // 2) as pair:
                for i in range(2):
                    tile = pair * 2 + i
                    e = sp.value_load(tile_expert[0:1, bass.ds(tile, 1)], min_val=0, max_val=E - 1)
                    sp.wait_ge(y_ready, pair * 2 + i + 1)
                    sp.sem_inc(relay, 1)
                    sp.dma_start(xt[i][:], xs_dram[bass.ds(tile * SLOT_TILE, SLOT_TILE), :].rearrange("(t p) d -> p t d", p=P)
                                 ).then_inc(load_in[i], 16)
                    sp.dma_start(w1_sb[i][:], w1[bass.ds(e, 1)].rearrange("o (k p) n -> p (o k) n", p=P)).then_inc(load_in[i], 16)
                    sp.dma_start(b1_sb[i][:], b1[bass.ds(e, 1)].rearrange("o p j -> p (o j)")).then_inc(load_in[i], 16)
                    sp.dma_start(b2_sb[i][:], b2[bass.ds(e, 1)].rearrange("o d -> (o d)").partition_broadcast(P)).then_inc(load_in[i], 16)
                    sp.dma_start(w2_sb[i][:], w2[bass.ds(e, 1)].rearrange("o (j p) d -> p (o j) d", p=P)).then_inc(load_in[i], 16)

        @block.gpsimd
        def _(pool):
            make_identity(nc, pool, ident, ident_done)
            with pool.Fori(0, N_TILES // 2) as pair:
                for i in range(2):
                    pool.wait_ge(y_ready, pair * 2 + i + 3)
                    pool.sem_inc(relay, 1)
                    pool.dma_start(ys_dram[bass.ds((pair * 2 + i) * SLOT_TILE, SLOT_TILE), :].rearrange("(t p) d -> p t d", p=P),
                                   yt[i][:]).then_inc(stored[i], 16)
                    pool.wait_ge(stored[i], pair * 16 + 16)
                    pool.sem_inc(y_free, 1)

        @block.scalar
        def _(act):
            with act.Fori(0, N_TILES // 2) as pair:
                for i in range(2):
                    tile = pair * 2 + i
                    act.wait_ge(load_in[i], pair * 80 + 80)
                    for j in range(NH):
                        act.wait_ge(h_done, tile * NH + j + 1)
                        nc.scalar.activation(hid[i][:, j, :], ps_h[j % 4][:, 0:SLOT_TILE], ACT.Silu, bias=b1_sb[i][:, j:j + 1]
                                             ).then_inc(h_ready, 1)

        @block.vector
        def _(dve):
            with dve.Fori(0, N_TILES // 2) as pair:
                for i in range(2):
                    tile = pair * 2 + i
                    dve.wait_ge(turned, tile + 1)
                    nc.vector.tensor_copy(x_t[i][:], ps_t[:]).then_inc(x_ready, 1)
                    dve.wait_ge(y_done, tile + 3)
                    dve.wait_ge(y_free, tile + 1)
                    nc.vector.tensor_tensor(yt[i][:], ps_y[i][:], b2_sb[i][:].unsqueeze(1).to_broadcast([P, TB, D]), ALU.add
                                            ).then_inc(y_ready, 1)

        @block.tensor
        def _(pe):
            for free, count in ((y_done, 2), (x_ready, 1), (h_ready, 4), (y_ready, 2), (y_free, 2)):
                pe.sem_inc(free, count)
            pe.wait_ge(ident_done, 2)
            with pe.Fori(0, N_TILES // 2) as pair:
                for i in range(2):
                    tile = pair * 2 + i
                    pe.wait_ge(load_in[i], pair * 80 + 80)
                    pe.wait_ge(x_ready, tile + 1)
                    for t in range(TB):
                        for k in range(KD):
                            last = nc.tensor.transpose(ps_t[:, k, t * P:(t + 1) * P], xt[i][:, t, k * P:(k + 1) * P], ident[:])
                    last.then_inc(turned, 1)
                    pe.wait_ge(x_ready, tile + 2)
                    for j in range(NH):
                        pe.wait_ge(h_ready, tile * NH + j + 1)
                        for k in range(KD):
                            last = nc.tensor.matmul(ps_h[j % 4][:, 0:SLOT_TILE], w1_sb[i][:, k, j * P:(j + 1) * P], x_t[i][:, k, :],
                                                    start=k == 0, stop=k == KD - 1)
                        last.then_inc(h_done, 1)
                    pe.wait_ge(h_ready, tile * NH + NH + 4)
                    pe.wait_ge(y_ready, tile + 1)
                    for t in range(TB):
                        for j in range(NH):
                            last = nc.tensor.matmul(ps_y[i][:, t, :], hid[i][:, j, t * P:(t + 1) * P], w2_sb[i][:, j, :],
                                                    start=j == 0, stop=j == NH - 1)
                    last.then_inc(y_done, 1)


def combine(nc, x1_dram, ys_dram, slot, weight, out):
    with ExitStack() as ctx:
        m = Space(nc, ctx, "cb_")
        DEPTH = 4
        x1 = m.sb("x1", [P, NT, D])
        row = [[m.sb(f"row{c}_{i}", [P, D]) for i in range(DEPTH)] for c in range(2)]
        sem = m.sem
        x_in = sem("x_in")
        gathered = [sem(f"gathered{i}") for i in range(DEPTH)]
        added, ready, stored = sem("added"), sem("ready"), sem("stored")
        block = ctx.enter_context(nc.Block())

        @block.gpsimd
        def _(pool):
            for t in range(NT):
                if t >= DEPTH:
                    pool.wait_ge(ready, t - DEPTH + 1)
                for c in range(2):
                    nc.gpsimd.indirect_dma_start(row[c][t % DEPTH][:], None, ys_dram, bass.IndirectOffsetOnAxis(slot[:, c, t:t + 1], 0)
                                                 ).then_inc(gathered[t % DEPTH], 16)

        @block.vector
        def _(dve):
            dve.wait_ge(x_in, 16)
            for t in range(NT):
                dve.wait_ge(gathered[t % DEPTH], 32 * (t // DEPTH) + 32)
                nc.vector.scalar_tensor_tensor(out=x1[:, t, :], in0=row[0][t % DEPTH][:], scalar=weight[:, 0, t:t + 1],
                                               in1=x1[:, t, :], op0=ALU.mult, op1=ALU.add).then_inc(added, 1)
                dve.wait_ge(added, t + 1)
                nc.vector.scalar_tensor_tensor(out=x1[:, t, :], in0=row[1][t % DEPTH][:], scalar=weight[:, 1, t:t + 1],
                                               in1=x1[:, t, :], op0=ALU.mult, op1=ALU.add).then_inc(ready, 1)

        @block.sync
        def _(sp):
            view = out.rearrange("(t p) d -> p t d", p=P)
            sp.dma_start(x1[:], x1_dram.rearrange("(t p) d -> p t d", p=P)).then_inc(x_in, 16)
            for t in range(0, NT, 4):
                sp.wait_ge(ready, t + 4)
                sp.dma_start(view[:, t:t + 4, :], x1[:, t:t + 4, :]).then_inc(stored, 16)
            sp.wait_ge(stored, 16 * NT // 4)


def program(nc, x, ctx_t, boxes, g_xattn, g_ffn, wq, bq, wk, bk, wv, bv, wo, bo, wg_rows, wg_feat, bg,
            rw1, rb1, rw2, rb2, w1, b1, w2, b2, out):
    def scratch(name, shape):
        return nc.dram_tensor(name, shape, F32, kind="Internal").ap()

    q_dram = [scratch(f"q_{part}", [B, DK, H, S]) for part in ("hi", "lo")]
    k_dram = [scratch(f"k_{part}", [B, DK, H, S]) for part in ("hi", "lo")]
    v_dram = [scratch(f"v_{part}", [B, P, NB, HD]) for part in ("hi", "lo")]
    negm_dram = scratch("neg_max", [B, H, S])
    y_dram, z_dram = scratch("y_geometry", [NT, 3, SEP, YCOLS]), scratch("z_geometry", [3, SEP, B, S])
    c_dram = scratch("centre_rows", [2, B, S])
    x1_dram = scratch("x1_rows", [TOK, D])
    xs_dram, ys_dram = scratch("expert_in", [SLOTS, D]), scratch("expert_out", [SLOTS, D])
    with ExitStack() as ctx:
        m = Space(nc, ctx, "")
        with ExitStack() as boxes_ctx:
            k = Space(nc, boxes_ctx, "")
            centre, inv_size = k.sb("centre", [P, NT, 2]), k.sb("inv_size", [P, NT, 2])
            box_terms(nc, boxes, wg_rows, bg, y_dram, z_dram, c_dram, centre, inv_size)
            project(nc, x, ctx_t, wq, wk, wv, bq, bk, q_dram, k_dram, v_dram, negm_dram)
            attend(nc, x, q_dram, k_dram, v_dram, negm_dram, y_dram, z_dram, c_dram, wg_feat, wo, bv, bo, g_xattn,
                   centre, inv_size, x1_dram)
        slot = m.sb("slot", [P, 2, NT], U32)
        weight = m.sb("weight", [P, 2, NT])
        tile_expert = m.sb("tile_expert", [1, N_TILES], I32)
        route(nc, x1_dram, rw1, rb1, rw2, rb2, g_ffn, xs_dram, slot, weight, tile_expert)
        experts(nc, xs_dram, ys_dram, w1, b1, w2, b2, tile_expert)
        combine(nc, x1_dram, ys_dram, slot, weight, out)


def kernel(**inputs):
    import numpy as np
    import concourse.bacc as bacc
    from concourse.bass_utils import run_bass_kernel_spmd

    a = {n.replace("L0_xattn_", "").replace("L0_ffn_", "ffn_"): np.asarray(v) for n, v in inputs.items()}
    per_row = lambda v: v.reshape(-1, P).T
    laid = {
        "x": a["x"].reshape(TOK, D), "ctx_t": a["ctx_1024"].reshape(TOK, D).T, "boxes": a["fside_BxSx4_0"].reshape(TOK, 4),
        "g_xattn": a["g_xattn"], "g_ffn": a["g_ffn"],
        "wq": a["Wq"].T, "bq": per_row(a["bq"]), "wk": a["Wk"].T, "bk": per_row(a["bk"]),
        "wv": a["Wv"].T, "bv": per_row(a["bv"]), "wo": a["Wo"].T, "bo": a["bo"],
        "wg_rows": a["Wg"].T, "wg_feat": a["Wg"].T[[0, 2, 1, 3, 8, 10, 9, 11]], "bg": a["bg"],
        "rw1": a["ffn_rw1"], "rb1": per_row(a["ffn_rb1"]), "rw2": a["ffn_rw2"], "rb2": a["ffn_rb2"],
        "w1": a["ffn_w1"], "b1": a["ffn_b1"].reshape(E, -1, P).transpose(0, 2, 1), "w2": a["ffn_w2"], "b2": a["ffn_b2"],
    }
    laid = {n: np.ascontiguousarray(v) for n, v in laid.items()}
    nc = bacc.Bacc("TRN2", target_bir_lowering=False, num_devices=1)
    handles = {n: nc.dram_tensor("in_" + n, v.shape, mybir.dt.from_np(v.dtype), kind="ExternalInput").ap() for n, v in laid.items()}
    out = nc.dram_tensor("out", [TOK, D], F32, kind="ExternalOutput").ap()
    program(nc, out=out, **handles)
    got = run_bass_kernel_spmd(nc, [{"in_" + n: v for n, v in laid.items()}], core_ids=[0]).results[0]["out"]
    return got.reshape(B, S, D)
```

```python
from contextlib import ExitStack

import concourse.bass as bass
from concourse import mybir

P = 128
B, S, D = 8, 512, 256
H, DK = 16, 64
HD = H * DK
E, HID = 8, 1024
TOK = B * S
NT = TOK // P
KD = D // P
NB = S // P
PAIRS = H // 2
EPS = 1e-5
FREQ = (1.0, 1000.0 ** -0.5)
TWO_PI = 6.283185307179586
HALF_PI = TWO_PI / 4
ROUND = 12582912.0
GEO_MIN = 1e-6
SLOT_TILE = 256
N_TILES = 2 * TOK // SLOT_TILE + E
SLOTS = N_TILES * SLOT_TILE
SEP = 9
YCOLS = H * P

HALF = SEP * H // 2
GT = 8

ALU = mybir.AluOpType
ACT = mybir.ActivationFunctionType
F32 = mybir.dt.float32
F32R = mybir.dt.float32r
I32 = mybir.dt.int32
U32 = mybir.dt.uint32
AX = mybir.AxisListType.X




def wait(eng, sem, value):
    if not isinstance(value, int) or value > 0:
        eng.wait_ge(sem, value)


class Space:

    def __init__(self, nc, ctx, tag):
        self.nc, self.ctx, self.tag = nc, ctx, tag

    def sb(self, name, shape, dtype=F32):
        return self.ctx.enter_context(self.nc.sbuf_tensor(self.tag + name, shape, dtype))

    def ps(self, name, shape, dtype=F32):
        return self.ctx.enter_context(self.nc.psum_tensor(self.tag + name, shape, dtype))

    def sem(self, name):
        return self.ctx.enter_context(self.nc.semaphore(self.tag + name))


def make_identity(nc, pool, ident, done):
    nc.gpsimd.memset(ident[:], 0.0).then_inc(done, 1)
    pool.wait_ge(done, 1)
    nc.gpsimd.affine_select(out=ident[:], in_=ident[:], compare_op=ALU.not_equal, fill=1.0, base=0,
                            pattern=[[-1, P]], channel_multiplier=1).then_inc(done, 1)


def box_terms(nc, boxes, wg_rows, bg_row, y_dram, z_dram, c_dram, centre, inv_size):
    with ExitStack() as ctx:
        m = Space(nc, ctx, "box_")
        bx = m.sb("bx", [P, NT, 4])
        size = m.sb("size", [P, NT, 2])
        lg = m.sb("lg", [P, NT, 2])
        turn = m.sb("turn", [P, NT, 4])
        whole = m.sb("whole", [P, NT, 4])
        frac = m.sb("frac", [P, NT, 4])
        mag = m.sb("mag", [P, NT, 4])
        halfpi = m.sb("halfpi", [P, 1])
        sc = m.sb("sc", [P, NT, 2, 4])
        wgb = m.sb("wgb", [P, H, H])
        z = m.sb("z", [P, NT, SEP])
        y = m.sb("y", [P, NT, SEP, H])
        tmp = m.sb("tmp", [P, NT, 4, H])
        ident = m.sb("ident", [P, P])
        row = [[m.sb(f"row{part}{i}", [HALF, GT, 2, P], F32R) for i in range(2)] for part in ("hi", "lo")]
        zrow = [m.sb(f"zrow{part}", [SEP, NT * P], F32R) for part in ("hi", "lo")]
        crow = m.sb("crow", [2, NT * P])
        psy = [m.ps(f"psy{i}", [P, 512]) for i in range(4)]

        loaded, ident_done = m.sem("loaded"), m.sem("ident_done")
        step, logs, sines = m.sem("step"), m.sem("logs"), m.sem("sines")
        turned, moved, row_moved = m.sem("turned"), m.sem("moved"), m.sem("row_moved")
        row_stored = [m.sem(f"row_stored{i}") for i in range(2)]
        row_low, z_stored = m.sem("row_low"), m.sem("z_stored")
        NY, NZ = NT // 2, NT * P // 512

        def place(part, i):
            if i < NY:
                g, t = divmod(2 * i, GT)
                return row[part][g % 2][:, t:t + 2].rearrange("p t e n -> p (t e n)")
            return zrow[part][:, (i - NY) * 512:(i - NY + 1) * 512]

        def bank(i):
            return psy[i % 4][0:HALF if i < NY else SEP, :]

        block = ctx.enter_context(nc.Block())

        @block.sync
        def _(sp):
            sp.dma_start(bx[:], boxes.rearrange("(t p) c -> p t c", p=P)).then_inc(loaded, 16)
            sp.dma_start(wgb[:], wg_rows.partition_broadcast(P)).then_inc(loaded, 16)
            sp.dma_start(y[:, 0, SEP - 1, :], bg_row.partition_broadcast(P)).then_inc(loaded, 16)
            for g in range(NT // GT):
                sp.wait_ge(row_moved, GT // 2 * (g + 1))
                sp.wait_ge(row_low, GT // 2 * (g + 1))
                for part, stack in ((0, 0), (0, 1), (1, 2)):
                    rows = y_dram[GT * g:GT * (g + 1), stack].rearrange("t k (h n) -> (k h) t n", h=H)
                    for half in range(2):
                        sp.dma_start(rows[HALF * half:HALF * (half + 1)], row[part][g % 2][:, :, half, :].bitcast(F32)
                                     ).then_inc(row_stored[g % 2], 16)
            sp.wait_ge(row_moved, NY + 2 * NZ)
            sp.wait_ge(row_low, NY + NZ)
            for part, stack in ((0, 0), (1, 1), (0, 2)):
                sp.dma_start(z_dram[stack].rearrange("k b m -> k (b m)"), zrow[part][:].bitcast(F32)).then_inc(z_stored, 16)
            sp.dma_start(c_dram.rearrange("c b m -> c (b m)"), crow[:]).then_inc(z_stored, 16)
            for i in range(2):
                sp.wait_ge(row_stored[i], 96 * NT // GT // 2)
            sp.wait_ge(z_stored, 64)

        @block.gpsimd
        def _(pool):
            make_identity(nc, pool, ident, ident_done)

        @block.vector
        def _(dve):
            count = [0]

            def link(ins):
                count[0] += 1
                ins.then_inc(step, 1)
                dve.wait_ge(step, count[0])

            nc.vector.memset(halfpi[:], HALF_PI)
            nc.vector.memset(z[:, :, SEP - 1:SEP], 1.0)
            dve.wait_ge(loaded, 48)
            link(nc.vector.tensor_tensor(size[:], bx[:, :, 2:4], bx[:, :, 0:2], ALU.subtract))
            link(nc.vector.tensor_scalar(size[:], size[:], 1.0, None, ALU.add))
            nc.vector.reciprocal(inv_size[:], size[:])
            link(nc.vector.tensor_tensor(centre[:], bx[:, :, 0:2], bx[:, :, 2:4], ALU.add))
            link(nc.vector.tensor_scalar(centre[:], centre[:], 0.5, None, ALU.mult))
            nc.vector.tensor_copy(y[:, 1:NT, SEP - 1, :],
                                  y[:, 0, SEP - 1, :].unsqueeze(1).to_broadcast([P, NT - 1, H]))
            dve.wait_ge(logs, 1)
            for f in range(2):
                link(nc.vector.tensor_scalar(turn[:, :, f:4:2], lg[:], 100.0 * FREQ[f] / TWO_PI, None, ALU.mult))
            link(nc.vector.tensor_scalar(whole[:], turn[:], ROUND, None, ALU.add))
            link(nc.vector.tensor_scalar(whole[:], whole[:], ROUND, None, ALU.subtract))
            link(nc.vector.tensor_tensor(frac[:], turn[:], whole[:], ALU.subtract))
            link(nc.vector.tensor_single_scalar(mag[:].bitcast(I32), frac[:].bitcast(I32), 0x7FFFFFFF, op=ALU.bitwise_and))
            dve.wait_ge(sines, 2)
            nc.vector.tensor_copy(z[:, :, 0:8], sc[:].rearrange("p t s k -> p t (s k)"))

            def times(out, s, w):
                a = sc[:, :, s, :].unsqueeze(3).to_broadcast([P, NT, 4, H])
                c = wgb[:, w:w + 4, :].unsqueeze(1).to_broadcast([P, NT, 4, H])
                link(nc.vector.tensor_tensor(out, a, c, ALU.mult))

            times(y[:, :, 0:4, :], 1, 4)
            times(tmp[:], 0, 12)
            link(nc.vector.tensor_tensor(y[:, :, 0:4, :], y[:, :, 0:4, :], tmp[:], ALU.add))
            times(y[:, :, 4:8, :], 1, 12)
            times(tmp[:], 0, 4)
            link(nc.vector.tensor_tensor(y[:, :, 4:8, :], y[:, :, 4:8, :], tmp[:], ALU.subtract))
            dve.sem_inc(moved, 1)
            for i in range(NY + NZ):
                dve.wait_ge(row_moved, i + 1)
                nc.vector.tensor_tensor(place(1, i), bank(i), place(0, i).bitcast(F32), ALU.subtract).then_inc(row_low, 1)

        @block.scalar
        def _(act):
            act.wait_ge(step, 2)
            nc.scalar.activation(lg[:], size[:], ACT.Ln).then_inc(logs, 1)
            act.wait_ge(step, 10)
            nc.scalar.activation(sc[:, :, 1, :], frac[:], ACT.Sin, scale=TWO_PI).then_inc(sines, 1)
            nc.scalar.activation(sc[:, :, 0, :], mag[:], ACT.Sin, scale=-TWO_PI, bias=halfpi[:]).then_inc(sines, 1)
            for i in range(NY + 2 * NZ):
                act.wait_ge(turned, i + 1)
                g = 2 * i // GT
                if i < NY and g >= 2 and 2 * i % GT == 0:
                    act.wait_ge(row_stored[g % 2], 96 * (g // 2))
                if i < NY + NZ:
                    nc.scalar.copy(place(0, i), bank(i)).then_inc(row_moved, 1)
                else:
                    j = i - NY - NZ
                    nc.scalar.copy(crow[:, j * 512:(j + 1) * 512], psy[i % 4][0:2, :]).then_inc(row_moved, 1)

        @block.tensor
        def _(pe):
            pe.wait_ge(ident_done, 2)
            pe.wait_ge(moved, 1)
            for i in range(NY + 2 * NZ):
                if i >= 4:
                    pe.wait_ge(row_moved, i - 3)
                    pe.wait_ge(row_low, min(i - 3, NY + NZ))
                for q in range(4):
                    if i < NY:
                        src, rows = y[:, 2 * i + q // 2].rearrange("p k h -> p (k h)")[:, HALF * (q % 2):HALF * (q % 2 + 1)], HALF
                    elif i < NY + NZ:
                        src, rows = z[:, (i - NY) * 4 + q, :], SEP
                    else:
                        src, rows = centre[:, (i - NY - NZ) * 4 + q, :], 2
                    last = nc.tensor.transpose(psy[i % 4][0:rows, q * P:(q + 1) * P], src, ident[:])
                last.then_inc(turned, 1)


def project(nc, x, ctx_t, wq, wk, wv, bq, bk, q_dram, k_dram, v_dram, negm_dram):
    with ExitStack() as ctx:
        m = Space(nc, ctx, "prj_")
        stages = [m.sb(f"stage_{n}", [P, KD, HD]) for n in "qkv"]
        w_sb = [[m.sb(f"w{n}_{part}", [P, KD, HD], F32R) for part in ("hi", "lo")] for n in "qkv"]
        bq_sb, bk_sb = m.sb("bq", [P, PAIRS]), m.sb("bk", [P, PAIRS])
        ident = m.sb("ident", [P, P])
        eps = m.sb("eps", [P, 1])
        xt = m.sb("xt", [P, NB, D])
        ct = m.sb("ct", [P, KD, S])
        ct_p = [m.sb(f"ct_{part}", [P, KD, S], F32R) for part in ("hi", "lo")]
        xn_p = [m.sb(f"xn_{part}", [P, KD, S], F32R) for part in ("hi", "lo")]
        stats, mv = m.sb("stats", [P, NB, 6]), m.sb("mv", [P, NB, 2])
        sd, rstd = m.sb("sd", [P, NB]), m.sb("rstd", [P, NB])
        q_p, k_p = ([m.sb(f"{n}_{part}", [P, PAIRS, S], F32R) for part in ("hi", "lo")] for n in "qk")
        v_p = [m.sb(f"v_{part}", [P, NB, HD], F32R) for part in ("hi", "lo")]
        full = [m.sb(f"full{i}", [P, 512]) for i in range(2)]
        top = m.sb("top", [P, NB, H])
        negm = m.sb("negm", [H, S], F32R)
        ps_t = m.ps("ps_t", [P, 2, 512])
        ps_p = [m.ps(f"ps_p{i}", [P, 512]) for i in range(2)]
        ps_s = [m.ps(f"ps_s{i}", [P, 2, 512]) for i in range(2)]

        w_in = [m.sem(f"w{n}_in") for n in "qkv"]
        w_high, w_ready, b_in, x_in, c_in, ident_done, relay = (
            m.sem(n) for n in ("w_high", "w_ready", "b_in", "x_in", "c_in", "ident_done", "relay"))
        stat, scaled, normed, turned, xn_high, xn_ready, ct_high, ct_ready = (
            m.sem(n) for n in ("stat", "scaled", "normed", "turned", "xn_high", "xn_ready", "ct_high", "ct_ready"))
        proj_done, high, full_ready, low, score_done, max_done = (
            m.sem(n) for n in ("proj_done", "high", "full_ready", "low", "score_done", "max_done"))
        max_turned, negm_ready, negm_stored = m.sem("max_turned"), m.sem("negm_ready"), m.sem("negm_stored")
        GROUPS = 4
        qk_stored, v_stored = ([m.sem(f"{n}_stored{g}") for g in range(GROUPS)] for n in ("qk", "v"))
        NPROJ = 2 * PAIRS + 2 * NB
        TURN_AT = NPROJ - 1
        NSC = PAIRS * NB
        block = ctx.enter_context(nc.Block())

        def score_turns(i):
            if i < 2 * PAIRS:
                n = 2 * (i - 2)
                return range(n, n + 2)
            n = 2 * (2 * PAIRS - 2) + (i - 2 * PAIRS)
            return range(n, n + 1) if n < NSC else range(0)

        def place(parts, i):
            if i < 2 * PAIRS:
                return parts[i % 2][:, i // 2, :]
            t, half = divmod(i - 2 * PAIRS, 2)
            return parts[2][:, t, half * 512:(half + 1) * 512]

        @block.sync
        def _(sp):
            for stage, w, arrived in zip(stages, (wq, wk, wv), w_in):
                sp.dma_start(stage[:], w.rearrange("(k p) n -> p k n", p=P)).then_inc(arrived, 16)
            sp.dma_start(bq_sb[:], bq).then_inc(b_in, 16)
            sp.dma_start(bk_sb[:], bk).then_inc(b_in, 16)

            def load(b):
                wait(sp, turned, b)
                if not isinstance(b, int):
                    sp.sem_inc(relay, 1)
                sp.dma_start(xt[:], x[bass.ds(b * S, S), :].rearrange("(t p) d -> p t d", p=P)).then_inc(x_in, 16)
                wait(sp, ct_ready, b)
                if not isinstance(b, int):
                    sp.sem_inc(relay, 1)
                sp.dma_start(ct[:], ctx_t[:, bass.ds(b * S, S)].rearrange("(k p) s -> p k s", p=P)).then_inc(c_in, 16)

            def sequence(b, last=False):
                for g in range(GROUPS):
                    for done in (high, low):
                        sp.wait_ge(done, b * NPROJ + 4 * (g + 1))
                        sp.sem_inc(relay, 1)
                    for dram, parts in ((q_dram, q_p), (k_dram, k_p)):
                        for part in range(2):
                            for e in range(2):
                                sp.dma_start(dram[part][bass.ds(b, 1), :, 4 * g:4 * g + 4].rearrange("o d (j e) s -> d (o j) e s", e=2)[:, :, e, :],
                                             parts[part][64 * e:64 * e + 64, 2 * g:2 * g + 2].bitcast(F32)).then_inc(qk_stored[g], 16)
                    if g == 0 and not last:
                        load(b + 1)
                for t in range(NB):
                    for done in (high, low):
                        sp.wait_ge(done, b * NPROJ + 2 * PAIRS + 2 * (t + 1))
                        sp.sem_inc(relay, 1)
                    for part in range(2):
                        sp.dma_start(v_dram[part][bass.ds(b, 1), :, t, :].rearrange("o p n -> p (o n)"), v_p[part][:, t].bitcast(F32)
                                     ).then_inc(v_stored[t], 16)
                sp.wait_ge(negm_ready, b + 1)
                sp.sem_inc(relay, 1)
                sp.dma_start(negm_dram[bass.ds(b, 1)].rearrange("o h s -> h (o s)"), negm[:].bitcast(F32)).then_inc(negm_stored, 16)

            load(0)
            sequence(0)
            with sp.Fori(1, B - 1) as b:
                sequence(b)
            sequence(B - 1, last=True)
            for g in range(GROUPS):
                sp.wait_ge(qk_stored[g], 128 * B)
                sp.wait_ge(v_stored[g], 32 * B)
            sp.wait_ge(negm_stored, 16 * B)

        @block.gpsimd
        def _(pool):
            make_identity(nc, pool, ident, ident_done)

            def split_context(b):
                pool.wait_ge(ct_high, b + 1)
                nc.gpsimd.tensor_tensor(ct_p[1][:], ct[:], ct_p[0][:].bitcast(F32), ALU.subtract).then_inc(ct_ready, 1)

            def sequence(b, last=False):
                for i in range(NPROJ):
                    pool.wait_ge(full_ready, b * NPROJ + (i + 1))
                    nc.gpsimd.tensor_tensor(place((q_p[1], k_p[1], v_p[1]), i), full[i % 2][:],
                                            place((q_p[0], k_p[0], v_p[0]), i).bitcast(F32), ALU.subtract).then_inc(low, 1)
                if not last:
                    split_context(b + 1)

            split_context(0)
            sequence(0)
            with pool.Fori(1, B - 1) as b:
                sequence(b)
            sequence(B - 1, last=True)

        @block.vector
        def _(dve):
            nc.vector.memset(eps[:], EPS)
            for i in range(3):
                dve.wait_ge(w_high, i + 1)
                if i == 0:
                    nc.vector.scalar_tensor_tensor(out=w_sb[0][1][:].rearrange("p k n -> p (k n)"), in0=stages[0][:].rearrange("p k n -> p (k n)"),
                                                   scalar=DK ** -0.5, in1=w_sb[0][0][:].rearrange("p k n -> p (k n)").bitcast(F32),
                                                   op0=ALU.mult, op1=ALU.subtract).then_inc(w_ready, 1)
                else:
                    nc.vector.tensor_tensor(w_sb[i][1][:], stages[i][:], w_sb[i][0][:].bitcast(F32), ALU.subtract).then_inc(w_ready, 1)
            dve.wait_ge(b_in, 32)
            nc.vector.tensor_scalar(bq_sb[:], bq_sb[:], DK ** -0.5, None, ALU.mult).then_inc(w_ready, 1)
            dve.wait_ge(w_ready, 4)

            def normalize(b):
                dve.wait_ge(x_in, b * 16 + 16)
                for t in range(NB):
                    nc.vector.bn_stats(stats[:, t, :], xt[:, t, :]).then_inc(stat, 1)
                dve.wait_ge(stat, b * (2 * NB + 1) + NB)
                dve.sem_inc(relay, 1)
                for t in range(NB):
                    nc.vector.bn_aggr(mv[:, t, :], stats[:, t, :]).then_inc(stat, 1)
                dve.wait_ge(scaled, b + 1)
                nc.vector.reciprocal(rstd[:], sd[:]).then_inc(stat, 1)
                dve.wait_ge(stat, b * (2 * NB + 1) + 2 * NB + 1)
                for t in range(NB):
                    nc.vector.tensor_scalar(xt[:, t, :], xt[:, t, :], mv[:, t, 0:1], rstd[:, t:t + 1],
                                            ALU.subtract, ALU.mult).then_inc(normed, 1)

            def low_rows(b):
                dve.wait_ge(xn_high, b + 1)
                nc.vector.tensor_tensor(xn_p[1][:], ps_t[:], xn_p[0][:].bitcast(F32), ALU.subtract).then_inc(xn_ready, 1)

            def sequence(b, last=False):
                def maximum(i):
                    j, t = divmod(i, NB)
                    dve.wait_ge(score_done, b * NSC + i + 1)
                    nc.vector.tensor_reduce(top[:, t, 2 * j:2 * j + 2], ps_s[i % 2][:], op=ALU.max, axis=AX).then_inc(max_done, 1)

                for n in range(NSC):
                    maximum(n)
                    if n == NSC - 3 and not last:
                        normalize(b + 1)
                if not last:
                    low_rows(b + 1)

            normalize(0)
            low_rows(0)
            sequence(0)
            with dve.Fori(1, B - 1) as b:
                sequence(b)
            sequence(B - 1, last=True)

        @block.scalar
        def _(act):
            for i in range(3):
                act.wait_ge(w_in[i], 16)
                if i == 0:
                    nc.scalar.activation(w_sb[0][0][:], stages[0][:], ACT.Copy, scale=DK ** -0.5).then_inc(w_high, 1)
                else:
                    nc.scalar.copy(w_sb[i][0][:], stages[i][:]).then_inc(w_high, 1)
            act.wait_ge(w_ready, 4)

            def deviation(b):
                act.wait_ge(stat, b * (2 * NB + 1) + 2 * NB)
                nc.scalar.activation(sd[:], mv[:, :, 1], ACT.Sqrt, bias=eps[:]).then_inc(scaled, 1)

            def high_context(b):
                act.wait_ge(c_in, b * 16 + 16)
                wait(act, proj_done, b * NPROJ)
                nc.scalar.copy(ct_p[0][:], ct[:]).then_inc(ct_high, 1)

            def high_rows(b):
                act.wait_ge(turned, b + 1)
                nc.scalar.copy(xn_p[0][:], ps_t[:]).then_inc(xn_high, 1)

            def sequence(b, last=False):
                for i in range(NPROJ):
                    act.wait_ge(proj_done, b * NPROJ + i + 1)
                    if i < 2 * PAIRS and i % 4 == 0:
                        wait(act, qk_stored[i // 4], b * 128)
                    elif i >= 2 * PAIRS and i % 2 == 0:
                        wait(act, v_stored[(i - 2 * PAIRS) // 2], b * 32)
                    hi, src = place((q_p[0], k_p[0], v_p[0]), i), ps_p[i % 2][:]
                    if i < 2 * PAIRS:
                        bias = (bq_sb, bk_sb)[i % 2][:, i // 2:i // 2 + 1]
                        nc.scalar.activation(hi, src, ACT.Identity, bias=bias).then_inc(high, 1)
                    else:
                        nc.scalar.copy(hi, src).then_inc(high, 1)
                    wait(act, low, b * NPROJ + (i - 1))
                    if i < 2 * PAIRS:
                        nc.scalar.activation(full[i % 2][:], src, ACT.Identity, bias=bias).then_inc(full_ready, 1)
                    else:
                        nc.scalar.copy(full[i % 2][:], src).then_inc(full_ready, 1)
                    if i == NPROJ - 3 and not last:
                        deviation(b + 1)
                    if i == TURN_AT and not last:
                        high_rows(b + 1)
                if not last:
                    high_context(b + 1)
                act.wait_ge(max_turned, b + 1)
                wait(act, negm_stored, b * 16)
                nc.scalar.activation(negm[:], ps_s[0][0:H, 0, :], ACT.Copy, scale=-1.0).then_inc(negm_ready, 1)

            deviation(0)
            high_context(0)
            high_rows(0)
            sequence(0)
            with act.Fori(1, B - 1) as b:
                sequence(b)
            sequence(B - 1, last=True)

        @block.tensor
        def _(pe):
            pe.wait_ge(ident_done, 2)
            pe.wait_ge(w_ready, 4)

            def turn(b):
                pe.wait_ge(normed, b * NB + NB)
                wait(pe, xn_ready, b)
                for t in range(NB):
                    for k in range(KD):
                        ins = nc.tensor.transpose(ps_t[:, k, t * P:(t + 1) * P], xt[:, t, k * P:(k + 1) * P], ident[:])
                ins.then_inc(turned, 1)

            def sequence(b, last=False):
                pe.wait_ge(xn_ready, b + 1)

                def product(i):
                    wait(pe, full_ready, b * NPROJ + (i - 1))
                    if i == 1:
                        pe.wait_ge(ct_ready, b + 1)
                    out = ps_p[i % 2][:]
                    n = 0
                    for k in range(KD):
                        for a, c in ((0, 0), (0, 1), (1, 0)):
                            if i < 2 * PAIRS:
                                w, src = (w_sb[0], xn_p) if i % 2 == 0 else (w_sb[1], ct_p)
                                j = i // 2
                                lhs, rhs = w[a][:, k, j * P:(j + 1) * P], src[c][:, k, :]
                            else:
                                t, half = divmod(i - 2 * PAIRS, 2)
                                lhs, rhs = ct_p[a][:, k, t * P:(t + 1) * P], w_sb[2][c][:, k, half * 512:(half + 1) * 512]
                            ins = nc.tensor.matmul(out, lhs, rhs, start=n == 0, stop=n == 3 * KD - 1)
                            n += 1
                    ins.then_inc(proj_done, 1)

                def score(i):
                    j, t = divmod(i, NB)
                    pe.wait_ge(high, b * NPROJ + 2 * j + 2)
                    wait(pe, max_done, b * NSC + i - 1)
                    if i == 0:
                        wait(pe, negm_ready, b)
                    for e in range(2):
                        r = slice(64 * e, 64 * e + 64)
                        ins = nc.tensor.matmul(ps_s[i % 2][:, e, :], q_p[0][r, j, t * P:(t + 1) * P], k_p[0][r, j, :],
                                                start=True, stop=True)
                    ins.then_inc(score_done, 1)

                for i in range(NPROJ):
                    product(i)
                    if i >= 2:
                        for n in score_turns(i):
                            score(n)
                    if i == TURN_AT and not last:
                        turn(b + 1)
                pe.wait_ge(max_done, b * NSC + NSC)
                for t in range(NB):
                    ins = nc.tensor.transpose(ps_s[0][0:H, 0, t * P:(t + 1) * P], top[:, t, :], ident[:])
                ins.then_inc(max_turned, 1)

            turn(0)
            sequence(0)
            with pe.Fori(1, B - 1) as b:
                sequence(b)
            sequence(B - 1, last=True)


def attend(nc, x, q_dram, k_dram, v_dram, negm_dram, y_dram, z_dram, c_dram, wg_feat, wo, bv, bo, gate,
           centre, inv_size, x1_dram):
    RQ = S // 2
    QB = RQ // P
    CH = RQ // 32
    QUADS = H // 4
    with ExitStack() as ctx:
        m = Space(nc, ctx, "att_")
        prob = m.sb("prob", [P, H, RQ])
        p_hi, p_lo = m.sb("p_hi", [P, H, RQ], F32R), m.sb("p_lo", [P, H, RQ], F32R)
        q_hi, q_lo = m.sb("q_hi", [P, H, RQ], F32R), m.sb("q_lo", [P, H, RQ], F32R)
        k_sb = m.sb("k", [P, H, P], F32R)
        v_hi = m.sb("v_hi", [P, PAIRS, 192], F32R)
        v_lo = m.sb("v_lo", [P, PAIRS, 192], F32R)
        negm = m.sb("negm", [P, 2 * RQ], F32R)
        pick = m.sb("pick", [P, PAIRS], F32R)
        acc = m.sb("acc", [P, 2, PAIRS, RQ])
        raw = m.sb("raw", [P, 8, QB, P])
        f_hi = [m.sb(f"f_hi{i}", [P, 8, P], F32R) for i in range(QB)]
        f_lo = [m.sb(f"f_lo{i}", [P, 8, P], F32R) for i in range(QB)]
        wide = [m.sb(f"wide{i}", [P, H, 16], F32R) for i in range(2)]
        ys = m.sb("ys", [P, QB, H, P], F32R)
        zs = [m.sb(f"zs{i}", [P, P], F32R) for i in range(2)]
        feat = m.sb("feat", [P, 8, QB, P])
        cm = [m.sb(f"cm{i}", [P, 2, P]) for i in range(2)]
        dist = [m.sb(f"dist{i}", [P, 2, QB, P]) for i in range(2)]
        turn = m.sb("turn", [P, 2, 2, 2, QB, P])
        frac, mag = turn[:, 0], turn[:, 1]
        wo_hi, wo_lo = m.sb("wo_hi", [P, PAIRS, D], F32R), m.sb("wo_lo", [P, PAIRS, D], F32R)
        x_sb = m.sb("x", [P, QB, D])
        bias_row = m.sb("bias_row", [P, D])
        tg, halfpi = m.sb("tg", [P, 1]), m.sb("halfpi", [P, 1])
        bv_sb = m.sb("bv", [P, PAIRS])
        sums, rec = m.sb("sums", [P, 32]), m.sb("rec", [P, 32])
        rec_hi, rec_lo = m.sb("rec_hi", [P, 32], F32R), m.sb("rec_lo", [P, 32], F32R)
        spread = m.sb("spread", [4, P], F32R)
        recs = p_lo[0:4].rearrange("p h n -> p (h n)")[:, 0:PAIRS * RQ]
        flat = p_hi[:].rearrange("p h n -> p (h n)")
        o_hi = flat[:, 0:PAIRS * RQ].rearrange("p (j n) -> p j n", j=PAIRS)
        o_lo = flat[:, PAIRS * RQ:].rearrange("p (j n) -> p j n", j=PAIRS)
        wo_in = acc[:].rearrange("p e j n -> p (e j n)")[:, 0:PAIRS * D].rearrange("p (j d) -> p j d", j=PAIRS)
        bvw = feat[:].rearrange("p f n m -> p (f n m)")[:, 0:PAIRS * P].rearrange("p (j n) -> p j n", j=PAIRS)
        mask = raw[:, 0, 0, 0:16]
        ident = raw[:, 1, 0, 0:PAIRS]
        wcol = raw[:, 2, 0, 0:H]
        wide_f = raw[:, 4:8].rearrange("p g b m -> p (g b m)")[:, 0:H * 16].rearrange("p (h n) -> p h n", h=H)
        sprd = raw[0:4, 3, 0, :]
        ps_s = [m.ps(f"ps_s{i}", [P, 2, 512]) for i in range(2)]
        ps_g = [m.ps(f"ps_g{i}", [P, 512]) for i in range(2)]
        ps_o = [m.ps(f"ps_o{i}", [P, 512]) for i in range(2)]

        sem = m.sem
        pro_in, pro_pool, pro_dve, pro_act, pro_pe = (sem(n) for n in ("pro_in", "pro_pool", "pro_dve", "pro_act", "pro_pe"))
        q_in, k_in, v_in, y_in, x_in, raw_in, relay = (sem(n) for n in ("q_in", "k_in", "v_in", "y_in", "x_in", "raw_in", "relay"))
        z_in, c_in = ([sem(f"{n}{i}") for i in range(2)] for n in ("z_in", "c_in"))
        delta, clipped, logs, turned, fracs, mags, sines, f_high, f_low = (
            sem(n) for n in ("delta", "clipped", "logs", "turned", "fracs", "mags", "sines", "f_high", "f_low"))
        s_done, exp_done, g_done, mult_done, p_high, p_low, pv_done, acc_done = (
            sem(n) for n in ("s_done", "exp_done", "g_done", "mult_done", "p_high", "p_low", "pv_done", "acc_done"))
        sum_in, rec_done, rec_in, bc_done, normed, o_high, o_low, out_done, x1_part, x1_done, x1_stored = (
            sem(n) for n in ("sum_in", "rec_done", "rec_in", "bc_done", "normed", "o_high", "o_low", "out_done",
                             "x1_part", "x1_done", "x1_stored"))
        block = ctx.enter_context(nc.Block())

        class Unit:
            def __init__(self, b, half, w):
                self.b, self.half, self.w = b, half, w
                self.n, self.r = b * 8 + (4 * half + w), b * 2 + half

            def plus(self, k):
                at = 4 * self.half + self.w + k
                b, at = (self.b + 1, at - 8) if at >= 8 else (self.b, at)
                return Unit(b, at // 4, at % 4)

            def exists(self):
                return not isinstance(self.b, int) or self.b < B

            def begun_early(self):
                return self.w == 0 and not (isinstance(self.n, int) and self.n == 0)

        def every_unit(eng, step):
            for half in range(2):
                for w in range(NB):
                    step(Unit(0, half, w))
            with eng.Fori(1, B - 1) as b:
                for half in range(2):
                    for w in range(NB):
                        step(Unit(b, half, w))
            for half in range(2):
                for w in range(NB):
                    step(Unit(B - 1, half, w))

        first = Unit(0, 0, 0)
        EARLY = 4
        POOL_CHUNKS = (0, 1, 2, 4, 5)

        @block.sync
        def _(sp):
            def after(s, value):
                wait(sp, s, value)
                if not isinstance(value, int):
                    sp.sem_inc(relay, 1)

            sp.dma_start(wo_in, wo.rearrange("(j p) d -> p j d", p=P)).then_inc(pro_in, 16)
            sp.dma_start(bias_row[:], bo.partition_broadcast(P)).then_inc(pro_in, 16)
            sp.dma_start(bv_sb[:], bv).then_inc(pro_in, 16)
            sp.dma_start(tg[:], gate.partition_broadcast(P)).then_inc(pro_in, 16)
            for n in range(16):
                sp.dma_start(wcol[8 * n:8 * n + 8, :], wg_feat).then_inc(pro_in, 16)

            def load_queries_high(u):
                after(s_done, u.n * QUADS)
                for at in (0, 64):
                    sp.dma_start(q_hi[at:at + 64].bitcast(F32), q_dram[0][bass.ds(u.b, 1), :, :, u.half * RQ:(u.half + 1) * RQ]
                                 .rearrange("o d h s -> d (o h) s")).then_inc(q_in, 16)

            def load_queries_low(u):
                after(s_done, u.n * QUADS)
                sp.dma_start(q_lo[0:64].bitcast(F32), q_dram[1][bass.ds(u.b, 1), :, :, u.half * RQ:(u.half + 1) * RQ]
                             .rearrange("o d h s -> d (o h) s")).then_inc(q_in, 16)
                sp.dma_start(negm[0:PAIRS, :].bitcast(F32).rearrange("p (e s) -> p e s", e=2), negm_dram[bass.ds(u.b, 1), :, u.half * RQ:(u.half + 1) * RQ]
                             .rearrange("o (j e) s -> (o j) e s", e=2)).then_inc(q_in, 16)

            def load_keys(u):
                after(s_done, u.n * QUADS)
                for part in range(2):
                    sp.dma_start(k_sb[64 * part:64 * part + 64].bitcast(F32), k_dram[part][bass.ds(u.b, 1), :, :, u.w * P:(u.w + 1) * P]
                                 .rearrange("o d h s -> d (o h) s")).then_inc(k_in, 16)

            def load_values(u):
                after(pv_done, u.n * PAIRS)
                for dst, part in ((v_hi, 0), (v_lo, 1)):
                    src = v_dram[part][bass.ds(u.b, 1), :, u.w, :].rearrange("o p (j e d) -> p (o j) e d", e=2, d=DK)
                    for e in range(2):
                        sp.dma_start(dst[:, :, 128 * e:128 * e + DK].bitcast(F32), src[:, :, e, :]).then_inc(v_in, 16)

            def load_centres(u):
                i = u.w % 2
                if isinstance(u.n, int) and u.n < 2:
                    pass
                else:
                    after(delta, (u.n - 2) * 3 + 1)
                for c in range(2):
                    sp.dma_start(cm[i][:, c, :], c_dram[c, bass.ds(u.b, 1), u.w * P:(u.w + 1) * P].rearrange("o s -> (o s)")
                                 .partition_broadcast(P)).then_inc(c_in[i], 16)

            def load_z(u):
                if not (isinstance(u.n, int) and u.n < 2):
                    after(g_done, (u.n - 1) * CH)
                sp.dma_start(zs[u.w % 2][0:3 * SEP, :].bitcast(F32), z_dram[:, :, bass.ds(u.b, 1), u.w * P:(u.w + 1) * P]
                             .rearrange("t k b s -> (t k) (b s)")).then_inc(z_in[u.w % 2], 16)

            def load_y(u):
                after(g_done, u.n * CH)
                for blk in range(QB):
                    sp.dma_start(ys[0:3 * SEP, blk].bitcast(F32), y_dram[bass.ds(u.r * QB + blk, 1)].rearrange("o t k (h n) -> (o t k) h n", h=H)
                                 ).then_inc(y_in, 16)

            def relabel(u):
                after(sines, u.n * 2 + 2)
                after(f_high, u.n * QB)
                after(f_low, u.n * QB)
                for g in range(8):
                    sp.dma_start(raw[:, g], feat[16 * g:16 * g + 16]).then_inc(raw_in, 16)

            sp.wait_ge(pro_dve, 2)
            load_queries_high(first)
            load_queries_low(first)
            load_keys(first)
            load_centres(first)
            load_centres(first.plus(1))
            load_centres(first.plus(2))
            load_values(first)
            sp.wait_ge(pro_dve, 9)
            load_z(first)
            load_y(first)
            relabel(first)
            load_keys(first.plus(1))

            def step(u):
                nxt, last = u.plus(1), u.w == NB - 1
                if u.w == 1:
                    after(x1_stored, u.r * 16)
                    sp.dma_start(x_sb[:], x[bass.ds(u.r * RQ, RQ), :].rearrange("(t p) d -> p t d", p=P)).then_inc(x_in, 16)
                if nxt.exists():
                    if u.plus(3).exists():
                        load_centres(u.plus(3))
                    load_z(nxt)
                    relabel(nxt)
                    if last:
                        load_queries_low(nxt)
                    if not last:
                        if u.plus(2).exists():
                            load_keys(u.plus(2))
                        load_values(nxt)
                    if u.w == NB - 2 and u.plus(2).exists():
                        load_queries_high(u.plus(2))
                if last:
                    if nxt.exists():
                        load_y(nxt)
                    after(acc_done, (u.n + 1) * PAIRS + 2)
                    for e, at in ((0, 64), (1, 0)):
                        sp.dma_start(sums[64 * e:64 * e + 64, :], acc[at:at + 1, e]).then_inc(sum_in, 16)
                    after(rec_done, (u.r + 1) * 3)
                    for row, (src, at) in enumerate(((rec_hi, 0), (rec_lo, 0), (rec_hi, 64), (rec_lo, 64))):
                        sp.dma_start(recs[row:row + 1, :].bitcast(F32), src[at:at + 64, :].bitcast(F32)).then_inc(rec_in, 16)
                    if nxt.exists():
                        load_values(nxt)
                        load_keys(u.plus(2))
                    after(x1_done, u.r + 1)
                    sp.dma_start(x1_dram[bass.ds(u.r * RQ, RQ), :].rearrange("(t p) d -> p t d", p=P), x_sb[:]).then_inc(x1_stored, 16)

            every_unit(sp, step)
            sp.wait_ge(x1_stored, 16 * 2 * B)

        @block.gpsimd
        def _(pool):
            nc.gpsimd.memset(mask, 1.0).then_inc(pro_pool, 1)
            nc.gpsimd.memset(ident, 0.0).then_inc(pro_pool, 1)
            nc.gpsimd.memset(sprd, 1.0).then_inc(pro_pool, 1)
            pool.wait_ge(pro_pool, 3)
            nc.gpsimd.affine_select(out=mask, in_=mask, compare_op=ALU.is_ge, fill=0.0, base=0,
                                    pattern=[[-8, 16]], channel_multiplier=1).then_inc(pro_pool, 1)
            nc.gpsimd.affine_select(out=ident, in_=ident, compare_op=ALU.not_equal, fill=1.0, base=0,
                                    pattern=[[-1, PAIRS]], channel_multiplier=1).then_inc(pro_pool, 1)
            nc.gpsimd.affine_select(out=sprd, in_=sprd, compare_op=ALU.is_ge, fill=0.0, base=0,
                                    pattern=[[-2, 2], [0, 64]], channel_multiplier=1).then_inc(pro_pool, 1)
            pool.wait_ge(pro_pool, 6)
            nc.gpsimd.affine_select(out=mask, in_=mask, compare_op=ALU.is_ge, fill=0.0, base=7,
                                    pattern=[[8, 16]], channel_multiplier=-1).then_inc(pro_pool, 1)
            nc.gpsimd.affine_select(out=sprd, in_=sprd, compare_op=ALU.is_ge, fill=0.0, base=1,
                                    pattern=[[2, 2], [0, 64]], channel_multiplier=-1).then_inc(pro_pool, 1)
            pool.wait_ge(pro_dve, 9)

            def distances(u):
                pool.wait_ge(c_in[u.w % 2], u.b * (4 * 32) + (4 * u.half + u.w) // 2 * 32 + 32)
                pool.sem_inc(relay, 1)
                wait(pool, fracs, u.n - 1)
                pool.sem_inc(relay, 1)
                d = dist[u.w % 2]
                for c in range(2):
                    cols = centre[:, bass.ds(u.r * QB, QB), c].unsqueeze(2).to_broadcast([P, QB, P])
                    last = nc.gpsimd.tensor_tensor(d[:, c], cm[u.w % 2][:, c, :].unsqueeze(1).to_broadcast([P, QB, P]), cols, ALU.subtract)
                last.then_inc(delta, 1)
                pool.wait_ge(delta, u.n * 3 + 1)
                pool.sem_inc(relay, 1)
                for c in range(2):
                    cols = inv_size[:, bass.ds(u.r * QB, QB), c].unsqueeze(2).to_broadcast([P, QB, P])
                    last = nc.gpsimd.tensor_tensor(d[:, c], d[:, c], cols, ALU.mult)
                last.then_inc(delta, 1)
                pool.wait_ge(delta, u.n * 3 + 2)
                nc.gpsimd.tensor_tensor(d[:], d[:], d[:], ALU.mult).then_inc(delta, 1)

            def low_features(u, blk):
                pool.wait_ge(f_high, u.n * QB + (blk + 1))
                nc.gpsimd.tensor_tensor(f_lo[blk][:], raw[:, :, blk], f_hi[blk][:].bitcast(F32), ALU.subtract).then_inc(f_low, 1)

            distances(first)
            distances(first.plus(1))
            for blk in range(QB):
                low_features(first, blk)
            distances(first.plus(2))

            def step(u):
                nxt = u.plus(1)
                for c in POOL_CHUNKS:
                    pool.wait_ge(p_high, u.n * CH + (c + 1))
                    at = (slice(None), slice(None), slice(32 * c, 32 * c + 32))
                    nc.gpsimd.tensor_tensor(p_lo[at], prob[at], p_hi[at].bitcast(F32), ALU.subtract).then_inc(p_low, 1)
                if u.plus(3).exists():
                    distances(u.plus(3))
                if nxt.exists():
                    for blk in range(QB):
                        low_features(nxt, blk)
                if u.w == NB - 1:
                    for i in range(4):
                        pool.wait_ge(o_high, u.r * 4 + (i + 1))
                        nc.gpsimd.tensor_tensor(o_lo[:, 2 * i:2 * i + 2], acc[:, 0, 2 * i:2 * i + 2, :],
                                                o_hi[:, 2 * i:2 * i + 2].bitcast(F32), ALU.subtract).then_inc(o_low, 1)

            every_unit(pool, step)

        @block.scalar
        def _(act):
            act.wait_ge(pro_in, 320)
            nc.scalar.activation(tg[:], tg[:], ACT.Tanh).then_inc(pro_act, 1)
            nc.scalar.copy(wo_hi[:], wo_in).then_inc(pro_act, 1)
            act.wait_ge(pro_dve, 9)

            def log(u):
                act.wait_ge(clipped, u.n + 1)
                nc.scalar.activation(dist[u.w % 2][:], dist[u.w % 2][:], ACT.Ln).then_inc(logs, 1)

            def exponential(u, q):
                act.wait_ge(s_done, u.n * QUADS + (q + 1))
                if q == 0:
                    wait(act, p_low, u.n * CH)
                nc.scalar.activation(prob[:, 4 * q:4 * q + 4, :], ps_s[q % 2][:].rearrange("p a (e s) -> p (a e) s", e=2),
                                     ACT.Exp).then_inc(exp_done, 1)

            def waves(u):
                act.wait_ge(fracs, u.n + 1)
                wait(act, raw_in, u.n * 128)
                nc.scalar.activation(feat[:, 0:4], frac.rearrange("p a b n m -> p (a b) n m"), ACT.Sin,
                                     scale=TWO_PI).then_inc(sines, 1)
                act.wait_ge(mags, u.n + 1)
                nc.scalar.activation(feat[:, 4:8], mag.rearrange("p a b n m -> p (a b) n m"), ACT.Sin,
                                     scale=-TWO_PI, bias=halfpi[:]).then_inc(sines, 1)

            def high_features(u, blk):
                act.wait_ge(raw_in, u.n * 128 + 128)
                wait(act, g_done, (u.n - 1) * CH + 4 * (blk + 1))
                nc.scalar.copy(f_hi[blk][:], raw[:, :, blk]).then_inc(f_high, 1)

            log(first)
            waves(first)
            log(first.plus(1))
            for q in range(QUADS):
                exponential(first, q)
            for blk in range(QB):
                high_features(first, blk)
            log(first.plus(2))

            def step(u):
                nxt = u.plus(1)
                if nxt.exists():
                    waves(nxt)
                for c in range(CH):
                    act.wait_ge(mult_done, u.n * CH + (c + 1) + 2)
                    if c == 0:
                        wait(act, pv_done, u.n * PAIRS)
                        if u.w == 0:
                            wait(act, out_done, u.r)
                    nc.scalar.copy(p_hi[:, :, 32 * c:32 * c + 32], prob[:, :, 32 * c:32 * c + 32]).then_inc(p_high, 1)
                if nxt.exists():
                    if u.w < NB - 1:
                        order = (0, 1, "f0", 2, "f1", 3)
                    else:
                        order = ("f0", "f1", 0, 1, 2, 3)
                    for what in order:
                        if what in ("f0", "f1"):
                            high_features(nxt, int(what[1]))
                        else:
                            exponential(nxt, what)
                if u.plus(3).exists():
                    log(u.plus(3))
                if u.w == NB - 1:
                    for i in range(4):
                        act.wait_ge(normed, u.r * 8 + (2 * i + 2))
                        nc.scalar.copy(o_hi[:, 2 * i:2 * i + 2], acc[:, 0, 2 * i:2 * i + 2, :]).then_inc(o_high, 1)

            every_unit(act, step)

        @block.vector
        def _(dve):
            nc.vector.memset(halfpi[:], HALF_PI)
            nc.vector.memset(q_lo[64:128].bitcast(F32), 0.0)
            nc.vector.memset(v_hi[:, :, DK:128].bitcast(F32), 1.0)
            nc.vector.memset(v_lo[:, :, DK:128].bitcast(F32), 0.0)
            nc.vector.memset(negm[:].bitcast(F32), 0.0).then_inc(pro_dve, 1)
            nc.vector.memset(ys[:].bitcast(F32), 0.0)
            for i in range(2):
                last = nc.vector.memset(zs[i][:].bitcast(F32), 0.0)
            last.then_inc(pro_dve, 1)
            dve.wait_ge(pro_in, 320)
            dve.wait_ge(pro_pool, 8)
            nc.vector.tensor_tensor(wide_f, mask.unsqueeze(1).to_broadcast([P, H, 16]), wcol.unsqueeze(2).to_broadcast([P, H, 16]),
                                    ALU.mult).then_inc(pro_dve, 1)
            nc.vector.tensor_copy(bvw, bv_sb[:].unsqueeze(2).to_broadcast([P, PAIRS, P])).then_inc(pro_dve, 1)
            nc.vector.tensor_copy(pick[:], ident)
            nc.vector.tensor_copy(spread[:], sprd)
            dve.wait_ge(pro_dve, 4)
            nc.vector.tensor_copy(wide[0][:], wide_f).then_inc(pro_dve, 1)
            dve.wait_ge(pro_dve, 5)
            nc.vector.tensor_tensor(wide[1][:], wide_f, wide[0][:].bitcast(F32), ALU.subtract).then_inc(pro_dve, 1)
            dve.wait_ge(pro_act, 2)
            nc.vector.tensor_tensor(wo_lo[:], wo_in, wo_hi[:].bitcast(F32), ALU.subtract).then_inc(pro_dve, 1)
            dve.wait_ge(pro_pe, 1)
            nc.vector.tensor_tensor(bias_row[:], ps_g[0][:, 0:D], bias_row[:], ALU.add).then_inc(pro_dve, 1)
            dve.wait_ge(pro_dve, 8)
            nc.vector.tensor_scalar(bias_row[:], bias_row[:], tg[:], None, ALU.mult).then_inc(pro_dve, 1)

            def clip(u):
                dve.wait_ge(delta, u.n * 3 + 3)
                nc.vector.tensor_scalar(dist[u.w % 2][:], dist[u.w % 2][:], 1e-6, None, ALU.max).then_inc(clipped, 1)

            def fractions(u, part):
                if part == 0:
                    dve.wait_ge(logs, u.n + 1)
                    wait(dve, sines, u.n * 2)
                    for f in range(2):
                        last = nc.vector.tensor_scalar(frac[:, f], dist[u.w % 2][:], 50.0 * FREQ[f] / TWO_PI, ROUND, ALU.mult, ALU.add)
                    last.then_inc(turned, 1)
                elif part == 1:
                    dve.wait_ge(turned, u.n * 2 + 1)
                    nc.vector.tensor_scalar(frac, frac, ROUND, None, ALU.subtract).then_inc(turned, 1)
                elif part == 2:
                    dve.wait_ge(turned, u.n * 2 + 2)
                    for f in range(2):
                        last = nc.vector.scalar_tensor_tensor(
                            out=frac[:, f].rearrange("p b n m -> p (b n m)"), in0=dist[u.w % 2][:].rearrange("p b n m -> p (b n m)"),
                            scalar=50.0 * FREQ[f] / TWO_PI, in1=frac[:, f].rearrange("p b n m -> p (b n m)"),
                            op0=ALU.mult, op1=ALU.subtract)
                    last.then_inc(fracs, 1)
                else:
                    dve.wait_ge(fracs, u.n + 1)
                    nc.vector.tensor_single_scalar(mag.bitcast(I32), frac.bitcast(I32), 0x7FFFFFFF, op=ALU.bitwise_and).then_inc(mags, 1)

            def low_part(u, c):
                dve.wait_ge(p_high, u.n * CH + (c + 1))
                at = (slice(None), slice(None), slice(32 * c, 32 * c + 32))
                nc.vector.tensor_tensor(p_lo[at], prob[at], p_hi[at].bitcast(F32), ALU.subtract).then_inc(p_low, 1)

            clip(first)
            for part in range(4):
                fractions(first, part)
            clip(first.plus(1))
            for part in range(4):
                fractions(first.plus(1), part)
            clip(first.plus(2))

            def multiply(u, c):
                if c == 0:
                    dve.wait_ge(exp_done, (u.n + 1) * QUADS)
                dve.wait_ge(g_done, u.n * CH + (c + 1))
                e = prob[:, :, 32 * c:32 * c + 32]
                nc.vector.scalar_tensor_tensor(out=e, in0=ps_g[c % 2][:].rearrange("p (h n) -> p h n", h=H),
                                               scalar=GEO_MIN, in1=e, op0=ALU.max, op1=ALU.mult).then_inc(mult_done, 1)

            def step(u):
                nxt, second, third = u.plus(1), u.plus(2), u.plus(3)
                for c in range(EARLY if u.begun_early() else 0, CH):
                    multiply(u, c)
                    if c == 6:
                        low_part(u, 3)
                low_part(u, 6)
                low_part(u, 7)
                for j in range(PAIRS):
                    dve.wait_ge(pv_done, u.n * PAIRS + (j + 1))
                    at = acc[:, :, j, :]
                    src = ps_o[j % 2][:].rearrange("p (e s) -> p e s", e=2)
                    if u.w == 0:
                        if j == 0:
                            wait(dve, o_low, u.r * 4)
                        ins = nc.vector.tensor_copy(at, src)
                    else:
                        ins = nc.vector.tensor_tensor(at, src, at, ALU.add)
                    ins.then_inc(acc_done, 1)
                    late = j >= 4 and u.w == NB - 1
                    if j in (0, 2, 4, 5) and second.exists() and not late:
                        fractions(second, (0, 2, 4, 5).index(j))
                    if j == 5 and third.exists() and not late:
                        clip(third)
                if u.w < NB - 1:
                    return
                if second.exists():
                    for part in (2, 3):
                        fractions(second, part)
                if third.exists():
                    clip(third)
                dve.wait_ge(sum_in, u.r * 32 + 32)
                nc.vector.reciprocal(rec[:], sums[:]).then_inc(rec_done, 1)
                dve.wait_ge(rec_done, u.r * 3 + 1)
                nc.vector.tensor_copy(rec_hi[:], rec[:]).then_inc(rec_done, 1)
                dve.wait_ge(rec_done, u.r * 3 + 2)
                nc.vector.tensor_tensor(rec_lo[:], rec[:], rec_hi[:].bitcast(F32), ALU.subtract).then_inc(rec_done, 1)
                if nxt.exists():
                    for c in range(EARLY // 2):
                        multiply(nxt, c)
                for i in range(4):
                    dve.wait_ge(bc_done, u.r * 4 + (i + 1))
                    js = slice(2 * i, 2 * i + 2)
                    src = ps_s[i // 2][:, i % 2, :].rearrange("p (j s) -> p j s", j=2)
                    for at, e in ((0, 0), (64, 1)):
                        rows = slice(at, at + 64)
                        nc.vector.tensor_tensor(acc[rows, 0, js, :], acc[rows, e, js, :], src[rows], ALU.mult).then_inc(normed, 1)
                if nxt.exists():
                    for c in range(EARLY // 2, EARLY):
                        multiply(nxt, c)
                dve.wait_ge(out_done, u.r + 1)
                dve.wait_ge(x_in, u.r * 16 + 16)
                for t in range(QB):
                    last = nc.vector.scalar_tensor_tensor(out=x_sb[:, t, :], in0=ps_o[t][:, 0:D], scalar=tg[:], in1=x_sb[:, t, :],
                                                          op0=ALU.mult, op1=ALU.add)
                last.then_inc(x1_part, 1)
                dve.wait_ge(x1_part, u.r + 1)
                nc.vector.tensor_tensor(x_sb[:], x_sb[:], bias_row[:].unsqueeze(1).to_broadcast([P, QB, D]), ALU.add).then_inc(x1_done, 1)

            every_unit(dve, step)

        @block.tensor
        def _(pe):
            pe.sem_inc(mult_done, 2)
            pe.sem_inc(acc_done, 2)
            pe.wait_ge(pro_in, 320)
            pe.wait_ge(pro_dve, 4)
            for j in range(PAIRS):
                last = nc.tensor.matmul(ps_g[0][:, 0:D], bvw[:, j, :], wo_in[:, j, :], start=j == 0, stop=j == PAIRS - 1)
            last.then_inc(pro_pe, 1)
            pe.wait_ge(pro_dve, 9)

            def scores(u, q):
                if q == 0:
                    pe.wait_ge(k_in, u.n * 32 + 32)
                    if u.w == 0:
                        pe.wait_ge(q_in, u.r * 64 + 64)
                wait(pe, exp_done, u.n * QUADS + (q - 1))
                for a in range(2):
                    nc.tensor.matmul(ps_s[q % 2][:, a, :], pick[:, 2 * q + a:2 * q + a + 1].to_broadcast([P, P]), negm[:],
                                     start=True, stop=False)
                    for e in range(2):
                        h = 4 * q + 2 * a + e
                        out = ps_s[q % 2][:, a, e * RQ:(e + 1) * RQ]
                        nc.tensor.matmul(out, k_sb[:, h, :], q_hi[:, h, :], start=False, stop=False)
                        last = nc.tensor.matmul(out, k_sb[:, h, :], q_lo[:, h, :], start=False, stop=e == 1)
                last.then_inc(s_done, 1)

            def geometry(u, c):
                blk = c // 4
                if c == 0:
                    pe.wait_ge(z_in[u.w % 2], u.b * (4 * 16) + (4 * u.half + u.w) // 2 * 16 + 16)
                    if u.w == 0:
                        pe.wait_ge(y_in, u.r * 32 + 32)
                if c % 4 == 0:
                    pe.wait_ge(f_high, u.n * QB + (blk + 1))
                    pe.wait_ge(f_low, u.n * QB + (blk + 1))
                pe.wait_ge(mult_done, u.n * CH + (c + 1))
                out = ps_g[c % 2][:].rearrange("p (h n) -> p h n", h=H)
                at = 32 * (c % 4)
                nc.tensor.matmul(out, zs[u.w % 2][:], ys[:, blk, :, at:at + 32], start=True, stop=False)
                for g in range(2):
                    grp = 2 * (c % 4) + g
                    for feats, w in ((f_hi, 0), (f_hi, 1), (f_lo, 0)):
                        last = nc.tensor.matmul(out[:, :, 16 * g:16 * g + 16], feats[blk][:, grp, :], wide[w][:],
                                                start=False, stop=g == 1 and feats is f_lo)
                last.then_inc(g_done, 1)

            def values(u, j):
                pe.wait_ge(acc_done, u.n * PAIRS + (j + 1))
                for e in range(2):
                    h = 2 * j + e
                    at = slice(DK * e, DK * e + P)
                    out = ps_o[j % 2][:, e * RQ:(e + 1) * RQ]
                    low = p_lo[:, h, :]
                    nc.tensor.matmul(out, v_hi[:, j, at], p_hi[:, h, :], start=True, stop=False)
                    nc.tensor.matmul(out, v_hi[:, j, at], low, start=False, stop=False)
                    last = nc.tensor.matmul(out, v_lo[:, j, at], p_hi[:, h, :], start=False, stop=True)
                last.then_inc(pv_done, 1)

            for q in range(QUADS):
                scores(first, q)

            def step(u):
                nxt = u.plus(1)
                beside = nxt.exists() and u.w < NB - 1
                for c in range(EARLY if u.begun_early() else 0, CH):
                    geometry(u, c)
                if beside:
                    scores(nxt, 0)
                    scores(nxt, 1)
                pe.wait_ge(p_low, u.n * CH + CH)
                pe.wait_ge(v_in, u.n * 64 + 64)
                if u.w == 0:
                    wait(pe, x1_part, u.r)
                for j in range(PAIRS):
                    values(u, j)
                    if beside and j in (1, 3):
                        scores(nxt, 2 + j // 2)
                if u.w < NB - 1:
                    return
                if nxt.exists():
                    for q in range(QUADS):
                        scores(nxt, q)
                    for c in range(EARLY // 2):
                        geometry(nxt, c)
                pe.wait_ge(exp_done, (nxt.n if nxt.exists() else u.n) * QUADS + QUADS)
                pe.wait_ge(rec_in, u.r * 64 + 64)
                for i in range(4):
                    nc.tensor.matmul(ps_s[i // 2][:, i % 2, :], spread[:], recs[:, 512 * i:512 * i + 512], start=True, stop=True
                                     ).then_inc(bc_done, 1)
                if nxt.exists():
                    for c in range(EARLY // 2, EARLY):
                        geometry(nxt, c)
                pe.wait_ge(acc_done, (u.n + 1) * PAIRS + 2)
                for j in range(PAIRS):
                    if j % 2 == 0:
                        pe.wait_ge(o_low, u.r * 4 + (j // 2 + 1))
                    for t in range(QB):
                        out = ps_o[t][:, 0:D]
                        for o, w in ((o_hi, wo_hi), (o_hi, wo_lo), (o_lo, wo_hi)):
                            last = nc.tensor.matmul(out, o[:, j, t * P:(t + 1) * P], w[:, j, :],
                                                    start=j == 0 and w is wo_hi and o is o_hi, stop=j == PAIRS - 1 and o is o_lo)
                last.then_inc(out_done, 1)

            every_unit(pe, step)


def route(nc, x1_dram, rw1, rb1, rw2, rb2, gate, xs_dram, slot, weight, tile_expert):
    with ExitStack() as ctx:
        m = Space(nc, ctx, "rt_")
        rw1_sb, rb1_sb = m.sb("rw1", [P, KD, HID]), m.sb("rb1", [P, HID // P])
        rw2_sb, rb2_sb = m.sb("rw2", [P, HID // P, E]), m.sb("rb2", [P, E])
        tg = m.sb("tg", [P, 1])
        ident, eps, zeros = m.sb("ident", [P, P]), m.sb("eps", [P, 1]), m.sb("zeros", [P, 8, D])
        below, ones = m.sb("below", [P, P]), m.sb("ones", [P, P])
        xn = m.sb("xn", [P, NT, D])
        xt = m.sb("xt", [P, NB, D])
        rw1_p = [m.sb(f"rw1_{part}", [P, KD, HID], F32R) for part in ("hi", "lo")]
        stats, mv = m.sb("stats", [P, NB, 6]), m.sb("mv", [P, NB, 2])
        sd, rstd = m.sb("sd", [P, NB]), m.sb("rstd", [P, NB])
        xn_p = [m.sb(f"xn_{part}", [P, KD, S], F32R) for part in ("hi", "lo")]
        hid = m.sb("hid", [P, HID // P, S])
        lg = m.sb("lg", [P, NT, E])
        top, top_i = m.sb("top", [P, NT, 8]), m.sb("top_i", [P, NT, 8], U32)
        top_f = m.sb("top_f", [P, NT, 2])
        iota_i, iota_f = m.sb("iota_i", [P, E], I32), m.sb("iota_f", [P, E])
        one_hot = [m.sb(f"one_hot{i}", [P, NT, E]) for i in range(2)]
        both, before, upto, total = (m.sb(n, [P, NT, E]) for n in ("both", "before", "upto", "total"))
        gap, den = m.sb("gap", [P, NT]), m.sb("den", [P, NT])
        tiles, tiles_r, first = m.sb("tiles", [P, E]), m.sb("tiles_r", [P, E]), m.sb("first", [P, E])
        slot_f = m.sb("slot_f", [P, NT, 2])
        tile_i, reached = m.sb("tile_i", [1, N_TILES], I32), m.sb("reached", [1, N_TILES, E])
        tile_f, te_f = m.sb("tile_f", [1, N_TILES]), m.sb("te_f", [1, N_TILES])
        ps_t = m.ps("ps_t", [P, 2, 512])
        ps_h = [m.ps(f"ps_h{i}", [P, 512]) for i in range(2)]
        ps_l, ps_c, ps_n = m.ps("ps_l", [P, NB, E]), m.ps("ps_c", [P, 512]), m.ps("ps_n", [P, 512])

        sem = m.sem
        w_in, x_in, zeroed, zero_stored, pool_done, eps_done, relay = (
            sem(n) for n in ("w_in", "x_in", "zeroed", "zero_stored", "pool_done", "eps_done", "relay"))
        stat, scaled, normed, kept, turned, w_high, w_low, xn_high, xn_ready = (
            sem(n) for n in ("stat", "scaled", "normed", "kept", "turned", "w_high", "w_low", "xn_high", "xn_ready"))
        h_done, h_ready, l_done, l_ready = (sem(n) for n in ("h_done", "h_ready", "l_done", "l_ready"))
        tg_done, step, gap_exp, counted, slots_ready, scattered = (
            sem(n) for n in ("tg_done", "step", "gap_exp", "counted", "slots_ready", "scattered"))
        NH = HID // P
        block = ctx.enter_context(nc.Block())

        @block.sync
        def _(sp):
            sp.dma_start(rw1_sb[:], rw1.rearrange("(k p) n -> p k n", p=P)).then_inc(w_in, 16)
            sp.dma_start(rb1_sb[:], rb1).then_inc(w_in, 16)
            sp.dma_start(rw2_sb[:], rw2.rearrange("(j p) e -> p j e", p=P)).then_inc(w_in, 16)
            sp.dma_start(rb2_sb[:], rb2.partition_broadcast(P)).then_inc(w_in, 16)
            sp.dma_start(tg[:], gate.partition_broadcast(P)).then_inc(w_in, 16)
            with sp.Fori(0, B) as b:
                sp.dma_start(xn[:, bass.ds(b * NB, NB), :], x1_dram[bass.ds(b * S, S), :].rearrange("(t p) d -> p t d", p=P)).then_inc(x_in, 16)
                sp.wait_ge(x_in, b * 16 + 16)
                sp.sem_inc(relay, 1)
            sp.wait_ge(zeroed, 1)
            for i in range(SLOTS // (8 * P)):
                sp.dma_start(xs_dram[i * 8 * P:(i + 1) * 8 * P, :].rearrange("(t p) d -> p t d", p=P), zeros[:]).then_inc(zero_stored, 16)
            sp.wait_ge(zero_stored, 16 * (SLOTS // (8 * P)))

        @block.gpsimd
        def _(pool):
            nc.gpsimd.memset(zeros[:], 0.0).then_inc(zeroed, 1)
            make_identity(nc, pool, ident, pool_done)
            nc.gpsimd.memset(ones[:], 1.0).then_inc(pool_done, 1)
            pool.wait_ge(pool_done, 3)
            nc.gpsimd.affine_select(out=below[:], in_=ones[:], compare_op=ALU.is_gt, fill=0.0, base=0,
                                    pattern=[[1, P]], channel_multiplier=-1).then_inc(pool_done, 1)
            nc.gpsimd.iota(iota_i[:], pattern=[[1, E]], base=0, channel_multiplier=0).then_inc(pool_done, 1)
            nc.gpsimd.iota(tile_i[:], pattern=[[SLOT_TILE, N_TILES]], base=0, channel_multiplier=0).then_inc(pool_done, 1)
            with pool.Fori(0, B) as b:
                pool.wait_ge(normed, b * NB + NB)
                pool.sem_inc(relay, 1)
                nc.gpsimd.tensor_copy(xn[:, bass.ds(b * NB, NB), :], xt[:]).then_inc(kept, 1)
            pool.wait_ge(kept, B)
            pool.wait_ge(slots_ready, 1)
            pool.wait_ge(zero_stored, 16 * (SLOTS // (8 * P)))
            for t in range(NT):
                for c in range(2):
                    nc.gpsimd.indirect_dma_start(xs_dram, bass.IndirectOffsetOnAxis(slot[:, c, t:t + 1], 0), xn[:, t, :], None
                                                 ).then_inc(scattered, 16)
            pool.wait_ge(scattered, 32 * NT)

        @block.vector
        def _(dve):
            nc.vector.memset(eps[:], EPS).then_inc(eps_done, 1)
            dve.wait_ge(w_high, 1)
            nc.vector.tensor_tensor(rw1_p[1][:], rw1_sb[:], rw1_p[0][:].bitcast(F32), ALU.subtract).then_inc(w_low, 1)

            def normalize(b):
                rows = xn[:, bass.ds(b * NB, NB), :]
                dve.wait_ge(x_in, b * 16 + 16)
                dve.sem_inc(relay, 1)
                for t in range(NB):
                    nc.vector.bn_stats(stats[:, t, :], rows[:, t, :]).then_inc(stat, 1)
                dve.wait_ge(stat, b * (2 * NB + 1) + NB)
                dve.sem_inc(relay, 1)
                for t in range(NB):
                    nc.vector.bn_aggr(mv[:, t, :], stats[:, t, :]).then_inc(stat, 1)
                dve.wait_ge(scaled, b + 1)
                nc.vector.reciprocal(rstd[:], sd[:]).then_inc(stat, 1)
                dve.wait_ge(stat, b * (2 * NB + 1) + 2 * NB + 1)
                wait(dve, turned, b)
                wait(dve, kept, b)
                for t in range(NB):
                    nc.vector.tensor_scalar(xt[:, t, :], rows[:, t, :], mv[:, t, 0:1], rstd[:, t:t + 1],
                                            ALU.subtract, ALU.mult).then_inc(normed, 1)

            def low_rows(b):
                dve.wait_ge(xn_high, b + 1)
                nc.vector.tensor_tensor(xn_p[1][:], ps_t[:], xn_p[0][:].bitcast(F32), ALU.subtract).then_inc(xn_ready, 1)

            def sequence(b, last=False):
                if not last:
                    normalize(b + 1)
                    low_rows(b + 1)
                dve.wait_ge(l_done, b + 1)
                nc.vector.tensor_tensor(lg[:, bass.ds(b * NB, NB), :], ps_l[:], rb2_sb[:].unsqueeze(1).to_broadcast([P, NB, E]),
                                        ALU.add).then_inc(l_ready, 1)

            normalize(0)
            low_rows(0)
            sequence(0)
            with dve.Fori(1, B - 1) as b:
                sequence(b)
            sequence(B - 1, last=True)
            count = [0]

            def link(ins):
                count[0] += 1
                ins.then_inc(step, 1)
                dve.wait_ge(step, count[0])

            dve.wait_ge(l_ready, B)
            dve.wait_ge(pool_done, 6)
            for t in range(NT):
                last = nc.vector.max(top[:, t, :], lg[:, t, :])
            link(last)
            for t in range(NT):
                nc.vector.max_index(top_i[:, t, :], top[:, t, :], lg[:, t, :])
            nc.vector.tensor_copy(iota_f[:], iota_i[:])
            nc.vector.tensor_copy(tile_f[:], tile_i[:])
            link(nc.vector.tensor_tensor(gap[:], top[:, :, 1], top[:, :, 0], ALU.subtract))
            link(nc.vector.tensor_copy(top_f[:], top_i[:, :, 0:2]))
            for c in range(2):
                link(nc.vector.tensor_tensor(one_hot[c][:], top_f[:, :, c:c + 1].to_broadcast([P, NT, E]),
                                             iota_f[:].unsqueeze(1).to_broadcast([P, NT, E]), ALU.is_equal))
            nc.vector.tensor_tensor(both[:], one_hot[0][:], one_hot[1][:], ALU.add).then_inc(counted, 1)
            dve.wait_ge(gap_exp, 1)
            link(nc.vector.tensor_scalar(den[:], gap[:], 1.0, None, ALU.add))
            link(nc.vector.reciprocal(den[:], den[:]))
            link(nc.vector.tensor_scalar(weight[:, 0, :], den[:], tg[:], None, ALU.mult))
            nc.vector.tensor_tensor(weight[:, 1, :], weight[:, 0, :], gap[:], ALU.mult)
            dve.wait_ge(counted, 2)
            link(nc.vector.tensor_copy(total[:].rearrange("p t e -> p (t e)"), ps_n[:, 0:NT * E]))
            for e in range(E):
                last = nc.vector.tensor_tensor_scan(out=upto[:, :, e], data0=total[:, :, e], data1=zeros[:, 0, 0:NT],
                                                    initial=0.0, op0=ALU.add, op1=ALU.add)
            link(last)
            nc.vector.tensor_tensor(before[:], upto[:], total[:], ALU.subtract)
            link(nc.vector.tensor_scalar(tiles[:], upto[:, NT - 1, :], 1.0 / SLOT_TILE,
                                         (SLOT_TILE - 1.0) / SLOT_TILE - 0.5 + 0.5 / SLOT_TILE, ALU.mult, ALU.add))
            link(nc.vector.tensor_scalar(tiles_r[:], tiles[:], ROUND, None, ALU.add))
            link(nc.vector.tensor_scalar(tiles[:], tiles_r[:], ROUND, float(SLOT_TILE), ALU.subtract, ALU.mult))
            link(nc.vector.tensor_tensor_scan(out=first[:], data0=tiles[:], data1=zeros[:, 0, 0:E], initial=0.0,
                                              op0=ALU.add, op1=ALU.add))
            link(nc.vector.tensor_tensor(first[:], first[:], tiles[:], ALU.subtract))
            link(nc.vector.tensor_tensor(before[:].rearrange("p t e -> p (t e)"), before[:].rearrange("p t e -> p (t e)"),
                                         ps_c[:, 0:NT * E], ALU.add))
            link(nc.vector.tensor_tensor(before[:], before[:], first[:].unsqueeze(1).to_broadcast([P, NT, E]), ALU.add))
            for c in range(2):
                link(nc.vector.tensor_tensor(one_hot[c][:], one_hot[c][:], before[:], ALU.mult))
                link(nc.vector.tensor_reduce(slot_f[:, :, c], one_hot[c][:], op=ALU.add, axis=AX))
                nc.vector.tensor_copy(slot[:, c, :], slot_f[:, :, c])
            link(nc.vector.tensor_tensor(reached[:], first[0:1, :].unsqueeze(1).to_broadcast([1, N_TILES, E]),
                                         tile_f[:].unsqueeze(2).to_broadcast([1, N_TILES, E]), ALU.is_le))
            link(nc.vector.tensor_reduce(te_f[:], reached[:, :, 1:E], op=ALU.add, axis=AX))
            nc.vector.tensor_copy(tile_expert[:], te_f[:]).then_inc(slots_ready, 1)

        @block.scalar
        def _(act):
            act.wait_ge(eps_done, 1)
            act.wait_ge(w_in, 80)
            nc.scalar.copy(rw1_p[0][:], rw1_sb[:]).then_inc(w_high, 1)

            def deviation(b):
                act.wait_ge(stat, b * (2 * NB + 1) + 2 * NB)
                nc.scalar.activation(sd[:], mv[:, :, 1], ACT.Sqrt, bias=eps[:]).then_inc(scaled, 1)

            def high_rows(b):
                act.wait_ge(turned, b + 1)
                nc.scalar.copy(xn_p[0][:], ps_t[:]).then_inc(xn_high, 1)

            def sequence(b, last=False):
                if not last:
                    deviation(b + 1)
                for j in range(NH):
                    act.wait_ge(h_done, b * NH + (j + 1))
                    if j == 0:
                        wait(act, l_done, b)
                    nc.scalar.activation(hid[:, j, :], ps_h[j % 2][:], ACT.Silu, bias=rb1_sb[:, j:j + 1]).then_inc(h_ready, 1)
                if not last:
                    high_rows(b + 1)

            deviation(0)
            high_rows(0)
            sequence(0)
            with act.Fori(1, B - 1) as b:
                sequence(b)
            sequence(B - 1, last=True)
            nc.scalar.activation(tg[:], tg[:], ACT.Tanh).then_inc(tg_done, 1)
            act.wait_ge(step, 3)
            act.wait_ge(tg_done, 1)
            nc.scalar.activation(gap[:], gap[:], ACT.Exp).then_inc(gap_exp, 1)

        @block.tensor
        def _(pe):
            pe.wait_ge(pool_done, 2)
            pe.wait_ge(w_low, 1)

            def turn(b):
                pe.wait_ge(normed, b * NB + NB)
                wait(pe, xn_ready, b)
                for t in range(NB):
                    for k in range(KD):
                        last = nc.tensor.transpose(ps_t[:, k, t * P:(t + 1) * P], xt[:, t, k * P:(k + 1) * P], ident[:])
                last.then_inc(turned, 1)

            def sequence(b, last=False):
                pe.wait_ge(xn_ready, b + 1)
                for j in range(NH):
                    wait(pe, h_ready, b * NH + (j - 1))
                    n = 0
                    for k in range(KD):
                        for a, c in ((0, 0), (0, 1), (1, 0)):
                            ins = nc.tensor.matmul(ps_h[j % 2][:], rw1_p[a][:, k, j * P:(j + 1) * P], xn_p[c][:, k, :],
                                                   start=n == 0, stop=n == 3 * KD - 1)
                            n += 1
                    ins.then_inc(h_done, 1)
                if not last:
                    turn(b + 1)
                pe.wait_ge(h_ready, b * NH + NH)
                wait(pe, l_ready, b)
                for t in range(NB):
                    for j in range(NH):
                        ins = nc.tensor.matmul(ps_l[:, t, :], hid[:, j, t * P:(t + 1) * P], rw2_sb[:, j, :],
                                               start=j == 0, stop=j == NH - 1)
                ins.then_inc(l_done, 1)

            turn(0)
            sequence(0)
            with pe.Fori(1, B - 1) as b:
                sequence(b)
            sequence(B - 1, last=True)
            pe.wait_ge(counted, 1)
            pe.wait_ge(pool_done, 4)
            flat = both[:].rearrange("p t e -> p (t e)")
            nc.tensor.matmul(ps_c[:, 0:NT * E], below[:], flat, start=True, stop=True)
            nc.tensor.matmul(ps_n[:, 0:NT * E], ones[:], flat, start=True, stop=True).then_inc(counted, 1)


def experts(nc, xs_dram, ys_dram, w1, b1, w2, b2, tile_expert):
    TB = SLOT_TILE // P
    NH = HID // P
    HALVES = 2
    with ExitStack() as ctx:
        m = Space(nc, ctx, "ex_")
        w1_sb = [m.sb(f"w1{i}", [P, KD, HID]) for i in range(2)]
        w2_sb = [m.sb(f"w2{i}", [P, NH, D]) for i in range(2)]
        w1_p = [[m.sb(f"w1_{part}{i}", [P, KD, HID], F32R) for part in ("hi", "lo")] for i in range(2)]
        w2_p = [[m.sb(f"w2_{part}{i}", [P, NH, D], F32R) for part in ("hi", "lo")] for i in range(2)]
        b1_sb = [m.sb(f"b1{i}", [P, NH]) for i in range(2)]
        b2_sb = [m.sb(f"b2{i}", [P, D]) for i in range(2)]
        xt = [m.sb(f"xt{i}", [P, TB, D]) for i in range(2)]
        x_p = [m.sb(f"x_{part}", [P, KD, SLOT_TILE], F32R) for part in ("hi", "lo")]
        hid = m.sb("hid", [P, NH, SLOT_TILE])
        hid_p = [[m.sb(f"hid_{part}{i}", [P, NH, SLOT_TILE], F32R) for part in ("hi", "lo")] for i in range(2)]
        yt = [m.sb(f"yt{i}", [P, TB, D]) for i in range(2)]
        ident = m.sb("ident", [P, P])
        ps_t = m.ps("ps_t", [P, KD, SLOT_TILE])
        ps_h = [m.ps(f"ps_h{i}", [P, 512]) for i in range(4)]
        ps_y = [m.ps(f"ps_y{i}", [P, TB, D]) for i in range(2)]
        sem = m.sem
        rows_in, w2_in, b1_in, b2_in, stored = ([sem(f"{n}{i}") for i in range(2)] for n in ("rows_in", "w2_in", "b1_in", "b2_in", "stored"))
        w1_high, w1_low, w2_high, w2_low, x_high, x_low, ident_done, relay = (
            sem(n) for n in ("w1_high", "w1_low", "w2_high", "w2_low", "x_high", "x_low", "ident_done", "relay"))
        turned, h_done, h_ready, hid_high, hid_low, y_done, y_ready = (
            sem(n) for n in ("turned", "h_done", "h_ready", "hid_high", "hid_low", "y_done", "y_ready"))
        block = ctx.enter_context(nc.Block())

        class Tile:
            def __init__(self, n, i, use):
                self.n, self.i, self.use = n, i, use
                self.last = isinstance(n, int) and n == N_TILES - 1

            def next(self):
                return Tile(self.n + 1, 1 - self.i, self.use + self.i)

        def every_tile(eng, front, back):
            tiles = [Tile(n, n % 2, n // 2) for n in range(3)]
            front(tiles[0])
            for n in (1, 2):
                front(tiles[n])
                back(tiles[n - 1])
            with eng.Fori(1, N_TILES // 2 - 1) as pair:
                before, odd, even = Tile(pair * 2, 0, pair), Tile(pair * 2 + 1, 1, pair), Tile(pair * 2 + 2, 0, pair + 1)
                front(odd)
                back(before)
                front(even)
                back(odd)
            last = Tile(N_TILES - 1, 1, N_TILES // 2 - 1)
            front(last)
            back(Tile(N_TILES - 2, 0, N_TILES // 2 - 1))
            back(last)

        @block.sync
        def _(sp):
            def after(s, value):
                wait(sp, s, value)
                if not isinstance(value, int):
                    sp.sem_inc(relay, 1)

            def load_first(t):
                e = sp.value_load(tile_expert[0:1, bass.ds(t.n, 1)], min_val=0, max_val=E - 1)
                after(turned, t.n - 1)
                after(w1_low, t.n - 1)
                sp.dma_start(xt[t.i][:], xs_dram[bass.ds(t.n * SLOT_TILE, SLOT_TILE), :].rearrange("(t p) d -> p t d", p=P)
                             ).then_inc(rows_in[t.i], 16)
                sp.dma_start(w1_sb[t.i][:], w1[bass.ds(e, 1)].rearrange("o (k p) n -> p (o k) n", p=P)).then_inc(rows_in[t.i], 16)
                after(h_ready, (t.n - 1) * NH)
                sp.dma_start(b1_sb[t.i][:], b1[bass.ds(e, 1)].rearrange("o p j -> p (o j)")).then_inc(b1_in[t.i], 16)

            def load_second(t):
                e = sp.value_load(tile_expert[0:1, bass.ds(t.n, 1)], min_val=0, max_val=E - 1)
                after(w2_low, t.n - 1)
                sp.dma_start(w2_sb[t.i][:], w2[bass.ds(e, 1)].rearrange("o (j p) d -> p (o j) d", p=P)).then_inc(w2_in[t.i], 16)
                after(y_ready, t.n - 1)
                sp.dma_start(b2_sb[t.i][:], b2[bass.ds(e, 1)].rearrange("o d -> (o d)").partition_broadcast(P)).then_inc(b2_in[t.i], 16)

            every_tile(sp, load_first, load_second)

        @block.gpsimd
        def _(pool):
            make_identity(nc, pool, ident, ident_done)

            def split(t):
                pool.wait_ge(w2_high, t.n + 1)
                nc.gpsimd.tensor_tensor(w2_p[t.i][1][:], w2_sb[t.i][:], w2_p[t.i][0][:].bitcast(F32), ALU.subtract).then_inc(w2_low, 1)

            def store(t):
                pool.wait_ge(y_ready, t.n + 1)
                pool.sem_inc(relay, 1)
                pool.dma_start(ys_dram[bass.ds(t.n * SLOT_TILE, SLOT_TILE), :].rearrange("(t p) d -> p t d", p=P), yt[t.i][:]
                               ).then_inc(stored[t.i], 16)

            every_tile(pool, split, store)
            for i in range(2):
                pool.wait_ge(stored[i], 16 * N_TILES // 2)

        @block.scalar
        def _(act):
            def split_first(t):
                act.wait_ge(rows_in[t.i], t.use * 32 + 32)
                wait(act, h_done, (t.n - 1) * NH)
                nc.scalar.copy(w1_p[t.i][0][:], w1_sb[t.i][:]).then_inc(w1_high, 1)
                act.wait_ge(turned, t.n + 1)
                nc.scalar.copy(x_p[0][:], ps_t[:]).then_inc(x_high, 1)

            def front(t):
                act.wait_ge(b1_in[t.i], t.use * 16 + 16)
                for j in range(NH):
                    act.wait_ge(h_done, t.n * NH + (j + 1))
                    if j % (NH // HALVES) == 0:
                        wait(act, hid_low, (t.n - 1) * HALVES + (j // (NH // HALVES) + 1))
                    nc.scalar.activation(hid[:, j, :], ps_h[j % 4][:, 0:SLOT_TILE], ACT.Silu, bias=b1_sb[t.i][:, j:j + 1]
                                         ).then_inc(h_ready, 1)
                if not t.last:
                    split_first(t.next())
                act.wait_ge(w2_in[t.i], t.use * 16 + 16)
                wait(act, y_done, t.n - 1)
                nc.scalar.copy(w2_p[t.i][0][:], w2_sb[t.i][:]).then_inc(w2_high, 1)

            split_first(Tile(0, 0, 0))
            every_tile(act, front, lambda t: None)

        @block.vector
        def _(dve):
            def split_first(t):
                dve.wait_ge(w1_high, t.n + 1)
                nc.vector.tensor_tensor(w1_p[t.i][1][:], w1_sb[t.i][:], w1_p[t.i][0][:].bitcast(F32), ALU.subtract).then_inc(w1_low, 1)
                dve.wait_ge(x_high, t.n + 1)
                nc.vector.tensor_tensor(x_p[1][:], ps_t[:], x_p[0][:].bitcast(F32), ALU.subtract).then_inc(x_low, 1)

            def front(t):
                for half in range(HALVES):
                    js = slice(half * NH // HALVES, (half + 1) * NH // HALVES)
                    dve.wait_ge(h_ready, t.n * NH + NH // HALVES * (half + 1))
                    wait(dve, y_done, t.n - 1)
                    nc.vector.tensor_copy(hid_p[t.i][0][:, js], hid[:, js]).then_inc(hid_high, 1)
                    dve.wait_ge(hid_high, t.n * HALVES + (half + 1))
                    nc.vector.tensor_tensor(hid_p[t.i][1][:, js], hid[:, js], hid_p[t.i][0][:, js].bitcast(F32), ALU.subtract
                                            ).then_inc(hid_low, 1)
                if not t.last:
                    split_first(t.next())

            def back(t):
                dve.wait_ge(y_done, t.n + 1)
                dve.wait_ge(b2_in[t.i], t.use * 16 + 16)
                wait(dve, stored[t.i], t.use * 16)
                nc.vector.tensor_tensor(yt[t.i][:], ps_y[t.i][:], b2_sb[t.i][:].unsqueeze(1).to_broadcast([P, TB, D]), ALU.add
                                        ).then_inc(y_ready, 1)

            split_first(Tile(0, 0, 0))
            every_tile(dve, front, back)

        @block.tensor
        def _(pe):
            pe.wait_ge(ident_done, 2)

            def turn(t):
                pe.wait_ge(rows_in[t.i], t.use * 32 + 32)
                wait(pe, x_low, t.n)
                for tb in range(TB):
                    for k in range(KD):
                        last = nc.tensor.transpose(ps_t[:, k, tb * P:(tb + 1) * P], xt[t.i][:, tb, k * P:(k + 1) * P], ident[:])
                last.then_inc(turned, 1)

            def front(t):
                pe.wait_ge(w1_low, t.n + 1)
                pe.wait_ge(x_low, t.n + 1)
                for j in range(NH):
                    wait(pe, h_ready, t.n * NH + (j - 3))
                    at = slice(j * P, (j + 1) * P)
                    n = 0
                    for k in range(KD):
                        for a, c in ((0, 0), (0, 1), (1, 0)):
                            last = nc.tensor.matmul(ps_h[j % 4][:, 0:SLOT_TILE], w1_p[t.i][a][:, k, at], x_p[c][:, k, :],
                                                    start=n == 0, stop=n == 3 * KD - 1)
                            n += 1
                    last.then_inc(h_done, 1)
                if not t.last:
                    turn(t.next())

            def back(t):
                pe.wait_ge(hid_low, (t.n + 1) * HALVES)
                pe.wait_ge(w2_low, t.n + 1)
                wait(pe, y_ready, t.n - 1)
                for tb in range(TB):
                    n = 0
                    for j in range(NH):
                        for a, c in ((0, 0), (0, 1), (1, 0)):
                            last = nc.tensor.matmul(ps_y[t.i][:, tb, :], hid_p[t.i][a][:, j, tb * P:(tb + 1) * P], w2_p[t.i][c][:, j, :],
                                                    start=n == 0, stop=n == 3 * NH - 1)
                            n += 1
                last.then_inc(y_done, 1)

            turn(Tile(0, 0, 0))
            every_tile(pe, front, back)


def combine(nc, x1_dram, ys_dram, slot, weight, out):
    with ExitStack() as ctx:
        m = Space(nc, ctx, "cb_")
        DEPTH = 4
        x1 = m.sb("x1", [P, NT, D])
        row = [[m.sb(f"row{c}_{i}", [P, D]) for i in range(DEPTH)] for c in range(2)]
        sem = m.sem
        x_in = sem("x_in")
        gathered = [sem(f"gathered{i}") for i in range(DEPTH)]
        added, ready, stored = sem("added"), sem("ready"), sem("stored")
        block = ctx.enter_context(nc.Block())

        @block.gpsimd
        def _(pool):
            for t in range(NT):
                if t >= DEPTH:
                    pool.wait_ge(ready, t - DEPTH + 1)
                for c in range(2):
                    nc.gpsimd.indirect_dma_start(row[c][t % DEPTH][:], None, ys_dram, bass.IndirectOffsetOnAxis(slot[:, c, t:t + 1], 0)
                                                 ).then_inc(gathered[t % DEPTH], 16)

        @block.vector
        def _(dve):
            dve.wait_ge(x_in, 16)
            for t in range(NT):
                dve.wait_ge(gathered[t % DEPTH], 32 * (t // DEPTH) + 32)
                nc.vector.scalar_tensor_tensor(out=x1[:, t, :], in0=row[0][t % DEPTH][:], scalar=weight[:, 0, t:t + 1],
                                               in1=x1[:, t, :], op0=ALU.mult, op1=ALU.add).then_inc(added, 1)
                dve.wait_ge(added, t + 1)
                nc.vector.scalar_tensor_tensor(out=x1[:, t, :], in0=row[1][t % DEPTH][:], scalar=weight[:, 1, t:t + 1],
                                               in1=x1[:, t, :], op0=ALU.mult, op1=ALU.add).then_inc(ready, 1)

        @block.sync
        def _(sp):
            view = out.rearrange("(t p) d -> p t d", p=P)
            sp.dma_start(x1[:], x1_dram.rearrange("(t p) d -> p t d", p=P)).then_inc(x_in, 16)
            for t in range(0, NT, 4):
                sp.wait_ge(ready, t + 4)
                sp.dma_start(view[:, t:t + 4, :], x1[:, t:t + 4, :]).then_inc(stored, 16)
            sp.wait_ge(stored, 16 * NT // 4)


def program(nc, x, ctx_t, boxes, g_xattn, g_ffn, wq, bq, wk, bk, wv, bv, wo, bo, wg_rows, wg_feat, bg,
            rw1, rb1, rw2, rb2, w1, b1, w2, b2, out):
    def scratch(name, shape):
        return nc.dram_tensor(name, shape, F32, kind="Internal").ap()

    q_dram = [scratch(f"q_{part}", [B, DK, H, S]) for part in ("hi", "lo")]
    k_dram = [scratch(f"k_{part}", [B, DK, H, S]) for part in ("hi", "lo")]
    v_dram = [scratch(f"v_{part}", [B, P, NB, HD]) for part in ("hi", "lo")]
    negm_dram = scratch("neg_max", [B, H, S])
    y_dram, z_dram = scratch("y_geometry", [NT, 3, SEP, YCOLS]), scratch("z_geometry", [3, SEP, B, S])
    c_dram = scratch("centre_rows", [2, B, S])
    x1_dram = scratch("x1_rows", [TOK, D])
    xs_dram, ys_dram = scratch("expert_in", [SLOTS, D]), scratch("expert_out", [SLOTS, D])
    with ExitStack() as ctx:
        m = Space(nc, ctx, "")
        with ExitStack() as boxes_ctx:
            k = Space(nc, boxes_ctx, "")
            centre, inv_size = k.sb("centre", [P, NT, 2]), k.sb("inv_size", [P, NT, 2])
            box_terms(nc, boxes, wg_rows, bg, y_dram, z_dram, c_dram, centre, inv_size)
            project(nc, x, ctx_t, wq, wk, wv, bq, bk, q_dram, k_dram, v_dram, negm_dram)
            attend(nc, x, q_dram, k_dram, v_dram, negm_dram, y_dram, z_dram, c_dram, wg_feat, wo, bv, bo, g_xattn,
                   centre, inv_size, x1_dram)
        slot = m.sb("slot", [P, 2, NT], U32)
        weight = m.sb("weight", [P, 2, NT])
        tile_expert = m.sb("tile_expert", [1, N_TILES], I32)
        route(nc, x1_dram, rw1, rb1, rw2, rb2, g_ffn, xs_dram, slot, weight, tile_expert)
        experts(nc, xs_dram, ys_dram, w1, b1, w2, b2, tile_expert)
        combine(nc, x1_dram, ys_dram, slot, weight, out)


def kernel(**inputs):
    import numpy as np
    import concourse.bacc as bacc
    from concourse.bass_utils import run_bass_kernel_spmd

    a = {n.replace("L0_xattn_", "").replace("L0_ffn_", "ffn_"): np.asarray(v) for n, v in inputs.items()}
    per_row = lambda v: v.reshape(-1, P).T
    laid = {
        "x": a["x"].reshape(TOK, D), "ctx_t": a["ctx_1024"].reshape(TOK, D).T, "boxes": a["fside_BxSx4_0"].reshape(TOK, 4),
        "g_xattn": a["g_xattn"], "g_ffn": a["g_ffn"],
        "wq": a["Wq"].T, "bq": per_row(a["bq"]), "wk": a["Wk"].T, "bk": per_row(a["bk"]),
        "wv": a["Wv"].T, "bv": per_row(a["bv"]), "wo": a["Wo"].T, "bo": a["bo"],
        "wg_rows": a["Wg"].T, "wg_feat": a["Wg"].T[[0, 2, 1, 3, 8, 10, 9, 11]], "bg": a["bg"],
        "rw1": a["ffn_rw1"], "rb1": per_row(a["ffn_rb1"]), "rw2": a["ffn_rw2"], "rb2": a["ffn_rb2"],
        "w1": a["ffn_w1"], "b1": a["ffn_b1"].reshape(E, -1, P).transpose(0, 2, 1), "w2": a["ffn_w2"], "b2": a["ffn_b2"],
    }
    laid = {n: np.ascontiguousarray(v) for n, v in laid.items()}
    nc = bacc.Bacc("TRN2", target_bir_lowering=False, num_devices=1)
    handles = {n: nc.dram_tensor("in_" + n, v.shape, mybir.dt.from_np(v.dtype), kind="ExternalInput").ap() for n, v in laid.items()}
    out = nc.dram_tensor("out", [TOK, D], F32, kind="ExternalOutput").ap()
    program(nc, out=out, **handles)
    got = run_bass_kernel_spmd(nc, [{"in_" + n: v for n, v in laid.items()}], core_ids=[0]).results[0]["out"]
    return got.reshape(B, S, D)
```
